# Optimizing a Trainium2 kernel written in Bass

```python
import numpy as np
import jax
import jax.numpy as jnp

def _softmax(x, axis=-1):
    return jax.nn.softmax(x, axis=axis)

def _gelu(x):
    return jax.nn.gelu(x, approximate=True)

def _silu(x):
    return jax.nn.silu(x)

def _sigmoid(x):
    return jax.nn.sigmoid(x)

def _layernorm(x, axis=-1, eps=1e-05):
    m = jnp.mean(x, axis=axis, keepdims=True)
    v = jnp.var(x, axis=axis, keepdims=True)
    return (x - m) / jnp.sqrt(v + eps)

def _scatter_add(tgt, idx, src, axis=0):
    return tgt.at[idx].add(src)

def _segment_sum(src, seg, n):
    return jax.ops.segment_sum(src, seg, n)
kernel_name = 'mk_gnn_ffn_d2_gnn_r32_93c08c'

def setup_inputs(seed: int=0):
    np.random.seed(seed)
    _w = jnp.asarray

    def _rec_inputs():
        import jax
        import jax.numpy as jnp
        _gk = jax.random.key(seed)
        x = -0.0002117 + 1 * jax.random.normal(jax.random.fold_in(_gk, 1), (3125, 256), jnp.float32)
        src = jax.random.randint(jax.random.fold_in(_gk, 2), (50000,), 0, 3125, jnp.int32)
        dst = jnp.minimum((3125 * jax.random.uniform(jax.random.fold_in(_gk, 3), (50000,)) ** 2.0).astype(jnp.int32), 99999)
        _o = jnp.argsort(dst, stable=True)
        src = src[_o]
        dst = dst[_o]
        edge_attr_3 = -1.09012e-05 + 0.99985 * jax.random.normal(jax.random.fold_in(_gk, 12), (50000, 3), jnp.float32)
        return (x, src, dst, edge_attr_3)
    x, src, dst, edge_attr_3 = _rec_inputs()

    def _L0_gnn_setup():
        import jax, jax.numpy as jnp
        import numpy as np
        N = 3125
        E = 25000
        EMB = 256
        HID = 256
        EPS = 1e-05

        def _pool_max(h, edge_src, edge_dst):
            pooled = jax.ops.segment_max(h[edge_src], edge_dst, num_segments=N)
            cnt = jax.ops.segment_sum(jnp.ones((edge_dst.shape[0],), h.dtype), edge_dst, num_segments=N)
            return jnp.where((cnt > 0)[:, None], pooled, jnp.zeros((), h.dtype))

        def _layernorm(x, g, b):
            mu = jnp.mean(x, axis=-1, keepdims=True)
            var = jnp.mean(jnp.square(x - mu), axis=-1, keepdims=True)
            return (x - mu) * jax.lax.rsqrt(var + EPS) * g + b
        key = jax.random.key(seed)
        ks = jax.random.split(key, 12)
        s = 0.05
        return {'embeddings': jax.random.normal(ks[0], (N, EMB), jnp.float32), 'edge_src': jax.random.randint(ks[1], (E,), 0, N, jnp.int32), 'edge_dst': jax.random.randint(ks[2], (E,), 0, N, jnp.int32), 'Wp1': jax.random.normal(ks[3], (HID, EMB), jnp.float32) * s, 'bp1': jnp.zeros((HID,), jnp.float32), 'Wm1': jax.random.normal(ks[4], (HID, EMB + HID), jnp.float32) * s, 'bm1': jnp.zeros((HID,), jnp.float32), 'Wm2': jax.random.normal(ks[5], (HID, 2 * HID), jnp.float32) * s, 'bm2': jnp.zeros((HID,), jnp.float32), 'Wm3': jax.random.normal(ks[6], (HID, 2 * HID), jnp.float32) * s, 'bm3': jnp.zeros((HID,), jnp.float32), 'ln2_g': jnp.ones((HID,), jnp.float32), 'ln2_b': jnp.zeros((HID,), jnp.float32), 'ln3_g': jnp.ones((HID,), jnp.float32), 'ln3_b': jnp.zeros((HID,), jnp.float32)}
    _L0_gnn_all = _L0_gnn_setup()
    _L0_gnn_in = {k: v for k, v in _L0_gnn_all.items() if k in ('Wp1', 'bp1', 'Wm1', 'bm1', 'Wm2', 'bm2', 'Wm3', 'bm3', 'ln2_g', 'ln2_b', 'ln3_g', 'ln3_b')}
    del _L0_gnn_all

    def _L0_ffn_setup():
        import jax, jax.numpy as jnp
        import numpy as np
        TOP_K = 2
        key = jax.random.key(seed)
        ks = jax.random.split(key, 4)
        B, L, D, H, E = (8, 128, 256, 1024, 8)
        s = 0.02
        return {'x': jax.random.normal(ks[0], (B, L, D), jnp.float32), 'Wg': jax.random.normal(ks[1], (D, E), jnp.float32) * s, 'bg': jnp.zeros((E,), jnp.float32), 'W1': jax.random.normal(ks[2], (E, D, H), jnp.float32) * s, 'b1': jnp.zeros((E, H), jnp.float32), 'W2': jax.random.normal(ks[3], (E, H, D), jnp.float32) * s, 'b2': jnp.zeros((E, D), jnp.float32)}
    _L0_ffn_all = _L0_ffn_setup()
    _L0_ffn_in = {k: v for k, v in _L0_ffn_all.items() if k in ('Wg', 'bg', 'W1', 'b1', 'W2', 'b2')}
    del _L0_ffn_all

    def _L1_gnn_setup():
        import jax, jax.numpy as jnp
        import numpy as np
        N = 50000
        E = 12500
        IN = 256
        H = 8
        D = 32
        EF = 3
        key = jax.random.key(seed)
        ks = jax.random.split(key, 8)
        x = jax.random.normal(ks[0], (N, IN), dtype=jnp.float32)
        edge_index = jax.random.randint(ks[1], (2, E), 0, N, dtype=jnp.int64)
        edge_attr = jax.random.normal(ks[2], (E, EF), dtype=jnp.float32)
        W = jax.random.normal(ks[3], (H * D, IN), dtype=jnp.float32) * np.float32(np.sqrt(2.0 / (IN + H * D)))
        a_src = jax.random.normal(ks[4], (H, D), dtype=jnp.float32) * np.float32(np.sqrt(2.0 / (H + D)))
        a_dst = jax.random.normal(ks[5], (H, D), dtype=jnp.float32) * np.float32(np.sqrt(2.0 / (H + D)))
        edge_W = jax.random.normal(ks[6], (H * D, EF), dtype=jnp.float32) * np.float32(np.sqrt(2.0 / (EF + H * D)))
        edge_b = jnp.zeros((H * D,), dtype=jnp.float32)
        bias = jnp.zeros((H * D,), dtype=jnp.float32)
        return {'x': x, 'W': W, 'a_src': a_src, 'a_dst': a_dst, 'edge_W': edge_W, 'edge_b': edge_b, 'bias': bias, 'edge_attr': edge_attr, 'edge_index': edge_index}
    _L1_gnn_all = _L1_gnn_setup()
    _L1_gnn_in = {k: v for k, v in _L1_gnn_all.items() if k in ('W', 'a_src', 'a_dst', 'edge_W', 'edge_b', 'bias')}
    del _L1_gnn_all

    def _L1_ffn_setup():
        import jax, jax.numpy as jnp
        import numpy as np
        D_MODEL = 256
        N_EXPERTS = 16
        HIDDEN = 512
        SCALE = 0.02
        key = jax.random.key(seed)
        ks = jax.random.split(key, 5)
        x = jax.random.normal(ks[0], (4, 256, D_MODEL), dtype=jnp.float32)
        gate_w = jax.random.normal(ks[1], (D_MODEL, N_EXPERTS), dtype=jnp.float32) * SCALE
        gate_b = jnp.zeros((N_EXPERTS,), dtype=jnp.float32)
        w1 = jax.random.normal(ks[2], (N_EXPERTS, D_MODEL, HIDDEN), dtype=jnp.float32) * SCALE
        w2 = jax.random.normal(ks[3], (N_EXPERTS, D_MODEL, HIDDEN), dtype=jnp.float32) * SCALE
        w3 = jax.random.normal(ks[4], (N_EXPERTS, HIDDEN, D_MODEL), dtype=jnp.float32) * SCALE
        return {'x': x, 'gate_w': gate_w, 'gate_b': gate_b, 'w1': w1, 'w2': w2, 'w3': w3}
    _L1_ffn_all = _L1_ffn_setup()
    _L1_ffn_in = {k: v for k, v in _L1_ffn_all.items() if k in ('gate_w', 'gate_b', 'w1', 'w2', 'w3')}
    del _L1_ffn_all
    return {'x': x, 'src': src, 'dst': dst, 'edge_attr_3': edge_attr_3, 'L0_gnn_Wp1': _L0_gnn_in['Wp1'], 'L0_gnn_bp1': _L0_gnn_in['bp1'], 'L0_gnn_Wm1': _L0_gnn_in['Wm1'], 'L0_gnn_bm1': _L0_gnn_in['bm1'], 'L0_gnn_Wm2': _L0_gnn_in['Wm2'], 'L0_gnn_bm2': _L0_gnn_in['bm2'], 'L0_gnn_Wm3': _L0_gnn_in['Wm3'], 'L0_gnn_bm3': _L0_gnn_in['bm3'], 'L0_gnn_ln2_g': _L0_gnn_in['ln2_g'], 'L0_gnn_ln2_b': _L0_gnn_in['ln2_b'], 'L0_gnn_ln3_g': _L0_gnn_in['ln3_g'], 'L0_gnn_ln3_b': _L0_gnn_in['ln3_b'], 'L0_ffn_Wg': _L0_ffn_in['Wg'], 'L0_ffn_bg': _L0_ffn_in['bg'], 'L0_ffn_W1': _L0_ffn_in['W1'], 'L0_ffn_b1': _L0_ffn_in['b1'], 'L0_ffn_W2': _L0_ffn_in['W2'], 'L0_ffn_b2': _L0_ffn_in['b2'], 'L1_gnn_W': _L1_gnn_in['W'], 'L1_gnn_a_src': _L1_gnn_in['a_src'], 'L1_gnn_a_dst': _L1_gnn_in['a_dst'], 'L1_gnn_edge_W': _L1_gnn_in['edge_W'], 'L1_gnn_edge_b': _L1_gnn_in['edge_b'], 'L1_gnn_bias': _L1_gnn_in['bias'], 'L1_ffn_gate_w': _L1_ffn_in['gate_w'], 'L1_ffn_gate_b': _L1_ffn_in['gate_b'], 'L1_ffn_w1': _L1_ffn_in['w1'], 'L1_ffn_w2': _L1_ffn_in['w2'], 'L1_ffn_w3': _L1_ffn_in['w3']}

def reference(x, src, dst, edge_attr_3, L0_gnn_Wp1, L0_gnn_bp1, L0_gnn_Wm1, L0_gnn_bm1, L0_gnn_Wm2, L0_gnn_bm2, L0_gnn_Wm3, L0_gnn_bm3, L0_gnn_ln2_g, L0_gnn_ln2_b, L0_gnn_ln3_g, L0_gnn_ln3_b, L0_ffn_Wg, L0_ffn_bg, L0_ffn_W1, L0_ffn_b1, L0_ffn_W2, L0_ffn_b2, L1_gnn_W, L1_gnn_a_src, L1_gnn_a_dst, L1_gnn_edge_W, L1_gnn_edge_b, L1_gnn_bias, L1_ffn_gate_w, L1_ffn_gate_b, L1_ffn_w1, L1_ffn_w2, L1_ffn_w3):
    import jax
    import jax.numpy as jnp

    def _L0_gnn_ref(embeddings, edge_src, edge_dst, Wp1, bp1, Wm1, bm1, Wm2, bm2, Wm3, bm3, ln2_g, ln2_b, ln3_g, ln3_b):
        import jax, jax.numpy as jnp
        import numpy as np
        N = 3125
        E = 25000
        EMB = 256
        HID = 256
        EPS = 1e-05

        def _pool_max(h, edge_src, edge_dst):
            pooled = jax.ops.segment_max(h[edge_src], edge_dst, num_segments=N)
            cnt = jax.ops.segment_sum(jnp.ones((edge_dst.shape[0],), h.dtype), edge_dst, num_segments=N)
            return jnp.where((cnt > 0)[:, None], pooled, jnp.zeros((), h.dtype))

        def _layernorm(x, g, b):
            mu = jnp.mean(x, axis=-1, keepdims=True)
            var = jnp.mean(jnp.square(x - mu), axis=-1, keepdims=True)
            return (x - mu) * jax.lax.rsqrt(var + EPS) * g + b
        h1 = jax.nn.relu(embeddings @ Wp1.T + bp1)
        p1 = _pool_max(h1, edge_src, edge_dst)
        x = jax.nn.relu(jnp.concatenate([embeddings, p1], axis=1) @ Wm1.T + bm1)
        p2 = _pool_max(x, edge_src, edge_dst)
        y2 = jax.nn.relu(jnp.concatenate([x, p2], axis=1) @ Wm2.T + bm2)
        x = _layernorm(y2 + x, ln2_g, ln2_b)
        p3 = _pool_max(x, edge_src, edge_dst)
        y3 = jax.nn.relu(jnp.concatenate([x, p3], axis=1) @ Wm3.T + bm3)
        x = _layernorm(y3 + x, ln3_g, ln3_b)
        return x

    def _L0_ffn_ref(x, Wg, bg, W1, b1, W2, b2):
        import jax, jax.numpy as jnp
        import numpy as np
        TOP_K = 2
        B, L, D = x.shape
        E = W1.shape[0]
        xf = x.reshape(-1, D)
        gate_logits = xf @ Wg + bg
        top_w, top_i = jax.lax.top_k(gate_logits, TOP_K)
        top_w = jax.nn.softmax(top_w, axis=-1)
        w_dense = jnp.sum(jax.nn.one_hot(top_i, E, dtype=xf.dtype) * top_w[..., None], axis=1)
        out = jnp.zeros_like(xf)
        for e in range(E):
            h = jax.nn.gelu(xf @ W1[e] + b1[e], approximate=False)
            out = out + w_dense[:, e:e + 1] * (h @ W2[e] + b2[e])
        return out.reshape(B, L, D)

    def _L1_gnn_ref(x, W, a_src, a_dst, edge_W, edge_b, bias, edge_attr, edge_index):
        import jax, jax.numpy as jnp
        import numpy as np
        N = 50000
        E = 12500
        IN = 256
        H = 8
        D = 32
        EF = 3
        n = x.shape[0]
        h = (x @ W.T).reshape(n, H, D)
        src, dst = (edge_index[0], edge_index[1])
        h_src = h[src]
        h_dst = h[dst]
        alpha = jnp.einsum('ehd,hd->eh', h_src, a_src) + jnp.einsum('ehd,hd->eh', h_dst, a_dst)
        enc = jax.nn.relu(edge_attr @ edge_W.T + edge_b).reshape(-1, H, D)
        alpha = alpha + jnp.sum(enc * h_dst, axis=-1)
        alpha = jnp.where(alpha >= 0, alpha, 0.2 * alpha)
        amax = jax.ops.segment_max(alpha, dst, num_segments=n)
        ex = jnp.exp(alpha - amax[dst])
        denom = jax.ops.segment_sum(ex, dst, num_segments=n)
        attn = ex / jnp.maximum(denom[dst], 1e-10)
        out = jax.ops.segment_sum(h_src * attn[..., None], dst, num_segments=n)
        return out.reshape(n, H * D) + bias

    def _L1_ffn_ref(x, gate_w, gate_b, w1, w2, w3):
        import jax, jax.numpy as jnp
        import numpy as np
        D_MODEL = 256
        N_EXPERTS = 16
        HIDDEN = 512
        SCALE = 0.02
        n_experts = w1.shape[0]
        logits = jnp.einsum('bsd,de->bse', x, gate_w) + gate_b
        probs = jax.nn.softmax(logits, axis=-1)
        top_probs, top_idx = jax.lax.top_k(probs, 2)
        top_probs = top_probs / jnp.sum(top_probs, axis=-1, keepdims=True)
        dispatch = jnp.sum(jax.nn.one_hot(top_idx, n_experts, dtype=x.dtype) * top_probs[..., None], axis=-2)
        h1 = jnp.einsum('bsd,edh->bseh', x, w1)
        h2 = jnp.einsum('bsd,edh->bseh', x, w2)
        hidden = jax.nn.silu(h1) * h2
        expert_out = jnp.einsum('bseh,eho->bseo', hidden, w3)
        return jnp.einsum('bseo,bse->bso', expert_out, dispatch)
    edge_index = jnp.stack([src, dst])
    x = x + _L0_gnn_ref(_layernorm(x, axis=-1), src, dst, L0_gnn_Wp1, L0_gnn_bp1, L0_gnn_Wm1, L0_gnn_bm1, L0_gnn_Wm2, L0_gnn_bm2, L0_gnn_Wm3, L0_gnn_bm3, L0_gnn_ln2_g, L0_gnn_ln2_b, L0_gnn_ln3_g, L0_gnn_ln3_b)
    x = x + _L0_ffn_ref(_layernorm(x, axis=-1)[None], L0_ffn_Wg, L0_ffn_bg, L0_ffn_W1, L0_ffn_b1, L0_ffn_W2, L0_ffn_b2)[0]
    x = x + _L1_gnn_ref(_layernorm(x, axis=-1), L1_gnn_W, L1_gnn_a_src, L1_gnn_a_dst, L1_gnn_edge_W, L1_gnn_edge_b, L1_gnn_bias, edge_attr_3, edge_index)
    x = x + _L1_ffn_ref(_layernorm(x, axis=-1)[None], L1_ffn_gate_w, L1_ffn_gate_b, L1_ffn_w1, L1_ffn_w2, L1_ffn_w3)[0]
    return x

_drawn_inputs = setup_inputs


def setup_inputs(seed=0):
    import zlib

    import numpy as np

    out = dict(_drawn_inputs(seed))
    spreads = {'L0_gnn_bp1': (0.0, 0.1),
     'L0_gnn_bm1': (0.0, 0.1),
     'L0_gnn_bm2': (0.0, 0.1),
     'L0_gnn_bm3': (0.0, 0.1),
     'L0_gnn_ln2_g': (1.0, 0.2),
     'L0_gnn_ln2_b': (0.0, 0.1),
     'L0_gnn_ln3_g': (1.0, 0.2),
     'L0_gnn_ln3_b': (0.0, 0.1),
     'L0_ffn_bg': (0.0, 0.1),
     'L0_ffn_b1': (0.0, 0.441),
     'L0_ffn_b2': (0.0, 0.1),
     'L1_gnn_edge_b': (0.0, 0.286),
     'L1_gnn_bias': (0.0, 0.1),
     'L1_ffn_gate_b': (0.0, 0.8)}
    factors = {'L1_ffn_gate_w': 5.935, 'L1_ffn_w1': 5.45, 'L1_ffn_w2': 5.417, 'L1_ffn_w3': 5.373}
    for name, (base, spread) in spreads.items():
        noise = np.random.default_rng([zlib.crc32(name.encode()), seed]).standard_normal(out[name].shape)
        drawn = base * np.exp(spread * noise) if base else spread * noise
        out[name] = jnp.asarray(drawn.astype(out[name].dtype))
    for name, factor in factors.items():
        out[name] = (out[name] * factor).astype(out[name].dtype)
    return out
```

```python
from contextlib import ExitStack, contextmanager

import concourse.bass as bass
from concourse import mybir

ALU = mybir.AluOpType
ACT = mybir.ActivationFunctionType
AX = mybir.AxisListType
F32 = mybir.dt.float32
BF16 = mybir.dt.bfloat16
I32 = mybir.dt.int32
U32 = mybir.dt.uint32

P = 128
N = 3125
NB = 25
NPAD = P * NB
E = 50000
EC = 392
EPAD = P * EC
D = 256
H = 8
HD = D // H
EF = 6
SRC, DST = 4, 5
BIG = 1e38
MAGIC = 12582912.0
EPS = 1e-5
ds = bass.ds


class DmaCount:

    def __init__(self, sem):
        self.sem, self.base = sem, 16

    def at(self, n):
        return self.base + n


class Chain:

    def __init__(self, eng, sem, at=0):
        self.eng, self.sem, self.n = eng, sem, at

    def mark(self, ins):
        self.n = self.n + 1
        ins.then_inc(self.sem, 1)

    def link(self, ins):
        self.mark(ins)
        self.eng.wait_ge(self.sem, self.n)


def staged(write):
    def run(g, *args, **kwargs):
        with g.stage():
            return write(g, *args, **kwargs)
    return run


class Program:

    def __init__(self, nc, ctx):
        self.nc, self.ctx = nc, ctx
        counts = lambda name, n: [DmaCount(ctx.enter_context(nc.semaphore(f"{name}{k}"))) for k in range(n)]
        self.dma_counts = counts("gpsimd_dma", 14)
        self.place_counts = counts("place_dma", 8)
        self.store_counts = counts("sync_store", 2)
        self.out_counts = counts("gpsimd_store", 2)

    def sem(self, name):
        handle = self.stage_ctx.enter_context(self.nc.semaphore(name))
        self.stage_sems.append(handle)
        return handle

    @contextmanager
    def stage(self):
        self.stage_sems = []
        with ExitStack() as self.stage_ctx:
            yield
            for handle in self.stage_sems:
                self.nc.gpsimd.sem_clear(handle)

    def sb(self, name, shape, dt=F32, ctx=None):
        return (ctx or self.ctx).enter_context(self.nc.sbuf_tensor("sb_" + name, shape, dt))

    def ps(self, name, shape, dt=F32, ctx=None):
        return (ctx or self.ctx).enter_context(self.nc.psum_tensor("ps_" + name, shape, dt))

    def dram(self, name, shape, dt=F32):
        return self.nc.dram_tensor("dram_" + name, shape, dt, kind="Internal").ap()


def floor_div(ch, eng, out, in_, by, ctx_tmp):
    ch.link(eng.tensor_scalar(ctx_tmp, in_, -(by - 1) / 2.0, 1.0 / by, ALU.add, ALU.mult))
    ch.link(eng.tensor_scalar(out, ctx_tmp, MAGIC, None, ALU.add))
    ch.link(eng.tensor_scalar(out, out, -MAGIC, None, ALU.add))


def resident(g):
    g.x = g.sb("x", [P, NB, D])
    g.cur = g.sb("cur", [P, NB, D])
    g.new = g.sb("new", [P, NB, D])
    g.src_at = g.sb("src_at", [P, EC], I32)
    g.dst_at = g.sb("dst_at", [P, EC], I32)
    g.keep = g.sb("keep", [P, EC])
    g.keep_neg = g.sb("keep_neg", [P, EC])
    g.cont = g.sb("cont", [P, P])
    g.cont_neg = g.sb("cont_neg", [P, P])


@staged
def constants(g, src):
    nc = g.nc
    g.ident = g.sb("ident", [P, P])
    g.identb = g.sb("identb", [P, P], BF16)
    g.below = g.sb("below", [P, P])
    g.belowb = g.sb("belowb", [P, P], BF16)
    g.ones = g.sb("ones", [P, P])
    g.node_base = g.sb("node_base", [P, P])
    g.ramp = g.sb("ramp", [P, P])
    zero_done, tri_done, ramp_done = g.sem("zero_done"), g.sem("tri_done"), g.sem("ramp_done")
    g.first_load = g.sb("first_load", [1, 32], I32)
    with nc.Block() as block:
        @block.sync
        def _(sp):
            for k, q in enumerate(g.store_counts):
                sp.dma_start(g.first_load[:, k:k + 1], src[k:k + 1].rearrange("(a n) -> a n", a=1)).then_inc(q.sem, 16)
            for q in g.store_counts:
                sp.wait_ge(q.sem, 16)

        @block.gpsimd
        def _(pool):
            for k, q in enumerate(g.dma_counts + g.place_counts + g.out_counts, 2):
                pool.dma_start(g.first_load[:, k:k + 1], src[k:k + 1].rearrange("(a n) -> a n", a=1)).then_inc(q.sem, 16)
            pool.memset(g.ident[:], 0.0).then_inc(zero_done, 1)
            pool.memset(g.below[:], 1.0).then_inc(zero_done, 1)
            pool.memset(g.ones[:], 1.0)
            pool.wait_ge(zero_done, 2)
            pool.affine_select(out=g.ident[:], in_=g.ident[:], compare_op=ALU.not_equal, fill=1.0,
                               base=0, pattern=[[-1, P]], channel_multiplier=1).then_inc(tri_done, 1)
            pool.affine_select(out=g.below[:], in_=g.below[:], compare_op=ALU.is_ge, fill=0.0,
                               base=-1, pattern=[[1, P]], channel_multiplier=-1).then_inc(tri_done, 1)
            pool.iota(g.ramp[:], pattern=[[1, P]], base=0, channel_multiplier=0,
                      allow_small_or_imprecise_dtypes=True).then_inc(ramp_done, 1)
            for q in g.dma_counts + g.place_counts + g.out_counts:
                pool.wait_ge(q.sem, 16)

        @block.vector
        def _(dve):
            dve.wait_ge(tri_done, 2)
            dve.tensor_copy(g.identb[:], g.ident[:])
            dve.tensor_copy(g.belowb[:], g.below[:])
            dve.wait_ge(ramp_done, 1)
            dve.tensor_scalar(g.node_base[:], g.ramp[:], float(NB), None, ALU.mult)


def load_edges(g, name, src, tile, sem, eng, width=1):
    full = E // EC
    rest = E - full * EC
    if width == 1:
        eng.dma_start(tile[0:full, :], src[0:full * EC].rearrange("(p c) -> p c", c=EC)).then_inc(sem, 16)
        eng.dma_start(tile[full:full + 1, 0:rest], src[full * EC:E].rearrange("(p c) -> p c", p=1)).then_inc(sem, 16)
    else:
        eng.dma_start(tile[0:full, :, :], src[0:full * EC, :].rearrange("(p c) w -> p c w", c=EC)).then_inc(sem, 16)
        eng.dma_start(tile[full:full + 1, 0:rest, :],
                      src[full * EC:E, :].rearrange("(p c) w -> p c w", p=1)).then_inc(sem, 16)


@staged
def sort_edges(g, src, dst, attr):
    nc = g.nc
    g.sorted_edges = g.dram("sorted_edges", [EPAD, EF])
    g.has_edge = g.sb("has_edge", [P, NB])
    g.carried = g.sb("carried", [P, NB])
    g.carried_neg = g.sb("carried_neg", [P, NB])
    g.last_at = g.sb("last_at", [P, NB], I32)
    g.last_part = g.sb("last_part", [P, NB], I32)
    g.unsorted = g.sb("unsorted", [P, 1], I32)
    sorted_v = g.sorted_edges.rearrange("(p c) f -> p c f", p=P)
    U = 8
    ROUNDS = EC // U
    loaded, filled = g.sem("edges_loaded"), g.sem("edges_filled")
    rows_ready, rows_stored = g.sem("rows_ready"), g.sem("rows_stored")
    hot_done, counted, ranged = g.sem("hot_done"), g.sem("counted"), g.sem("ranged")
    prefix_done, offsets_done, seeded, rows_done = (g.sem("prefix_done"), g.sem("offsets_done"),
                                                    g.sem("start_seeded"), g.sem("rows_done"))
    with ExitStack() as ctx:
        sb = lambda n, s, d=F32: g.sb(n, s, d, ctx)
        src_i, dst_i = sb("src_i", [P, EC], I32), sb("dst_i", [P, EC], I32)
        attr_t = sb("attr_t", [P, EC, 3])
        rows = sb("rows", [P, EC, EF])
        part_base, col = sb("part_base", [P, EC]), sb("col", [P, EC])
        hot_a, hot_b = sb("hot_a", [P, EC, P], BF16), sb("hot_b", [P, EC, NB], BF16)
        count, upto, row_sum, start, tmp = (sb("count", [P, NB]), sb("upto", [P, NB]),
                                            sb("row_sum", [P, 1]), sb("start", [P, NB]), sb("tmp_n", [P, NB]))
        part_of = sb("part_of", [P, NB])
        next_i, step_down = sb("next_i", [P, 1], I32), sb("step_down", [P, EC])
        next_dst, steps_down = sb("next_dst", [P, 1]), sb("steps_down", [P, 1])
        ps_count = g.ps("count", [P, 512], F32, ctx)

        with nc.Block() as block:
            @block.sync
            def _(sp):
                sp.wait_ge(filled, 4)
                load_edges(g, "dst", dst, dst_i, loaded, sp)
                load_edges(g, "src", src, src_i, loaded, sp)
                load_edges(g, "attr", attr, attr_t, loaded, sp, 3)
                sp.dma_start(next_i[0:P - 1, :], dst[EC:(P - 1) * EC + 1:EC].unsqueeze(1),
                             allow_slow_non_contiguous=True).then_inc(loaded, 16)
                sp.wait_ge(rows_ready, 1)
                sp.dma_start(sorted_v, rows[:]).then_inc(rows_stored, 16)
                sp.wait_ge(rows_stored, 16)

            @block.vector
            def _(dve):
                ch = Chain(dve, prefix_done)
                dve.memset(dst_i[:], N).then_inc(filled, 1)
                dve.memset(src_i[:], 0).then_inc(filled, 1)
                dve.memset(attr_t[:], 0.0).then_inc(filled, 1)
                dve.memset(next_i[:], N).then_inc(filled, 1)
                ch.mark(dve.memset(rows[:, :, 3:4], 1.0))
                dve.wait_ge(loaded, 112)
                ch.mark(dve.tensor_copy(rows[:, :, SRC], src_i[:]))
                ch.mark(dve.tensor_copy(rows[:, :, 0:3], attr_t[:]))
                ch.mark(dve.tensor_copy(next_dst[:], next_i[:]))
                ch.link(dve.tensor_copy(rows[:, :, DST], dst_i[:]))
                dve.sem_inc(rows_ready, 1)
                ch.mark(dve.tensor_tensor(step_down[:, 0:EC - 1], rows[:, 0:EC - 1, DST], rows[:, 1:EC, DST], ALU.is_gt))
                ch.link(dve.tensor_tensor(step_down[:, EC - 1:EC], rows[:, EC - 1:EC, DST], next_dst[:], ALU.is_gt))
                ch.link(dve.tensor_reduce(steps_down[:], step_down[:], AX.X, ALU.add))
                floor_div(ch, dve, part_base[:], rows[:, :, DST], NB, col[:])
                ch.link(dve.tensor_scalar(part_base[:], part_base[:], float(NB), None, ALU.mult))
                ch.link(dve.tensor_tensor(col[:], rows[:, :, DST], part_base[:], ALU.subtract))
                with dve.Fori(0, ROUNDS) as i:
                    dve.tensor_tensor(hot_a[:, ds(U * i, U), :],
                                      part_base[:, ds(U * i, U)].unsqueeze(2).broadcast_to([P, U, P]),
                                      g.node_base[:].unsqueeze(1).broadcast_to([P, U, P]),
                                      ALU.is_equal).then_inc(hot_done, 1)
                    dve.tensor_tensor(hot_b[:, ds(U * i, U), :],
                                      col[:, ds(U * i, U)].unsqueeze(2).broadcast_to([P, U, NB]),
                                      g.ramp[:, 0:NB].unsqueeze(1).broadcast_to([P, U, NB]),
                                      ALU.is_equal).then_inc(hot_done, 1)
                dve.wait_ge(counted, 1)
                ch.link(dve.tensor_copy(count[:], ps_count[:, 0:NB]))
                ch.link(dve.tensor_tensor_scan(upto[:], g.ones[:, 0:NB], count[:], 0.0, ALU.mult, ALU.add))
                dve.tensor_copy(row_sum[:], upto[:, NB - 1:NB]).then_inc(ranged, 1)
                dve.wait_ge(offsets_done, 1)
                dve.tensor_scalar(g.unsorted[:], ps_count[:, NB + 1:NB + 2], 1.0, None, ALU.min)
                ch.link(dve.tensor_scalar(upto[:], upto[:], ps_count[:, NB:NB + 1], None, ALU.add))
                dve.tensor_tensor(start[:], upto[:], count[:], ALU.subtract).then_inc(seeded, 1)
                dve.tensor_scalar(g.has_edge[:], count[:], 0.0, None, ALU.is_gt)
                ch.link(dve.tensor_scalar(tmp[:], upto[:], -1.0, 0.0, ALU.add, ALU.max))
                ch.mark(dve.tensor_copy(g.last_at[:], tmp[:]))
                floor_div(ch, dve, part_of[:], tmp[:], EC, upto[:])
                ch.mark(dve.tensor_copy(g.last_part[:], part_of[:]))
                ch.link(dve.tensor_scalar(part_of[:], part_of[:], float(EC), None, ALU.mult))
                dve.wait_ge(seeded, 1)
                ch.link(dve.tensor_tensor(g.carried[:], start[:], part_of[:], ALU.is_lt))
                dve.tensor_scalar(g.carried_neg[:], g.carried[:], -1.0, BIG, ALU.add, ALU.mult)

            @block.tensor
            def _(pe):
                pe.wait_ge(hot_done, 2)
                pe.matmul(ps_count[:, 0:NB], hot_a[:, 0, :], hot_b[:, 0, :], start=True, stop=False)
                for c in range(1, U):
                    pe.matmul(ps_count[:, 0:NB], hot_a[:, c, :], hot_b[:, c, :], start=False, stop=False)
                with pe.Fori(1, ROUNDS - 1) as i:
                    pe.wait_ge(hot_done, 2 * i + 2)
                    for c in range(U):
                        pe.matmul(ps_count[:, 0:NB], hot_a[:, ds(U * i + c, 1), :].rearrange("p a b -> p (a b)"),
                                  hot_b[:, ds(U * i + c, 1), :].rearrange("p a b -> p (a b)"),
                                  start=False, stop=False)
                pe.wait_ge(hot_done, 2 * ROUNDS)
                for c in range(EC - U, EC):
                    last = pe.matmul(ps_count[:, 0:NB], hot_a[:, c, :], hot_b[:, c, :],
                                     start=False, stop=(c == EC - 1))
                last.then_inc(counted, 1)
                pe.wait_ge(ranged, 1)
                pe.matmul(ps_count[:, NB:NB + 1], g.below[:], row_sum[:], start=True, stop=True)
                pe.matmul(ps_count[:, NB + 1:NB + 2], g.ones[:], steps_down[:], start=True, stop=True)\
                  .then_inc(offsets_done, 1)

        place_edges(g, ctx, rows, hot_a, hot_b, start)


def place_edges(g, ctx, rows, hot_a, hot_b, start):
    nc = g.nc
    U = 8
    ROUNDS = EC // U
    sb = lambda n, s, d=F32: g.sb(n, s, d, ctx)
    hotT_f = sb("hotT_f", [P, U, P])
    hotT_b = sb("hotT_b", [P, U, P], BF16)
    seen = sb("seen", [P, U, NB])
    same = sb("same", [P, U, P], BF16)
    picked = sb("picked", [P, U, NB])
    pos_f = sb("pos_f", [P, U])
    pos_i = sb("pos_i", [P, U], I32)
    row_slot = sb("row_slot", [P, U, EF])
    ps_hotT = g.ps("hotT", [P, 2, 1024], BF16, ctx)
    ps_same = g.ps("same", [P, 2, 512], F32, ctx)
    ps_seen = g.ps("seen", [P, 512], F32, ctx)
    ps_pos = g.ps("pos", [P, 2, 512], F32, ctx)
    turned, turned_copied = g.sem("hot_turned"), g.sem("hot_turned_copied")
    seen_ready, seen_copied = g.sem("seen_ready"), g.sem("seen_copied")
    same_ready, same_cut = g.sem("same_ready"), g.sem("same_cut")
    pos_ready, pos_picked = g.sem("pos_ready"), g.sem("pos_picked")
    block_ready, gate, own = g.sem("edge_block_ready"), g.sem("scatter_gate"), g.sem("place_chain")
    placed = g.place_counts

    with nc.Block() as block:
        @block.tensor
        def _(pe):
            unsorted = pe.value_load(g.unsorted[0:1, 0:1], min_val=0, max_val=1)
            with pe.If(unsorted > 0):
                pe.matmul(ps_seen[:, 0:NB], g.ident[:], start[:], start=True, stop=True).then_inc(seen_ready, 1)

                def step(c, k, last=False):
                    hot = hot_a[:, k_ap(c), :].rearrange("p a b -> p (a b)")
                    hot_col = hot_b[:, k_ap(c), :].rearrange("p a b -> p (a b)")
                    pe.wait_ge(turned_copied, c + 1)
                    pe.transpose(ps_hotT[:, k % 2, 0:P], hot, g.identb[:]).then_inc(turned, 1)
                    pe.wait_ge(turned_copied, c + 3)
                    pe.wait_ge(same_cut, c + 1)
                    pe.matmul(ps_same[:, k % 2, 0:P], hotT_b[:, k, :], hotT_b[:, k, :], start=True, stop=True)\
                      .then_inc(same_ready, 1)
                    pe.wait_ge(seen_copied, c + 1)
                    pe.wait_ge(pos_picked, c + 1)
                    pe.matmul(ps_pos[:, k % 2, 0:NB], hotT_f[:, k, :], seen[:, k, :], start=True, stop=False)
                    pe.wait_ge(same_cut, c + 3)
                    pe.matmul(ps_pos[:, k % 2, 0:NB], same[:, k, :], hot_col, start=False, stop=True)\
                      .then_inc(pos_ready, 1)
                    pe.matmul(ps_seen[:, 0:NB], hot, hot_col, start=False, stop=True,
                              skip_group_check=True).then_inc(seen_ready, 1)

                def k_ap(c):
                    return ds(c, 1)

                with pe.Fori(0, ROUNDS) as i:
                    for k in range(U):
                        step(U * i + k, k)

        @block.scalar
        def _(act):
            unsorted = act.value_load(g.unsorted[0:1, 0:1], min_val=0, max_val=1)
            with act.If(unsorted > 0):
                act.preload_act_table(ACT.Copy)
                act.sem_inc(turned_copied, 2)
                with act.Fori(0, ROUNDS) as i:
                    for k in range(U):
                        act.wait_ge(placed[k].sem, placed[k].at(16 * i))
                    act.activation(row_slot[:], rows[:, ds(U * i, U), :], ACT.Copy).then_inc(block_ready, 1)
                    for k in range(U):
                        c = U * i + k
                        act.wait_ge(seen_ready, c + 1)
                        act.activation(seen[:, k, :], ps_seen[:, 0:NB], ACT.Copy).then_inc(seen_copied, 1)
                        act.wait_ge(turned, c + 1)
                        act.activation(hotT_b[:, k, :], ps_hotT[:, k % 2, 0:P], ACT.Copy)
                        act.activation(hotT_f[:, k, :], ps_hotT[:, k % 2, 0:P], ACT.Copy)\
                           .then_inc(turned_copied, 1)

        @block.vector
        def _(dve):
            unsorted = dve.value_load(g.unsorted[0:1, 0:1], min_val=0, max_val=1)
            with dve.If(unsorted > 0):
                dve.sem_inc(same_cut, 2)
                dve.sem_inc(pos_picked, 2)
                with dve.Fori(0, ROUNDS) as i:
                    for k in range(U):
                        c = U * i + k
                        dve.wait_ge(same_ready, c + 1)
                        dve.tensor_tensor(same[:, k, :], ps_same[:, k % 2, 0:P], g.below[:], ALU.mult)\
                           .then_inc(same_cut, 1)
                        dve.wait_ge(pos_ready, c + 1)
                        dve.scalar_tensor_tensor(out=picked[:, k, :], in0=ps_pos[:, k % 2, 0:NB], scalar=0.0,
                                                 in1=hot_b[:, ds(c, 1), :].rearrange("p a b -> p (a b)"),
                                                 op0=ALU.add, op1=ALU.mult, accum_out=pos_f[:, k:k + 1])\
                           .then_inc(pos_picked, 1)
                    for k in range(U):
                        dve.wait_ge(placed[k].sem, placed[k].at(16 * i))
                    dve.wait_ge(pos_picked, U * i + U + 2)
                    dve.tensor_copy(pos_i[:], pos_f[:]).then_inc(own, 1)

        @block.gpsimd
        def _(pool):
            unsorted = pool.value_load(g.unsorted[0:1, 0:1], min_val=0, max_val=1)
            with pool.If(unsorted > 0):
                with pool.Fori(0, ROUNDS) as i:
                    pool.wait_ge(own, i + 1)
                    pool.wait_ge(block_ready, i + 1)
                    pool.sem_inc(gate, 1)
                    for k in range(U):
                        pool.wait_ge(gate, 1)
                        pool.indirect_dma_start(
                            out=g.sorted_edges, out_offset=bass.IndirectOffsetOnAxis(ap=pos_i[:, k:k + 1], axis=0),
                            in_=row_slot[:, k, :], in_offset=None).then_inc(placed[k].sem, 16)
                for k in range(U):
                    pool.wait_ge(placed[k].sem, placed[k].at(16 * ROUNDS))


@staged
def edge_tables(g, x):
    nc = g.nc
    loaded, filled, ready, turned = (g.sem("sorted_loaded"), g.sem("tables_filled"),
                                     g.sem("tables_chain"), g.sem("cont_turned"))
    g.edge_rows = g.sb("edge_rows", [P, EC, EF])
    g.before = g.sb("before", [P, 1])
    g.after = g.sb("after", [P, 1])
    sorted_v = g.sorted_edges.rearrange("(p c) f -> p c f", p=P)
    with ExitStack() as ctx:
        goes_on = g.sb("goes_on", [P, 1], ctx=ctx)
        goes_on_row = g.sb("goes_on_row", [P, P], ctx=ctx)
        ps_cont = g.ps("cont", [P, 512], ctx=ctx)
        with nc.Block() as block:
            @block.sync
            def _(sp):
                sp.dma_start(g.edge_rows[:], sorted_v).then_inc(loaded, 16)
                sp.wait_ge(filled, 3)
                sp.dma_start(g.before[1:P, :], sorted_v[0:P - 1, EC - 1, DST:DST + 1], allow_slow_non_contiguous=True).then_inc(loaded, 16)
                sp.dma_start(g.after[0:P - 1, :], sorted_v[1:P, 0, DST:DST + 1], allow_slow_non_contiguous=True).then_inc(loaded, 16)
                sp.dma_start(g.x[0:N // NB, :, :], x.rearrange("(a b) f -> a b f", b=NB)).then_inc(loaded, 16)
                sp.wait_ge(loaded, 64)

            @block.vector
            def _(dve):
                ch = Chain(dve, ready)
                dve.memset(g.before[:], -1.0).then_inc(filled, 1)
                dve.memset(g.after[:], -1.0).then_inc(filled, 1)
                dve.memset(g.x[:], 0.0).then_inc(filled, 1)
                dve.wait_ge(loaded, 64)
                dst = g.edge_rows[:, :, DST]
                dve.tensor_copy(g.src_at[:], g.edge_rows[:, :, SRC])
                dve.tensor_copy(g.dst_at[:], dst)
                ch.mark(dve.memset(g.keep[:, 0:1], 0.0))
                ch.mark(dve.tensor_tensor(g.keep[:, 1:EC], dst[:, 1:EC], dst[:, 0:EC - 1], ALU.is_equal))
                ch.link(dve.tensor_tensor(goes_on[:], dst[:, EC - 1:EC], g.before[:], ALU.is_equal))
                ch.mark(dve.tensor_scalar(g.keep_neg[:], g.keep[:], -1.0, BIG, ALU.add, ALU.mult))
                ch.mark(dve.tensor_scalar(goes_on_row[:], g.ones[:], goes_on[:, 0:1], None, ALU.mult))
                dve.wait_ge(turned, 1)
                ch.link(dve.tensor_copy(g.cont[:], ps_cont[:, 0:P]))
                dve.tensor_scalar(g.cont_neg[:], g.cont[:], -1.0, BIG, ALU.add, ALU.mult)

            @block.tensor
            def _(pe):
                pe.wait_ge(ready, 5)
                pe.matmul(ps_cont[:, 0:P], goes_on_row[:], g.ident[:], start=True, stop=True).then_inc(turned, 1)


@staged
def layer_weights(g, w):
    nc = g.nc
    layers = ["L0_gnn_Wp1", "L0_gnn_Wm1", "L0_gnn_Wm2", "L0_gnn_Wm3", "L1_gnn_W"]
    rows = ["L0_gnn_bp1", "L0_gnn_bm1", "L0_gnn_bm2", "L0_gnn_bm3"]
    spread = ["L0_gnn_ln2_g", "L0_gnn_ln2_b", "L0_gnn_ln3_g", "L0_gnn_ln3_b", "L1_gnn_bias"]
    g.w, g.row, g.wide = {}, {}, {}
    for n in layers:
        g.w[n] = g.sb(n, [P, w[n].shape[1] // P, D])
    for n in rows:
        g.row[n] = g.sb(n, [1, D])
    for n in spread:
        g.wide[n] = g.sb(n, [P, D])
    loaded, turned, copied = g.sem("weights_loaded"), g.sem("weights_turned"), g.sem("weights_copied")
    small = g.sem("small_loaded")
    with ExitStack() as ctx:
        raw = {n: g.sb("raw_" + n, [P, 2, w[n].shape[1]], ctx=ctx) for n in layers}
        ps = g.ps("weights", [P, 2, 512], ctx=ctx)
        blocks = [(n, k) for n in layers for k in range(w[n].shape[1] // P)]
        with nc.Block() as block:
            @block.sync
            def _(sp):
                for n in layers:
                    sp.dma_start(raw[n][:], w[n].rearrange("(o p) k -> p o k", p=P)).then_inc(loaded, 16)
                for n in rows:
                    sp.dma_start(g.row[n][:], w[n].rearrange("(a n) -> a n", a=1)).then_inc(small, 16)
                for n in spread:
                    sp.dma_start(g.wide[n][:], w[n].rearrange("(a n) -> a n", a=1).broadcast_to([P, D]))\
                      .then_inc(small, 16)
                sp.wait_ge(small, 16 * (len(rows) + len(spread)))

            @block.tensor
            def _(pe):
                pe.wait_ge(loaded, 16 * len(layers))
                for j, (n, k) in enumerate(blocks):
                    if j >= 2:
                        pe.wait_ge(copied, j - 1)
                    for o in range(2):
                        last = pe.transpose(ps[:, j % 2, o * P:(o + 1) * P], raw[n][:, o, k * P:(k + 1) * P], g.ident[:])
                    last.then_inc(turned, 1)

            @block.vector
            def _(dve):
                for j, (n, k) in enumerate(blocks):
                    dve.wait_ge(turned, j + 1)
                    dve.tensor_copy(g.w[n][:, k, :], ps[:, j % 2, 0:D]).then_inc(copied, 1)


@staged
def normalise(g, name, src, out, scale=None, shift=None, add_to=None, table=None):
    nc = g.nc
    R = 5
    own, var_ready, std_ready, stored, done = (g.sem(name + "_chain"), g.sem(name + "_var"),
                                               g.sem(name + "_std"), g.sem(name + "_stored"),
                                               g.sem(name + "_done"))
    with ExitStack() as ctx:
        stats = g.sb(name + "_stats", [P, R, 6], ctx=ctx)
        moments = g.sb(name + "_moments", [P, R, 2], ctx=ctx)
        mean, var = g.sb(name + "_mean", [P, NB], ctx=ctx), g.sb(name + "_variance", [P, NB], ctx=ctx)
        std = g.sb(name + "_stdev", [P, NB], ctx=ctx)
        tmp = g.sb(name + "_tmp", [P, 2, D], ctx=ctx)
        with nc.Block() as block:
            @block.vector
            def _(dve):
                PER = 2 * R + 2
                with dve.Fori(0, NB // R) as i:
                    ch = Chain(dve, own, PER * i)
                    for k in range(R):
                        ch.mark(dve.bn_stats(stats[:, k, :], src[:, ds(R * i + k, 1), :].rearrange("p a f -> p (a f)")))
                    dve.wait_ge(own, ch.n)
                    dve.sem_inc(done, 1)
                    dve.wait_ge(done, 1)
                    for k in range(R):
                        ch.mark(dve.bn_aggr(moments[:, k, :], stats[:, k, :]))
                    dve.wait_ge(own, ch.n)
                    ch.mark(dve.tensor_copy(mean[:, ds(R * i, R)], moments[:, :, 0]))
                    ch.link(dve.tensor_scalar(var[:, ds(R * i, R)], moments[:, :, 1], EPS, None, ALU.add))
                at = PER * (NB // R)
                ch = Chain(dve, own, at)
                dve.tensor_copy(var[:, 0:1], var[:, 0:1]).then_inc(var_ready, 1)
                dve.wait_ge(std_ready, 1)
                ch.link(dve.reciprocal(std[:], std[:]))
                at += 1
                PER = 2 if scale is not None else 1
                with dve.Fori(0, NB) as i:
                    ch = Chain(dve, own, at + PER * i)
                    x_b, out_b = (t[:, ds(i, 1), :].rearrange("p a f -> p (a f)") for t in (src, out))
                    if scale is None:
                        ch.mark(dve.tensor_scalar(out_b, x_b, mean[:, ds(i, 1)], std[:, ds(i, 1)],
                                                  ALU.subtract, ALU.mult))
                    else:
                        ch.link(dve.scalar_tensor_tensor(out=tmp[:, 0, :], in0=x_b, scalar=mean[:, ds(i, 1)],
                                                         in1=scale, op0=ALU.subtract, op1=ALU.mult))
                        ch.link(dve.scalar_tensor_tensor(out=out_b, in0=tmp[:, 0, :], scalar=std[:, ds(i, 1)],
                                                         in1=shift, op0=ALU.mult, op1=ALU.add))
                dve.wait_ge(own, at + PER * NB)
                if add_to is not None:
                    dve.tensor_tensor(add_to[:], add_to[:], out[:], ALU.add)

            @block.scalar
            def _(act):
                act.wait_ge(var_ready, 1)
                act.activation(std[:], var[:], ACT.Sqrt).then_inc(std_ready, 1)

            if table is not None:
                @block.sync
                def _(sp):
                    sp.wait_ge(own, PER_TOTAL(scale))
                    sp.dma_start(table.rearrange("(p b) f -> p b f", p=P), out[:]).then_inc(stored, 16)
                    sp.wait_ge(stored, 16)


def PER_TOTAL(scale):
    return 12 * (NB // 5) + 1 + (2 if scale is not None else 1) * NB


@staged
def pool_max(g, name, table, states, carries):
    nc = g.nc
    HALF = 7
    U = 2 * HALF
    ROUNDS = EC // U
    indices, reached, turned, carried = (g.sem(name + "_indices"), g.sem(name + "_reached"),
                                         g.sem(name + "_turned"), g.sem(name + "_carried"))
    gate, out_done = g.sem(name + "_gate"), g.sem(name + "_carries_stored")
    got = g.dma_counts[0:U]
    stored = g.store_counts
    states_v = states.rearrange("(p c) f -> p c f", p=P)
    with ExitStack() as ctx:
        index = g.sb(name + "_index", [P, U], I32, ctx)
        rows = g.sb(name + "_rows", [P, U, D], ctx=ctx)
        state = g.sb(name + "_state", [P, U, D], ctx=ctx)
        runs = g.sb(name + "_runs", [P, 2, P + 1], ctx=ctx)
        carry = g.sb(name + "_carry", [P, D], ctx=ctx)
        ps_t = g.ps(name + "_t", [P, 512], ctx=ctx)
        ps_c = g.ps(name + "_c", [P, 512], ctx=ctx)
        with nc.Block() as block:
            @block.scalar
            def _(act):
                act.preload_act_table(ACT.Copy)
                with act.Fori(0, ROUNDS) as i:
                    for h in range(2):
                        act.wait_ge(reached, U * i + HALF * (h + 1))
                        act.copy(index[:, HALF * h:HALF * (h + 1)], g.src_at[:, ds(U * i + HALF * h, HALF)])\
                           .then_inc(indices, 1)

            @block.gpsimd
            def _(pool):
                with pool.Fori(0, ROUNDS) as i:
                    for h in range(2):
                        pool.wait_ge(indices, 2 * i + h + 1)
                        pool.sem_inc(gate, 1)
                        for k in range(HALF * h, HALF * (h + 1)):
                            pool.wait_ge(gate, 1)
                            pool.indirect_dma_start(
                                out=rows[:, k, :], out_offset=None, in_=table,
                                in_offset=bass.IndirectOffsetOnAxis(ap=index[:, k:k + 1], axis=0)).then_inc(got[k].sem, 16)

            @block.vector
            def _(dve):
                dve.memset(state[:, U - 1, :], -BIG).then_inc(reached, U)
                dve.memset(runs[:, :, 0:1], -BIG)
                with dve.Fori(0, ROUNDS) as i:
                    for k in range(U):
                        if k % HALF == 0:
                            dve.wait_ge(stored[k // HALF].sem, stored[k // HALF].at(16 * i))
                        dve.wait_ge(got[k].sem, got[k].at(16 * i + 16))
                        dve.wait_ge(reached, U * i + U + k)
                        dve.scalar_tensor_tensor(out=state[:, k, :], in0=state[:, (k - 1) % U, :],
                                                 scalar=g.keep_neg[:, ds(U * i + k, 1)], in1=rows[:, k, :],
                                                 op0=ALU.add, op1=ALU.max).then_inc(reached, 1)
                dve.wait_ge(turned, 1)
                for j in range(2):
                    last = dve.tensor_tensor_scan(runs[:, j, 1:P + 1], g.cont_neg[:], ps_t[:, j * P:(j + 1) * P],
                                                  -BIG, ALU.add, ALU.max)
                last.then_inc(carried, 1)
                dve.wait_ge(turned, 2)
                dve.tensor_copy(carry[:], ps_c[:, 0:D]).then_inc(carried, 1)

            @block.tensor
            def _(pe):
                pe.wait_ge(reached, U + EC)
                for j in range(2):
                    last = pe.transpose(ps_t[:, j * P:(j + 1) * P], state[:, U - 1, j * P:(j + 1) * P], g.ident[:])
                last.then_inc(turned, 1)
                pe.wait_ge(carried, 1)
                for j in range(2):
                    last = pe.transpose(ps_c[:, j * P:(j + 1) * P], runs[:, j, 0:P], g.ident[:])
                last.then_inc(turned, 1)

            @block.sync
            def _(sp):
                with sp.Fori(0, ROUNDS) as i:
                    for h in range(2):
                        sp.wait_ge(reached, U * i + U + HALF * (h + 1))
                        sp.dma_start(states_v[:, ds(U * i + HALF * h, HALF), :],
                                     state[:, HALF * h:HALF * (h + 1), :]).then_inc(stored[h].sem, 16)
                sp.wait_ge(carried, 2)
                sp.dma_start(carries, carry[:]).then_inc(out_done, 16)
                for h in range(2):
                    sp.wait_ge(stored[h].sem, stored[h].at(16 * ROUNDS))
                sp.wait_ge(out_done, 16)
    for q in got + stored:
        q.base += 16 * ROUNDS


@staged
def dense(g, name, x, weights, bias, width, finish, out, table=None, pooled=None):
    nc = g.nc
    R = 5
    nk = 2 * (2 if pooled else 1)
    x_in, row_turned, row_copied, multiplied, finished = (
        g.sem(name + "_x_in"), g.sem(name + "_turned"), g.sem(name + "_copied"),
        g.sem(name + "_multiplied"), g.sem(name + "_finished"))
    own, stored = g.sem(name + "_chain"), g.sem(name + "_stored")
    if pooled:
        indices, gate, pool_in = g.sem(name + "_indices"), g.sem(name + "_gate"), g.sem(name + "_pool_in")
        got = g.dma_counts[0:R]
    with ExitStack() as ctx:
        sb = lambda n, s, d=F32: g.sb(name + "_" + n, s, d, ctx)
        slot = sb("slot", [P, R, D])
        turned = sb("slot_turned", [P, R, nk * P])
        if pooled:
            at, part = sb("at", [P, R], I32), sb("part", [P, R], I32)
            last_row, carry_row, best = sb("last_row", [P, R, D]), sb("carry_row", [P, R, D]), sb("best", [P, R, D])
        if finish == "attention":
            by_head = sb("by_head", [P, 2, D])
        ps_t = g.ps(name + "_t", [P, 3, 512], ctx=ctx)
        ps_y = g.ps(name + "_y", [P, R, 512], ctx=ctx)
        with nc.Block() as block:
            @block.scalar
            def _(act):
                act.preload_act_table(ACT.Copy)
                act.sem_inc(row_copied, 2)
                with act.Fori(0, NB // R) as i:
                    if pooled:
                        for k in range(R):
                            act.wait_ge(got[k].sem, got[k].at(32 * i))
                        act.copy(at[:], g.last_at[:, ds(R * i, R)])
                        act.copy(part[:], g.last_part[:, ds(R * i, R)]).then_inc(indices, 1)
                    for k in range(R):
                        act.wait_ge(row_turned, R * i + k + 1)
                        act.copy(slot[:, k, :], x[:, ds(R * i + k, 1), :].rearrange("p a f -> p (a f)"))\
                           .then_inc(x_in, 1)
                    for k in range(R):
                        b = R * i + k
                        act.wait_ge(row_turned, b + 1 + R)
                        act.wait_ge(multiplied, b + 1)
                        act.copy(turned[:, k, :], ps_t[:, k % 3, 0:nk * P]).then_inc(row_copied, 1)

            if pooled:
                @block.gpsimd
                def _(pool):
                    states, carries = pooled
                    with pool.Fori(0, NB // R) as i:
                        pool.wait_ge(indices, i + 1)
                        pool.wait_ge(pool_in, R * i + 1)
                        pool.sem_inc(gate, 1)
                        for k in range(R):
                            pool.wait_ge(gate, 1)
                            pool.indirect_dma_start(
                                out=last_row[:, k, :], out_offset=None, in_=states,
                                in_offset=bass.IndirectOffsetOnAxis(ap=at[:, k:k + 1], axis=0)).then_inc(got[k].sem, 16)
                            pool.indirect_dma_start(
                                out=carry_row[:, k, :], out_offset=None, in_=carries,
                                in_offset=bass.IndirectOffsetOnAxis(ap=part[:, k:k + 1], axis=0)).then_inc(got[k].sem, 16)

            @block.tensor
            def _(pe):
                pe.sem_inc(row_turned, R)
                pe.sem_inc(multiplied, R)
                with pe.Fori(0, NB // R) as i:
                    def turn(k):
                        b = R * i + k
                        pe.wait_ge(x_in, b + 1)
                        pe.wait_ge(row_copied, b + 1)
                        for j in range(2):
                            last = pe.transpose(ps_t[:, k % 3, j * P:(j + 1) * P], slot[:, k, j * P:(j + 1) * P], g.ident[:])
                        if pooled:
                            pe.wait_ge(pool_in, b + 2)
                            for j in range(2):
                                last = pe.transpose(ps_t[:, k % 3, (2 + j) * P:(3 + j) * P],
                                                    best[:, k, j * P:(j + 1) * P], g.ident[:])
                        last.then_inc(row_turned, 1)

                    def multiply(k):
                        b = R * i + k
                        pe.wait_ge(row_copied, b + 3)
                        pe.wait_ge(finished, b + 1)
                        for j in range(nk):
                            last = pe.matmul(ps_y[:, k, 0:width], turned[:, k, j * P:(j + 1) * P], weights[:, j, :],
                                             start=(j == 0), stop=(j == nk - 1 and bias is None))
                        if bias is not None:
                            last = pe.matmul(ps_y[:, k, 0:width], g.ones[0:1, :], bias, start=False, stop=True)
                        last.then_inc(multiplied, 1)

                    turn(0)
                    for k in range(1, R):
                        turn(k)
                        multiply(k - 1)
                    multiply(R - 1)

            @block.vector
            def _(dve):
                dve.sem_inc(finished, R)
                if pooled:
                    dve.sem_inc(pool_in, 1)
                PER = R * ((2 if pooled else 0) + (5 if finish == "attention" else 0))
                with dve.Fori(0, NB // R) as i:
                    ch = Chain(dve, own, PER * i)
                    if pooled:
                        for k in range(R):
                            b = ds(R * i + k, 1)
                            dve.wait_ge(got[k].sem, got[k].at(32 * i + 32))
                            dve.wait_ge(row_turned, R * i + k + 1)
                            ch.link(dve.scalar_tensor_tensor(out=last_row[:, k, :], in0=carry_row[:, k, :],
                                                             scalar=g.carried_neg[:, b], in1=last_row[:, k, :],
                                                             op0=ALU.add, op1=ALU.max))
                            ch.mark(dve.tensor_scalar(best[:, k, :], last_row[:, k, :], g.has_edge[:, b], None,
                                                      ALU.mult))
                            dve.wait_ge(own, ch.n)
                            dve.sem_inc(pool_in, 1)
                    for k in range(R):
                        dve.wait_ge(multiplied, R * i + k + 1 + R)
                        out_b = out[:, ds(R * i + k, 1), :].rearrange("p a f -> p (a f)")
                        y = ps_y[:, k, 0:width]
                        if finish == "relu":
                            dve.tensor_scalar(out_b, y, 0.0, None, ALU.max).then_inc(finished, 1)
                        elif finish == "relu_add":
                            dve.scalar_tensor_tensor(out=out_b, in0=y, scalar=0.0,
                                                     in1=x[:, ds(R * i + k, 1), :].rearrange("p a f -> p (a f)"),
                                                     op0=ALU.max, op1=ALU.add).then_inc(finished, 1)
                        elif finish == "copy":
                            dve.tensor_copy(out_b, y).then_inc(finished, 1)
                        else:
                            ch.mark(dve.tensor_tensor(by_head[:, 0, :], y, g.wide["a_src"][:], ALU.mult))
                            ch.link(dve.tensor_tensor(by_head[:, 1, :], y, g.wide["a_dst"][:], ALU.mult))
                            for j in range(2):
                                ch.mark(dve.tensor_reduce(out_b[:, D + H * j:D + H * (j + 1)],
                                                          by_head[:, j, :].rearrange("p (h d) -> p h d", h=H), AX.X, ALU.add))
                            ch.link(dve.tensor_copy(out_b[:, 0:D], y))
                            dve.sem_inc(finished, 1)

            if table is not None:
                @block.sync
                def _(sp):
                    table_v = table.rearrange("(p b) f -> p b f", p=P)
                    with sp.Fori(0, NB // R) as i:
                        sp.wait_ge(finished, R * i + 2 * R)
                        sp.dma_start(table_v[:, ds(R * i, R), :], out[:, ds(R * i, R), :]).then_inc(stored, 16)
                    sp.wait_ge(stored, 16 * (NB // R))
    if pooled:
        for q in got:
            q.base += 32 * (NB // R)


@staged
def attention_weights(g, w):
    nc = g.nc
    G = 8
    g.encode = g.sb("encode", [G * EF, G, D])
    for n in ("a_src", "a_dst"):
        g.wide[n] = g.sb(n, [P, D])
    zeroed, loaded = g.sem("encode_zeroed"), g.sem("encode_loaded")
    with nc.Block() as block:
        @block.vector
        def _(dve):
            dve.memset(g.encode[:], 0.0).then_inc(zeroed, 1)

        @block.sync
        def _(sp):
            for n in ("a_src", "a_dst"):
                sp.dma_start(g.wide[n][:], w["L1_gnn_" + n].rearrange("(a h) d -> a (h d)", a=1).broadcast_to([P, D]))\
                  .then_inc(loaded, 16)
            sp.wait_ge(zeroed, 1)
            for j in range(G):
                sp.dma_start(g.encode[EF * j:EF * j + 3, j, :], w["L1_gnn_edge_W"].rearrange("o f -> f o"),
                             allow_slow_non_contiguous=True).then_inc(loaded, 16)
                sp.dma_start(g.encode[EF * j + 3:EF * j + 4, j, :], w["L1_gnn_edge_b"].rearrange("(a n) -> a n", a=1))\
                  .then_inc(loaded, 16)
            sp.wait_ge(loaded, 16 * (2 + 2 * G))


@staged
def edge_scores(g, name, table, source_rows, scores):
    nc = g.nc
    HALF = 4
    U = 2 * HALF
    ROUNDS = EC // U
    W = D + 2 * H
    indices, edges_in, edges_turned, edges_ready = (
        g.sem(name + "_indices"), g.sem(name + "_edges_in"), g.sem(name + "_edges_turned"),
        g.sem(name + "_edges_ready"))
    encoded, weighed, scored, own, gate = (g.sem(name + "_encoded"), g.sem(name + "_weighed"),
                                           g.sem(name + "_scored"), g.sem(name + "_chain"), g.sem(name + "_gate"))
    turn_gate = g.sem(name + "_turn_gate")
    got = g.dma_counts[0:U]
    stored = g.store_counts
    source_v = source_rows.rearrange("(p c) f -> p c f", p=P)
    with ExitStack() as ctx:
        sb = lambda n, s, d=F32: g.sb(name + "_" + n, s, d, ctx)
        src_slot, dst_slot = sb("src_slot", [P, U], I32), sb("dst_slot", [P, U], I32)
        at_dst, at_src = sb("at_dst", [P, U, W]), sb("at_src", [P, U, W])
        group, group_t = sb("group", [P, U * EF]), sb("group_t", [U * EF, P])
        prod = sb("prod", [P, 2, HALF, D])
        part = sb("part", [P, 2, HALF, H])
        ps_g = g.ps(name + "_g", [P, 512], ctx=ctx)
        ps_e = g.ps(name + "_e", [P, U, D], ctx=ctx)
        with nc.Block() as block:
            @block.scalar
            def _(act):
                act.preload_act_table(ACT.Copy)
                act.sem_inc(edges_ready, 1)
                with act.Fori(0, ROUNDS) as i:
                    for h in range(2):
                        act.wait_ge(scored, 2 * i + h + 1)
                        act.wait_ge(stored[h].sem, stored[h].at(16 * i))
                        cols = slice(HALF * h, HALF * (h + 1))
                        act.copy(src_slot[:, cols], g.src_at[:, ds(U * i + HALF * h, HALF)])
                        act.copy(dst_slot[:, cols], g.dst_at[:, ds(U * i + HALF * h, HALF)]).then_inc(indices, 1)
                        if h == 0:
                            act.wait_ge(edges_turned, i + 1)
                            act.copy(group[:], g.edge_rows[:, ds(U * i, U), :].rearrange("p c f -> p (c f)"))\
                               .then_inc(edges_in, 1)
                            act.wait_ge(edges_turned, i + 2)
                            act.wait_ge(encoded, 2 * i + 1)
                            act.copy(group_t[:], ps_g[0:U * EF, 0:P]).then_inc(edges_ready, 1)

            @block.gpsimd
            def _(pool):
                with pool.Fori(0, ROUNDS) as i:
                    for h in range(2):
                        pool.wait_ge(indices, 2 * i + h + 1)
                        pool.sem_inc(gate, 1)
                        for k in range(HALF * h, HALF * (h + 1)):
                            for rows, slot in ((at_dst, dst_slot), (at_src, src_slot)):
                                pool.wait_ge(gate, 1)
                                pool.indirect_dma_start(
                                    out=rows[:, k, :], out_offset=None, in_=table,
                                    in_offset=bass.IndirectOffsetOnAxis(ap=slot[:, k:k + 1], axis=0))\
                                    .then_inc(got[k].sem, 16)

            @block.tensor
            def _(pe):
                pe.sem_inc(edges_turned, 1)
                pe.sem_inc(encoded, 1)
                with pe.Fori(0, ROUNDS) as i:
                    pe.wait_ge(edges_in, i + 1)
                    pe.wait_ge(edges_ready, i + 1)
                    pe.sem_inc(turn_gate, 1)
                    pe.wait_ge(turn_gate, 1)
                    pe.transpose(ps_g[0:U * EF, 0:P], group[:], g.ident[:]).then_inc(edges_turned, 1)
                    pe.wait_ge(edges_ready, i + 2)
                    for h in range(2):
                        pe.wait_ge(weighed, 2 * i + h + 1)
                        for k in range(HALF * h, HALF * (h + 1), 2):
                            last = pe.matmul(ps_e[:, k:k + 2, :].rearrange("p a f -> p (a f)"), group_t[:],
                                             g.encode[:, k:k + 2, :].rearrange("p a f -> p (a f)"),
                                             start=True, stop=True)
                        last.then_inc(encoded, 1)

            @block.vector
            def _(dve):
                dve.sem_inc(weighed, 2)
                dve.sem_inc(scored, 2)
                PER = 3
                with dve.Fori(0, ROUNDS) as i:
                    for h in range(2):
                        ch = Chain(dve, own, PER * (2 * i + h))
                        cols = slice(HALF * h, HALF * (h + 1))
                        for k in range(HALF * h, HALF * (h + 1)):
                            dve.wait_ge(got[k].sem, got[k].at(32 * i + 32))
                        dve.wait_ge(encoded, 2 * i + h + 2)
                        dve.scalar_tensor_tensor(out=prod[:, h, :, :], in0=ps_e[:, cols, :], scalar=0.0,
                                                 in1=at_dst[:, cols, 0:D], op0=ALU.max, op1=ALU.mult)\
                           .then_inc(weighed, 1)
                        ch.mark(dve.tensor_tensor(part[:, h, :, :], at_dst[:, cols, D + H:W],
                                                  at_src[:, cols, D:D + H], ALU.add))
                        dve.wait_ge(weighed, 2 * i + h + 3)
                        out = scores[:, ds(U * i + HALF * h, HALF), :].rearrange("p c h -> p (c h)")
                        ch.mark(dve.tensor_reduce(out, prod[:, h, :, :].rearrange("p c (h d) -> p (c h) d", h=H),
                                                  AX.X, ALU.add))
                        dve.wait_ge(own, ch.n)
                        ch.mark(dve.tensor_tensor(out, out, part[:, h, :, :].rearrange("p c h -> p (c h)"), ALU.add))
                        dve.wait_ge(own, ch.n)
                        dve.sem_inc(scored, 1)

            @block.sync
            def _(sp):
                with sp.Fori(0, ROUNDS) as i:
                    for h in range(2):
                        sp.wait_ge(weighed, 2 * i + h + 3)
                        sp.dma_start(source_v[:, ds(U * i + HALF * h, HALF), :],
                                     at_src[:, HALF * h:HALF * (h + 1), 0:D]).then_inc(stored[h].sem, 16)
                for h in range(2):
                    sp.wait_ge(stored[h].sem, stored[h].at(16 * ROUNDS))
    for q in got:
        q.base += 32 * ROUNDS
    for q in stored:
        q.base += 16 * ROUNDS


@staged
def edge_softmax(g, scores):
    nc = g.nc
    own, ready, turned, shifted, done = (g.sem("softmax_chain"), g.sem("softmax_ends"), g.sem("softmax_turned"),
                                         g.sem("softmax_shifted"), g.sem("softmax_done"))
    with ExitStack() as ctx:
        sb = lambda n, s, d=F32: g.sb("softmax_" + n, s, d, ctx)
        fore, back = sb("fore", [P, EC, H]), sb("back", [P, EC, H])
        next_neg = sb("next_neg", [P, EC])
        in_first, in_last = sb("in_first", [P, EC]), sb("in_last", [P, EC])
        ends = sb("ends", [P, 2, H])
        runs = sb("runs", [H, 2, P + 1])
        on = sb("on", [P, 1])
        on_row = sb("on_row", [P, P])
        on_neg = sb("on_neg", [P, P])
        carry = sb("carry", [P, 2, H])
        ps_e = g.ps("softmax_e", [P, 512], ctx=ctx)
        ps_o = g.ps("softmax_o", [P, 512], ctx=ctx)
        ps_c = g.ps("softmax_c", [P, 512], ctx=ctx)
        dst = g.edge_rows[:, :, DST]
        with nc.Block() as block:
            @block.vector
            def _(dve):
                ch = Chain(dve, own)
                ch.mark(dve.tensor_tensor(next_neg[:, 0:EC - 1], dst[:, 1:EC], dst[:, 0:EC - 1], ALU.is_equal))
                ch.mark(dve.memset(next_neg[:, EC - 1:EC], 0.0))
                ch.mark(dve.tensor_scalar(in_first[:], dst, g.before[:, 0:1], None, ALU.is_equal))
                ch.mark(dve.tensor_scalar(in_last[:], dst, g.after[:, 0:1], None, ALU.is_equal))
                ch.mark(dve.memset(runs[:], -BIG))
                ch.mark(dve.tensor_tensor(on[:], dst[:, 0:1], g.after[:], ALU.is_equal))
                ch.link(dve.scalar_tensor_tensor(out=scores[:], in0=scores[:], scalar=0.2, in1=scores[:],
                                                 op0=ALU.mult, op1=ALU.max))
                ch.mark(dve.tensor_scalar(next_neg[:], next_neg[:], -1.0, BIG, ALU.add, ALU.mult))
                ch.mark(dve.tensor_scalar(in_first[:], in_first[:], -1.0, BIG, ALU.add, ALU.mult))
                ch.mark(dve.tensor_scalar(in_last[:], in_last[:], -1.0, BIG, ALU.add, ALU.mult))
                ch.link(dve.tensor_scalar(on_row[:], g.ones[:], on[:, 0:1], None, ALU.mult))
                for h in range(H):
                    ch.mark(dve.tensor_tensor_scan(fore[:, :, h], g.keep_neg[:], scores[:, :, h], -BIG,
                                                   ALU.add, ALU.max))
                    ch.mark(dve.tensor_tensor_scan(back[:, ::-1, h], next_neg[:, ::-1], scores[:, ::-1, h], -BIG,
                                                   ALU.add, ALU.max))
                dve.wait_ge(own, ch.n)
                ch.link(dve.tensor_copy(ends[:, 0, :], fore[:, EC - 1, :]))
                dve.tensor_copy(ends[:, 1, :], back[:, 0, :]).then_inc(ready, 1)
                ch.link(dve.tensor_tensor(fore[:], fore[:], back[:], ALU.max))
                dve.wait_ge(turned, 1)
                ch.link(dve.tensor_scalar(on_neg[:], ps_o[:, 0:P], -1.0, BIG, ALU.add, ALU.mult))
                ch.mark(dve.tensor_tensor_scan(runs[:, 0, 1:P + 1], g.cont_neg[0:H, :], ps_e[0:H, 0:P], -BIG,
                                               ALU.add, ALU.max))
                dve.tensor_tensor_scan(runs[:, 1, P - 1::-1], on_neg[0:H, ::-1], ps_e[0:H, 2 * P - 1:P - 1:-1], -BIG,
                                       ALU.add, ALU.max).then_inc(shifted, 1)
                dve.wait_ge(own, ch.n)
                dve.wait_ge(turned, 2)
                ch.link(dve.tensor_copy(carry[:], ps_c[:, 0:2 * H].rearrange("p (a h) -> p a h", a=2)))
                for j, mask in enumerate((in_first, in_last)):
                    for h in range(H):
                        ch.mark(dve.scalar_tensor_tensor(out=fore[:, :, h], in0=mask[:], scalar=carry[:, j, h:h + 1],
                                                         in1=fore[:, :, h], op0=ALU.add, op1=ALU.max))
                    dve.wait_ge(own, ch.n)
                dve.tensor_tensor(scores[:], scores[:], fore[:], ALU.subtract).then_inc(done, 1)

            @block.tensor
            def _(pe):
                pe.wait_ge(ready, 1)
                pe.transpose(ps_e[0:H, 0:P], ends[:, 0, :], g.ident[:])
                pe.transpose(ps_e[0:H, P:2 * P], ends[:, 1, :], g.ident[:])
                pe.matmul(ps_o[:, 0:P], on_row[:], g.ident[:], start=True, stop=True).then_inc(turned, 1)
                pe.wait_ge(shifted, 1)
                pe.transpose(ps_c[:, 0:H], runs[:, 0, 0:P], g.ident[0:H, 0:H])
                pe.transpose(ps_c[:, H:2 * H], runs[:, 1, 1:P + 1], g.ident[0:H, 0:H]).then_inc(turned, 1)

            @block.scalar
            def _(act):
                act.wait_ge(done, 1)
                act.activation(scores[:], scores[:], ACT.Exp)


@staged
def edge_sums(g, name, source_rows, scores, states, carries):
    nc = g.nc
    HALF = 7
    U = 2 * HALF
    ROUNDS = EC // U
    W = D + H
    weighted, weights_in, reached, turned, carried, out_done = (
        g.sem(name + "_weighted"), g.sem(name + "_weights_in"), g.sem(name + "_reached"),
        g.sem(name + "_turned"), g.sem(name + "_carried"), g.sem(name + "_carries_stored"))
    loaded = [g.sem(f"{name}_loaded{h}") for h in range(2)]
    stored = g.store_counts
    states_v = states.rearrange("(p c) f -> p c f", p=P)
    source_v = source_rows.rearrange("(p c) f -> p c f", p=P)
    blocks = [(0, P), (P, P), (2 * P, H)]
    with ExitStack() as ctx:
        sb = lambda n, s, d=F32: g.sb(name + "_" + n, s, d, ctx)
        rows, part, state = sb("rows", [P, U, D]), sb("part", [P, U, W]), sb("state", [P, U, W])
        runs = sb("runs", [P, 3, P + 1])
        carry = sb("carry", [P, W])
        ps_t = g.ps(name + "_t", [P, 512], ctx=ctx)
        ps_c = g.ps(name + "_c", [P, 512], ctx=ctx)
        with nc.Block() as block:
            @block.sync
            def _(sp):
                with sp.Fori(0, ROUNDS) as i:
                    for h in range(2):
                        sp.wait_ge(reached, U * i + U + HALF * (h + 1))
                        sp.dma_start(states_v[:, ds(U * i + HALF * h, HALF), :],
                                     state[:, HALF * h:HALF * (h + 1), :]).then_inc(stored[h].sem, 16)
                sp.wait_ge(carried, 2)
                sp.dma_start(carries, carry[:]).then_inc(out_done, 16)
                for h in range(2):
                    sp.wait_ge(stored[h].sem, stored[h].at(16 * ROUNDS))
                sp.wait_ge(out_done, 16)

            @block.gpsimd
            def _(pool):
                pool.sem_inc(weighted, 2)
                with pool.Fori(0, ROUNDS) as i:
                    for h in range(2):
                        cols = slice(HALF * h, HALF * (h + 1))
                        at = ds(U * i + HALF * h, HALF)
                        pool.wait_ge(loaded[h], 16 * i + 16)
                        pool.wait_ge(reached, U * i + HALF * (h + 1))
                        pool.tensor_tensor(part[:, cols, 0:D].rearrange("p c (h d) -> p c h d", h=H),
                                           rows[:, cols, :].rearrange("p c (h d) -> p c h d", h=H),
                                           scores[:, at, :].unsqueeze(3).broadcast_to([P, HALF, H, HD]),
                                           ALU.mult).then_inc(weighted, 1)

            @block.scalar
            def _(act):
                act.preload_act_table(ACT.Copy)
                with act.Fori(0, ROUNDS) as i:
                    for h in range(2):
                        act.wait_ge(weighted, 2 * i + h + 1)
                        act.dma_start(rows[:, HALF * h:HALF * (h + 1), :],
                                      source_v[:, ds(U * i + HALF * h, HALF), :]).then_inc(loaded[h], 16)
                    for h in range(2):
                        act.wait_ge(reached, U * i + HALF * (h + 1))
                        act.copy(part[:, HALF * h:HALF * (h + 1), D:W], scores[:, ds(U * i + HALF * h, HALF), :])\
                           .then_inc(weights_in, 1)

            @block.vector
            def _(dve):
                dve.memset(state[:, U - 1, :], 0.0).then_inc(reached, U)
                dve.memset(runs[:, :, 0:1], 0.0)
                with dve.Fori(0, ROUNDS) as i:
                    for k in range(U):
                        if k % HALF == 0:
                            dve.wait_ge(stored[k // HALF].sem, stored[k // HALF].at(16 * i))
                            dve.wait_ge(weighted, 2 * i + k // HALF + 3)
                            dve.wait_ge(weights_in, 2 * i + k // HALF + 1)
                        dve.wait_ge(reached, U * i + U + k)
                        dve.scalar_tensor_tensor(out=state[:, k, :], in0=state[:, (k - 1) % U, :],
                                                 scalar=g.keep[:, ds(U * i + k, 1)], in1=part[:, k, :],
                                                 op0=ALU.mult, op1=ALU.add).then_inc(reached, 1)
                dve.wait_ge(turned, 1)
                for j, (_, n) in enumerate(blocks):
                    last = dve.tensor_tensor_scan(runs[0:n, j, 1:P + 1], g.cont[0:n, :], ps_t[0:n, j * P:(j + 1) * P],
                                                  0.0, ALU.mult, ALU.add)
                last.then_inc(carried, 1)
                dve.wait_ge(turned, 2)
                dve.tensor_copy(carry[:], ps_c[:, 0:W]).then_inc(carried, 1)

            @block.tensor
            def _(pe):
                pe.wait_ge(reached, U + EC)
                for j, (at, n) in enumerate(blocks):
                    last = pe.transpose(ps_t[0:n, j * P:(j + 1) * P], state[:, U - 1, at:at + n], g.ident[:])
                last.then_inc(turned, 1)
                pe.wait_ge(carried, 1)
                for j, (at, n) in enumerate(blocks):
                    last = pe.transpose(ps_c[:, at:at + n], runs[0:n, j, 0:P], g.ident[0:n, 0:n])
                last.then_inc(turned, 1)
    for q in stored:
        q.base += 16 * ROUNDS


@staged
def attend(g, name, states, carries, x, bias):
    nc = g.nc
    R = 5
    W = D + H
    indices, gate, own, used = g.sem(name + "_indices"), g.sem(name + "_gate"), g.sem(name + "_chain"), g.sem(name + "_used")
    got = g.dma_counts[0:R]
    with ExitStack() as ctx:
        sb = lambda n, s, d=F32: g.sb(name + "_" + n, s, d, ctx)
        at, part = sb("at", [P, R], I32), sb("part", [P, R], I32)
        last_row, carry_row = sb("last_row", [P, R, W]), sb("carry_row", [P, R, W])
        with nc.Block() as block:
            @block.scalar
            def _(act):
                act.preload_act_table(ACT.Copy)
                with act.Fori(0, NB // R) as i:
                    act.wait_ge(used, R * i + 1)
                    act.copy(at[:], g.last_at[:, ds(R * i, R)])
                    act.copy(part[:], g.last_part[:, ds(R * i, R)]).then_inc(indices, 1)

            @block.gpsimd
            def _(pool):
                with pool.Fori(0, NB // R) as i:
                    pool.wait_ge(indices, i + 1)
                    pool.sem_inc(gate, 1)
                    for k in range(R):
                        for rows, table, slot in ((last_row, states, at), (carry_row, carries, part)):
                            pool.wait_ge(gate, 1)
                            pool.indirect_dma_start(
                                out=rows[:, k, :], out_offset=None, in_=table,
                                in_offset=bass.IndirectOffsetOnAxis(ap=slot[:, k:k + 1], axis=0))\
                                .then_inc(got[k].sem, 16)

            @block.vector
            def _(dve):
                PER = 6 * R
                dve.sem_inc(used, 1)
                with dve.Fori(0, NB // R) as i:
                    ch = Chain(dve, own, PER * i)
                    for k in range(R):
                        b = ds(R * i + k, 1)
                        dve.wait_ge(got[k].sem, got[k].at(32 * i + 32))
                        ch.link(dve.scalar_tensor_tensor(out=last_row[:, k, :], in0=carry_row[:, k, :],
                                                         scalar=g.carried[:, b], in1=last_row[:, k, :],
                                                         op0=ALU.mult, op1=ALU.add))
                        ch.link(dve.tensor_scalar(last_row[:, k, :], last_row[:, k, :], g.has_edge[:, b], None,
                                                  ALU.mult))
                        ch.link(dve.tensor_scalar(carry_row[:, k, 0:H], last_row[:, k, D:W], 1e-10, None, ALU.max))
                        ch.link(dve.reciprocal(carry_row[:, k, 0:H], carry_row[:, k, 0:H]))
                        ch.link(dve.tensor_tensor(last_row[:, k, 0:D].rearrange("p (h d) -> p h d", h=H),
                                                  last_row[:, k, 0:D].rearrange("p (h d) -> p h d", h=H),
                                                  carry_row[:, k, 0:H].unsqueeze(2).broadcast_to([P, H, HD]), ALU.mult))
                        x_b = x[:, b, :].rearrange("p a f -> p (a f)")
                        ch.link(dve.tensor_tensor(x_b, x_b, last_row[:, k, 0:D], ALU.add))
                        dve.sem_inc(used, 1)
                dve.tensor_tensor(x[:], x[:], bias.unsqueeze(1).broadcast_to([P, NB, D]), ALU.add)
    for q in got:
        q.base += 32 * (NB // R)


class Mixture:

    def __init__(self, g, name, experts, hidden, gated):
        self.name, self.experts, self.hidden, self.gated = name, experts, hidden, gated
        self.pairs = 2 * NB
        tiles = (P * self.pairs + experts * (P - 1)) // P
        self.tiles = tiles + tiles % 2
        self.rows_in = g.dram(name + "_rows_in", [self.tiles * P, D])
        self.rows_out = g.dram(name + "_rows_out", [self.tiles * P, D])


@staged
def clear_rows(g, m):
    nc = g.nc
    zeroed, cleared = g.sem("rows_zeroed"), g.sem("rows_cleared")
    with ExitStack() as ctx:
        zero = g.sb(m.name + "_zero_rows", [P, D], ctx=ctx)
        with nc.Block() as block:
            @block.vector
            def _(dve):
                dve.memset(zero[:], 0.0).then_inc(zeroed, 1)

            @block.sync
            def _(sp):
                sp.wait_ge(zeroed, 1)
                sp.dma_start(m.rows_in.rearrange("(p t) f -> p t f", p=P),
                             zero[:].unsqueeze(1).broadcast_to([P, m.tiles, D])).then_inc(cleared, 16)
                sp.wait_ge(cleared, 16)


@staged
def route(g, m, logits):
    nc = g.nc
    n, X, C = m.name, m.experts, m.pairs
    m.row = g.sb(n + "_row", [P, C], I32, m.ctx)
    m.weight = g.sb(n + "_weight", [P, C], ctx=m.ctx)
    m.tile_expert = g.sb(n + "_tile_expert", [P, m.tiles], I32, m.ctx)
    own, gap_ready, exp_ready, summed, totals = (g.sem(n + "_chain"), g.sem(n + "_gap"), g.sem(n + "_exp"),
                                                 g.sem(n + "_summed"), g.sem(n + "_totals"))
    with ExitStack() as ctx:
        sb = lambda k, s, d=F32: g.sb(n + "_" + k, s, d, ctx)
        best, which = sb("best", [P, NB, 8]), sb("which", [P, NB, 8], U32)
        chosen, hot, upto = sb("chosen", [P, NB, 2]), sb("hot", [P, C, X]), sb("upto", [P, C, X])
        gap, total = sb("gap", [P, NB]), sb("total", [P, NB])
        across, expert_sum = sb("across", [P, X]), sb("expert_sum", [P, X])
        tiles_of, tiles_upto, base = sb("tiles_of", [P, X]), sb("tiles_upto", [P, X]), sb("base", [P, X])
        row_f, passed, tile_f = sb("row_f", [P, C]), sb("passed", [P, m.tiles, X]), sb("tile_f", [P, m.tiles])
        ps = g.ps(n + "_route", [P, 2, 512], ctx=ctx)
        with nc.Block() as block:
            @block.vector
            def _(dve):
                ch = Chain(dve, own)
                for b in range(NB):
                    ch.mark(dve.max(best[:, b, :], logits[:, b, 0:X]))
                dve.wait_ge(own, ch.n)
                for b in range(NB):
                    ch.mark(dve.max_index(which[:, b, :], best[:, b, :], logits[:, b, 0:X]))
                dve.tensor_tensor(gap[:], best[:, :, 1], best[:, :, 0], ALU.subtract).then_inc(gap_ready, 1)
                dve.wait_ge(own, ch.n)
                ch.link(dve.tensor_copy(chosen[:], which[:, :, 0:2]))
                ch.link(dve.tensor_tensor(hot[:], chosen[:].rearrange("p b j -> p (b j)").unsqueeze(2).broadcast_to([P, C, X]),
                                          g.ramp[:, 0:X].unsqueeze(1).broadcast_to([P, C, X]), ALU.is_equal))
                for e in range(X):
                    ch.mark(dve.tensor_tensor_scan(upto[:, :, e], g.ones[:, 0:C], hot[:, :, e], 0.0, ALU.mult, ALU.add))
                dve.wait_ge(own, ch.n)
                dve.tensor_copy(expert_sum[:], upto[:, C - 1, :]).then_inc(summed, 1)
                dve.wait_ge(exp_ready, 1)
                ch.link(dve.tensor_scalar(total[:], gap[:], 1.0, None, ALU.add))
                ch.link(dve.reciprocal(total[:], total[:]))
                pair = m.weight[:].rearrange("p (b j) -> p b j", j=2)
                dve.tensor_copy(pair[:, :, 0], total[:])
                dve.tensor_tensor(pair[:, :, 1], gap[:], total[:], ALU.mult)
                dve.wait_ge(totals, 1)
                ch.mark(dve.tensor_copy(across[:], ps[:, 0, 0:X]))
                ch.link(dve.tensor_scalar(expert_sum[:], ps[:, 1, 0:X], float(P - 1), None, ALU.add))
                floor_div(ch, dve, tiles_of[:], expert_sum[:], P, base[:])
                ch.link(dve.tensor_tensor_scan(tiles_upto[:], g.ones[:, 0:X], tiles_of[:], 0.0, ALU.mult, ALU.add))
                ch.link(dve.tensor_tensor(base[:], tiles_upto[:], tiles_of[:], ALU.subtract))
                ch.link(dve.scalar_tensor_tensor(out=base[:], in0=base[:], scalar=float(P), in1=across[:],
                                                 op0=ALU.mult, op1=ALU.add))
                ch.link(dve.tensor_tensor(upto[:], upto[:], base[:].unsqueeze(1).broadcast_to([P, C, X]), ALU.add))
                ch.link(dve.tensor_tensor(upto[:], upto[:], hot[:], ALU.mult))
                ch.link(dve.tensor_reduce(row_f[:], upto[:], AX.X, ALU.add))
                ch.link(dve.tensor_scalar(row_f[:], row_f[:], -1.0, None, ALU.add))
                dve.tensor_copy(m.row[:], row_f[:])
                ch.link(dve.tensor_tensor(passed[:], g.ramp[:, 0:m.tiles].unsqueeze(2).broadcast_to([P, m.tiles, X]),
                                          tiles_upto[:].unsqueeze(1).broadcast_to([P, m.tiles, X]), ALU.is_ge))
                ch.link(dve.tensor_reduce(tile_f[:], passed[:], AX.X, ALU.add))
                ch.link(dve.tensor_scalar(tile_f[:], tile_f[:], float(X - 1), None, ALU.min))
                dve.tensor_copy(m.tile_expert[:], tile_f[:])

            @block.scalar
            def _(act):
                act.wait_ge(gap_ready, 1)
                act.activation(gap[:], gap[:], ACT.Exp).then_inc(exp_ready, 1)

            @block.tensor
            def _(pe):
                pe.wait_ge(summed, 1)
                pe.matmul(ps[:, 0, 0:X], g.below[:], expert_sum[:], start=True, stop=True)
                pe.matmul(ps[:, 1, 0:X], g.ones[:], expert_sum[:], start=True, stop=True).then_inc(totals, 1)


@staged
def dispatch(g, m, x):
    nc = g.nc
    R = 5
    indices, gate = g.sem(m.name + "_indices"), g.sem(m.name + "_gate")
    sent = g.dma_counts[0:R]
    with ExitStack() as ctx:
        slot = g.sb(m.name + "_slot", [P, R, D], ctx=ctx)
        row = g.sb(m.name + "_row_slot", [P, 2 * R], I32, ctx)
        with nc.Block() as block:
            @block.scalar
            def _(act):
                act.preload_act_table(ACT.Copy)
                with act.Fori(0, NB // R) as i:
                    for k in range(R):
                        act.wait_ge(sent[k].sem, sent[k].at(32 * i))
                    act.copy(row[:], m.row[:, ds(2 * R * i, 2 * R)])
                    act.copy(slot[:], x[:, ds(R * i, R), :]).then_inc(indices, 1)

            @block.gpsimd
            def _(pool):
                with pool.Fori(0, NB // R) as i:
                    pool.wait_ge(indices, i + 1)
                    pool.sem_inc(gate, 1)
                    for k in range(R):
                        for j in range(2):
                            c = 2 * k + j
                            pool.wait_ge(gate, 1)
                            pool.indirect_dma_start(
                                out=m.rows_in, out_offset=bass.IndirectOffsetOnAxis(ap=row[:, c:c + 1], axis=0),
                                in_=slot[:, k, :], in_offset=None).then_inc(sent[k].sem, 16)
                for k in range(R):
                    pool.wait_ge(sent[k].sem, sent[k].at(32 * (NB // R)))
    for q in sent:
        q.base += 32 * (NB // R)


@staged
def gelu_biases(g, m, b1, b2):
    nc = g.nc
    X, HC = m.experts, m.hidden // P
    m.b1 = g.sb(m.name + "_b1", [P, X, HC], ctx=m.ctx)
    m.b2 = g.sb(m.name + "_b2", [P, X, D], ctx=m.ctx)
    loaded, turned = g.sem("biases_loaded"), g.sem("biases_turned")
    with ExitStack() as ctx:
        raw = g.sb(m.name + "_b1_raw", [X, m.hidden], ctx=ctx)
        ps = g.ps(m.name + "_b1", [P, 512], ctx=ctx)
        with nc.Block() as block:
            @block.sync
            def _(sp):
                sp.dma_start(raw[:], b1).then_inc(loaded, 16)
                sp.dma_start(m.b2[:], b2.unsqueeze(0).broadcast_to([P, X, D])).then_inc(loaded, 16)
                sp.wait_ge(loaded, 32)

            @block.tensor
            def _(pe):
                pe.wait_ge(loaded, 32)
                for c in range(HC):
                    last = pe.transpose(ps[:, c * X:(c + 1) * X], raw[:, c * P:(c + 1) * P], g.ident[0:X, 0:X])
                last.then_inc(turned, 1)

            @block.vector
            def _(dve):
                dve.wait_ge(turned, 1)
                dve.tensor_copy(m.b1[:].rearrange("p e c -> p c e"), ps[:, 0:HC * X].rearrange("p (c e) -> p c e", c=HC))


@staged
def experts(g, m, weights_in, weights_out):
    nc = g.nc
    n, HC = m.name, m.hidden // P
    NI = len(weights_in)
    COLS = HC * NI * P
    T = m.tiles
    row_loaded = [g.sem(f"{n}_row_loaded{s}") for s in range(2)]
    w_in_loaded = [g.sem(f"{n}_w_in_loaded{s}") for s in range(2)]
    w_out_loaded = [g.sem(f"{n}_w_out_loaded{s}") for s in range(2)]
    turned, copied, hidden_ready, active, out_ready, out_copied = (
        g.sem(n + "_rows_turned"), g.sem(n + "_rows_copied"), g.sem(n + "_hidden"), g.sem(n + "_active"),
        g.sem(n + "_out"), g.sem(n + "_out_copied"))
    half_active, gate = g.sem(n + "_half_active"), g.sem(n + "_load_gate")
    stored = g.out_counts
    rows_in = m.rows_in.rearrange("(t p) f -> p t f", p=P)
    rows_out = m.rows_out.rearrange("(t p) f -> p t f", p=P)
    with ExitStack() as ctx:
        sb = lambda k, s, d=F32: g.sb(n + "_" + k, s, d, ctx)
        w_in = sb("w_in", [P, 2, NI, 2, m.hidden])
        w_out = sb("w_out", [P, 2, HC, D])
        row, row_t = sb("rows", [P, 2, D]), sb("rows_t", [P, 2, 2 * P])
        act_t = sb("act_t", [P, 2, HC * P])
        gate_t = sb("gate_t", [P, 2, HC * P]) if m.gated else None
        out = sb("out", [P, 2, D])
        ps_t = g.ps(n + "_t", [P, 2, 512], ctx=ctx)
        ps_h = g.ps(n + "_h", [P, 2, COLS], ctx=ctx)
        ps_o = g.ps(n + "_o", [P, 2, 512], ctx=ctx)
        with nc.Block() as block:
            @block.sync
            def _(sp):
                with sp.Fori(0, T // 2) as i:
                    for s in range(2):
                        expert = sp.value_load(m.tile_expert[0:1, ds(2 * i + s, 1)], min_val=0, max_val=m.experts - 1)
                        sp.wait_ge(turned, 2 * i + s + 1)
                        sp.sem_inc(gate, 1)
                        sp.wait_ge(gate, 1)
                        sp.dma_start(row[:, s, :], rows_in[:, ds(2 * i + s, 1), :].rearrange("p a f -> p (a f)"))\
                          .then_inc(row_loaded[s], 16)
                        sp.wait_ge(hidden_ready, 2 * i + s + 1)
                        sp.sem_inc(gate, 1)
                        sp.wait_ge(gate, 1)
                        for j in range(NI):
                            sp.dma_start(w_in[:, s, j, :, :], weights_in[j][ds(expert, 1), :, :]
                                         .rearrange("e (k p) h -> p (e k) h", p=P)).then_inc(w_in_loaded[s], 16)
                        sp.wait_ge(out_ready, 2 * i + s + 1)
                        sp.sem_inc(gate, 1)
                        sp.wait_ge(gate, 1)
                        sp.dma_start(w_out[:, s, :, :], weights_out[ds(expert, 1), :, :]
                                     .rearrange("e (k p) h -> p (e k) h", p=P)).then_inc(w_out_loaded[s], 16)

            @block.tensor
            def _(pe):
                pe.sem_inc(turned, 2)
                pe.sem_inc(hidden_ready, 2)
                pe.sem_inc(out_ready, 2)

                def hidden(t, s, rnd):
                    pe.wait_ge(row_loaded[s], 16 * rnd + 16)
                    pe.wait_ge(copied, t + 1)
                    for j in range(2):
                        last = pe.transpose(ps_t[:, s, j * P:(j + 1) * P], row[:, s, j * P:(j + 1) * P], g.ident[:])
                    last.then_inc(turned, 1)
                    pe.wait_ge(copied, t + 3)
                    pe.wait_ge(w_in_loaded[s], 16 * NI * (rnd + 1))
                    pe.wait_ge(active, t + 1)
                    for j in range(NI):
                        for c in range(HC):
                            for k in range(2):
                                last = pe.matmul(ps_h[:, s, (j * HC + c) * P:(j * HC + c + 1) * P],
                                                 w_in[:, s, j, k, c * P:(c + 1) * P],
                                                 row_t[:, s, k * P:(k + 1) * P], start=(k == 0), stop=(k == 1))
                    last.then_inc(hidden_ready, 1)

                def output(t, s, rnd):
                    pe.wait_ge(active, t + 3)
                    pe.wait_ge(w_out_loaded[s], 16 * (rnd + 1))
                    pe.wait_ge(out_copied, t + 1)
                    for c in range(HC):
                        last = pe.matmul(ps_o[:, s, 0:D], act_t[:, s, c * P:(c + 1) * P], w_out[:, s, c, :],
                                         start=(c == 0), stop=(c == HC - 1))
                    last.then_inc(out_ready, 1)

                hidden(0, 0, 0)
                with pe.Fori(0, T // 2 - 1) as i:
                    hidden(2 * i + 1, 1, i)
                    output(2 * i, 0, i)
                    hidden(2 * i + 2, 0, i + 1)
                    output(2 * i + 1, 1, i)
                hidden(T - 1, 1, T // 2 - 1)
                output(T - 2, 0, T // 2 - 1)
                output(T - 1, 1, T // 2 - 1)

            @block.scalar
            def _(act):
                act.preload_act_table(ACT.Silu if m.gated else ACT.Gelu)
                act.sem_inc(copied, 2)
                if not m.gated:
                    act.sem_inc(active, 2)
                with act.Fori(0, T // 2) as i:
                    if not m.gated:
                        experts_of = [act.value_load(m.tile_expert[0:1, ds(2 * i + s, 1)], min_val=0,
                                                     max_val=m.experts - 1) for s in range(2)]
                    for s in range(2):
                        t = 2 * i + s
                        act.wait_ge(turned, t + 3)
                        act.wait_ge(hidden_ready, t + 1)
                        act.copy(row_t[:, s, :], ps_t[:, s, 0:2 * P]).then_inc(copied, 1)
                        act.wait_ge(hidden_ready, t + 3)
                        act.wait_ge(out_ready, t + 1)
                        if m.gated:
                            act.wait_ge(active, t + 1)
                            act.activation(gate_t[:, s, :], ps_h[:, s, 0:HC * P], ACT.Silu).then_inc(half_active, 1)
                        else:
                            b1 = m.b1[:].rearrange("p e c -> p (e c)")
                            for c in range(HC):
                                last = act.activation(act_t[:, s, c * P:(c + 1) * P], ps_h[:, s, c * P:(c + 1) * P],
                                                      ACT.Gelu, bias=b1[:, ds(experts_of[s] * HC + c, 1)])
                            last.then_inc(active, 1)

            @block.vector
            def _(dve):
                dve.sem_inc(out_copied, 2)
                if m.gated:
                    dve.sem_inc(active, 2)

                def act_mul(t, s):
                    dve.wait_ge(half_active, t + 1)
                    dve.tensor_tensor(act_t[:, s, :], gate_t[:, s, :], ps_h[:, s, HC * P:2 * HC * P], ALU.mult)\
                       .then_inc(active, 1)

                def take_out(t, s, rnd, expert):
                    dve.wait_ge(out_ready, t + 3)
                    dve.wait_ge(stored[s].sem, stored[s].at(16 * rnd))
                    if m.gated:
                        dve.tensor_copy(out[:, s, :], ps_o[:, s, 0:D]).then_inc(out_copied, 1)
                    else:
                        dve.tensor_tensor(out[:, s, :], ps_o[:, s, 0:D],
                                          m.b2[:, ds(expert, 1), :].rearrange("p a f -> p (a f)"), ALU.add)\
                           .then_inc(out_copied, 1)

                if m.gated:
                    act_mul(0, 0)
                    with dve.Fori(0, T // 2 - 1) as i:
                        act_mul(2 * i + 1, 1)
                        take_out(2 * i, 0, i, None)
                        act_mul(2 * i + 2, 0)
                        take_out(2 * i + 1, 1, i, None)
                    act_mul(T - 1, 1)
                    take_out(T - 2, 0, T // 2 - 1, None)
                    take_out(T - 1, 1, T // 2 - 1, None)
                else:
                    with dve.Fori(0, T // 2) as i:
                        for s in range(2):
                            expert = dve.value_load(m.tile_expert[0:1, ds(2 * i + s, 1)], min_val=0,
                                                    max_val=m.experts - 1)
                            take_out(2 * i + s, s, i, expert)

            @block.gpsimd
            def _(pool):
                with pool.Fori(0, T // 2) as i:
                    for s in range(2):
                        pool.wait_ge(out_copied, 2 * i + s + 3)
                        pool.dma_start(rows_out[:, ds(2 * i + s, 1), :].rearrange("p a f -> p (a f)"),
                                       out[:, s, :]).then_inc(stored[s].sem, 16)
                for s in range(2):
                    pool.wait_ge(stored[s].sem, stored[s].at(16 * (T // 2)))
    for q in stored:
        q.base += 16 * (T // 2)


@staged
def combine(g, m, x):
    nc = g.nc
    R = 5
    indices, gate, own, used = (g.sem(m.name + "_indices"), g.sem(m.name + "_gate"), g.sem(m.name + "_chain"),
                                g.sem(m.name + "_used"))
    got = g.dma_counts[0:R]
    with ExitStack() as ctx:
        slot = g.sb(m.name + "_back", [P, 2 * R, D], ctx=ctx)
        row = g.sb(m.name + "_row_back", [P, 2 * R], I32, ctx)
        with nc.Block() as block:
            @block.scalar
            def _(act):
                act.preload_act_table(ACT.Copy)
                with act.Fori(0, NB // R) as i:
                    act.wait_ge(used, R * i + 1)
                    act.copy(row[:], m.row[:, ds(2 * R * i, 2 * R)]).then_inc(indices, 1)

            @block.gpsimd
            def _(pool):
                with pool.Fori(0, NB // R) as i:
                    pool.wait_ge(indices, i + 1)
                    pool.sem_inc(gate, 1)
                    for c in range(2 * R):
                        pool.wait_ge(gate, 1)
                        pool.indirect_dma_start(
                            out=slot[:, c, :], out_offset=None, in_=m.rows_out,
                            in_offset=bass.IndirectOffsetOnAxis(ap=row[:, c:c + 1], axis=0)).then_inc(got[c // 2].sem, 16)

            @block.vector
            def _(dve):
                dve.sem_inc(used, 1)
                with dve.Fori(0, NB // R) as i:
                    ch = Chain(dve, own, 2 * R * i)
                    for k in range(R):
                        dve.wait_ge(got[k].sem, got[k].at(32 * i + 32))
                        x_b = x[:, ds(R * i + k, 1), :].rearrange("p a f -> p (a f)")
                        for j in range(2):
                            ch.link(dve.scalar_tensor_tensor(out=x_b, in0=slot[:, 2 * k + j, :],
                                                             scalar=m.weight[:, ds(2 * (R * i + k) + j, 1)],
                                                             in1=x_b, op0=ALU.mult, op1=ALU.add))
                        dve.sem_inc(used, 1)
    for q in got:
        q.base += 32 * (NB // R)


@staged
def store(g, x, out):
    nc = g.nc
    stored = g.sem("stored")
    with nc.Block() as block:
        @block.sync
        def _(sp):
            sp.dma_start(out.rearrange("(a b) f -> a b f", b=NB), x[0:N // NB]).then_inc(stored, 16)
            sp.wait_ge(stored, 16)


@staged
def gate_weights(g, gates):
    nc = g.nc
    loaded = g.sem("gates_loaded")
    with nc.Block() as block:
        @block.sync
        def _(sp):
            for name, (matrix, bias) in gates.items():
                X = matrix.shape[1]
                g.w[name] = g.sb(name, [P, 2, X])
                g.row[name] = g.sb(name + "_bias", [1, X])
                sp.dma_start(g.w[name][:], matrix.rearrange("(k p) e -> p k e", p=P)).then_inc(loaded, 16)
                sp.dma_start(g.row[name][:], bias.rearrange("(a n) -> a n", a=1)).then_inc(loaded, 16)
            sp.wait_ge(loaded, 32 * len(gates))


def mixture(g, m, x, biases, weights_in, weights_out):
    normalise(g, m.name + "_norm", x, g.cur)
    with ExitStack() as ctx:
        m.ctx = ctx
        logits = g.sb(m.name + "_logits", [P, NB, m.experts], ctx=ctx)
        clear_rows(g, m)
        dense(g, m.name + "_gate", g.cur, g.w[m.name], g.row[m.name][:], m.experts, "copy", logits)
        route(g, m, logits)
        dispatch(g, m, g.cur)
        if biases:
            gelu_biases(g, m, *biases)
        experts(g, m, weights_in, weights_out)
        combine(g, m, x)


def write_program(nc, A, out):
    with ExitStack() as ctx:
        g = Program(nc, ctx)
        constants(g, A["src"])
        sort_edges(g, A["src"], A["dst"], A["edge_attr_3"])
        resident(g)
        edge_tables(g, A["x"])
        layer_weights(g, A)
        gate_weights(g, {"L0_ffn": (A["L0_ffn_Wg"], A["L0_ffn_bg"]), "L1_ffn": (A["L1_ffn_gate_w"], A["L1_ffn_gate_b"])})
        attention_weights(g, A)

        table, states, carries = g.dram("table", [NPAD, D]), g.dram("states", [EPAD, D]), g.dram("carries", [P, D])
        pooled = (states, carries)
        normalise(g, "norm0", g.x, g.cur)
        dense(g, "pool_in", g.cur, g.w["L0_gnn_Wp1"], g.row["L0_gnn_bp1"][:], D, "relu", g.new, table)
        pool_max(g, "pool1", table, states, carries)
        dense(g, "mix1", g.cur, g.w["L0_gnn_Wm1"], g.row["L0_gnn_bm1"][:], D, "relu", g.cur, table, pooled)
        pool_max(g, "pool2", table, states, carries)
        dense(g, "mix2", g.cur, g.w["L0_gnn_Wm2"], g.row["L0_gnn_bm2"][:], D, "relu_add", g.new, None, pooled)
        normalise(g, "norm2", g.new, g.cur, g.wide["L0_gnn_ln2_g"][:], g.wide["L0_gnn_ln2_b"][:], None, table)
        pool_max(g, "pool3", table, states, carries)
        dense(g, "mix3", g.cur, g.w["L0_gnn_Wm3"], g.row["L0_gnn_bm3"][:], D, "relu_add", g.new, None, pooled)
        normalise(g, "norm3", g.new, g.cur, g.wide["L0_gnn_ln3_g"][:], g.wide["L0_gnn_ln3_b"][:], g.x)

        mixture(g, Mixture(g, "L0_ffn", 8, 1024, False), g.x, (A["L0_ffn_b1"], A["L0_ffn_b2"]),
                [A["L0_ffn_W1"]], A["L0_ffn_W2"])

        W = D + 2 * H
        rows, sums, sum_carries = g.dram("source_rows", [EPAD, D]), g.dram("sums", [EPAD, D + H]), g.dram("sum_carries", [P, D + H])
        head_table = g.dram("head_table", [NPAD, W])
        normalise(g, "norm4", g.x, g.cur)
        with ExitStack() as scope:
            heads = g.sb("heads", [P, NB, W], ctx=scope)
            dense(g, "heads", g.cur, g.w["L1_gnn_W"], None, D, "attention", heads, head_table)
        with ExitStack() as scope:
            scores = g.sb("scores", [P, EC, H], ctx=scope)
            edge_scores(g, "score", head_table, rows, scores)
            edge_softmax(g, scores)
            edge_sums(g, "sum", rows, scores, sums, sum_carries)
        attend(g, "attend", sums, sum_carries, g.x, g.wide["L1_gnn_bias"][:])

        mixture(g, Mixture(g, "L1_ffn", 16, 512, True), g.x, None, [A["L1_ffn_w1"], A["L1_ffn_w2"]], A["L1_ffn_w3"])
        store(g, g.x, out)


def kernel(**inputs):
    import numpy as _np
    import concourse.bacc as _bacc
    from concourse import mybir as _mybir
    from concourse.bass_utils import run_bass_kernel_spmd as _run

    nc = _bacc.Bacc("TRN2", target_bir_lowering=False, num_devices=1)
    arrays, args = {}, {}
    for name, value in inputs.items():
        a = _np.ascontiguousarray(value)
        arrays[f"in_{name}_dram"] = a
        args[name] = nc.dram_tensor(f"in_{name}_dram", a.shape, _mybir.dt.from_np(a.dtype), kind="ExternalInput").ap()
    out = nc.dram_tensor("out_0_dram", (N, D), _mybir.dt.float32, kind="ExternalOutput").ap()
    write_program(nc, args, out)
    r = _run(nc, [arrays], core_ids=[0])
    return r.results[0]["out_0_dram"]
```

```python
from contextlib import ExitStack, contextmanager

import concourse.bass as bass
from concourse import mybir

ALU = mybir.AluOpType
ACT = mybir.ActivationFunctionType
AX = mybir.AxisListType
F32 = mybir.dt.float32
BF16 = mybir.dt.bfloat16
I32 = mybir.dt.int32
U32 = mybir.dt.uint32

P = 128
N = 3125
NB = 25
NPAD = P * NB
E = 50000
EC = 392
EPAD = P * EC
D = 256
H = 8
HD = D // H
EF = 6
SRC, DST = 4, 5
BIG = 1e38
MAGIC = 12582912.0
EPS = 1e-5
ds = bass.ds


class DmaCount:

    def __init__(self, sem):
        self.sem, self.base = sem, 16

    def at(self, n):
        return self.base + n


class Chain:

    def __init__(self, eng, sem, at=0):
        self.eng, self.sem, self.n = eng, sem, at

    def mark(self, ins):
        self.n = self.n + 1
        ins.then_inc(self.sem, 1)

    def sync(self):
        self.eng.wait_ge(self.sem, self.n)

    def link(self, ins):
        self.mark(ins)
        self.sync()


def staged(write):
    def run(g, *args, **kwargs):
        with g.stage():
            return write(g, *args, **kwargs)
    return run


class Program:

    def __init__(self, nc, ctx):
        self.nc, self.ctx = nc, ctx
        counts = lambda name, n: [DmaCount(ctx.enter_context(nc.semaphore(f"{name}{k}"))) for k in range(n)]
        self.dma_counts = counts("gpsimd_dma", 14)
        self.place_counts = counts("place_dma", 8)
        self.store_counts = counts("sync_store", 2)
        self.out_counts = counts("gpsimd_store", 2)

    def sem(self, name):
        handle = self.stage_ctx.enter_context(self.nc.semaphore(name))
        self.stage_sems.append(handle)
        return handle

    @contextmanager
    def stage(self):
        self.stage_sems = []
        with ExitStack() as self.stage_ctx:
            yield
            for handle in self.stage_sems:
                self.nc.gpsimd.sem_clear(handle)

    def sb(self, name, shape, dt=F32, ctx=None):
        return (ctx or self.ctx).enter_context(self.nc.sbuf_tensor("sb_" + name, shape, dt))

    def ps(self, name, shape, dt=F32, ctx=None):
        return (ctx or self.ctx).enter_context(self.nc.psum_tensor("ps_" + name, shape, dt))

    def dram(self, name, shape, dt=F32):
        return self.nc.dram_tensor("dram_" + name, shape, dt, kind="Internal").ap()


def floor_div(ch, eng, out, in_, by, ctx_tmp):
    ch.link(eng.tensor_scalar(ctx_tmp, in_, -(by - 1) / 2.0, 1.0 / by, ALU.add, ALU.mult))
    ch.link(eng.tensor_scalar(out, ctx_tmp, MAGIC, None, ALU.add))
    ch.link(eng.tensor_scalar(out, out, -MAGIC, None, ALU.add))


def resident(g):
    g.x = g.sb("x", [P, NB, D])
    g.cur = g.sb("cur", [P, NB, D])
    g.new = g.sb("new", [P, NB, D])
    g.src_at = g.sb("src_at", [P, EC + 14], I32)
    g.dst_at = g.sb("dst_at", [P, EC], I32)
    g.keep = g.sb("keep", [P, EC])
    g.keep_neg = g.sb("keep_neg", [P, EC])
    g.cont = g.sb("cont", [P, P])
    g.cont_neg = g.sb("cont_neg", [P, P])


@staged
def constants(g, src):
    nc = g.nc
    g.ident = g.sb("ident", [P, P])
    g.identb = g.sb("identb", [P, P], BF16)
    g.below = g.sb("below", [P, P])
    g.belowb = g.sb("belowb", [P, P], BF16)
    g.ones = g.sb("ones", [P, P])
    g.node_base = g.sb("node_base", [P, P])
    g.ramp = g.sb("ramp", [P, P])
    g.first_pos = g.sb("first_pos", [P, 1])
    zero_done, tri_done, ramp_done = g.sem("zero_done"), g.sem("tri_done"), g.sem("ramp_done")
    g.first_load = g.sb("first_load", [1, 32], I32)
    with nc.Block() as block:
        @block.sync
        def _(sp):
            for k, q in enumerate(g.store_counts):
                sp.dma_start(g.first_load[:, k:k + 1], src[k:k + 1].rearrange("(a n) -> a n", a=1)).then_inc(q.sem, 16)
            for q in g.store_counts:
                sp.wait_ge(q.sem, 16)

        @block.gpsimd
        def _(pool):
            for k, q in enumerate(g.dma_counts + g.place_counts + g.out_counts, 2):
                pool.dma_start(g.first_load[:, k:k + 1], src[k:k + 1].rearrange("(a n) -> a n", a=1)).then_inc(q.sem, 16)
            pool.memset(g.ident[:], 0.0).then_inc(zero_done, 1)
            pool.memset(g.below[:], 1.0).then_inc(zero_done, 1)
            pool.memset(g.ones[:], 1.0)
            pool.wait_ge(zero_done, 2)
            pool.affine_select(out=g.ident[:], in_=g.ident[:], compare_op=ALU.not_equal, fill=1.0,
                               base=0, pattern=[[-1, P]], channel_multiplier=1).then_inc(tri_done, 1)
            pool.affine_select(out=g.below[:], in_=g.below[:], compare_op=ALU.is_ge, fill=0.0,
                               base=-1, pattern=[[1, P]], channel_multiplier=-1).then_inc(tri_done, 1)
            pool.iota(g.ramp[:], pattern=[[1, P]], base=0, channel_multiplier=0,
                      allow_small_or_imprecise_dtypes=True).then_inc(ramp_done, 1)
            pool.iota(g.first_pos[:], pattern=[[0, 1]], base=0, channel_multiplier=EC,
                      allow_small_or_imprecise_dtypes=True)
            for q in g.dma_counts + g.place_counts + g.out_counts:
                pool.wait_ge(q.sem, 16)

        @block.vector
        def _(dve):
            dve.wait_ge(tri_done, 2)
            dve.tensor_copy(g.identb[:], g.ident[:])
            dve.tensor_copy(g.belowb[:], g.below[:])
            dve.wait_ge(ramp_done, 1)
            dve.tensor_scalar(g.node_base[:], g.ramp[:], float(NB), None, ALU.mult)


def load_edges(g, name, src, tile, sem, eng, width=1):
    full = E // EC
    rest = E - full * EC
    if width == 1:
        eng.dma_start(tile[0:full, :], src[0:full * EC].rearrange("(p c) -> p c", c=EC)).then_inc(sem, 16)
        eng.dma_start(tile[full:full + 1, 0:rest], src[full * EC:E].rearrange("(p c) -> p c", p=1)).then_inc(sem, 16)
    else:
        eng.dma_start(tile[0:full, :, :], src[0:full * EC, :].rearrange("(p c) w -> p c w", c=EC)).then_inc(sem, 16)
        eng.dma_start(tile[full:full + 1, 0:rest, :],
                      src[full * EC:E, :].rearrange("(p c) w -> p c w", p=1)).then_inc(sem, 16)


@staged
def sort_edges(g, src, dst, attr, mixtures):
    nc = g.nc
    g.sorted_edges = g.dram("sorted_edges", [EPAD, EF])
    g.has_edge = g.sb("has_edge", [P, NB])
    g.last_at = g.sb("last_at", [P, NB], I32)
    g.unsorted = g.sb("unsorted", [P, 1], I32)
    sorted_v = g.sorted_edges.rearrange("(p c) f -> p c f", p=P)
    U = 7
    ROUNDS = EC // (2 * U)
    loaded, dst_loaded, filled = g.sem("edges_loaded"), g.sem("dst_loaded"), g.sem("edges_filled")
    rows_copied, hot_used, steps_ready = g.sem("rows_copied"), g.sem("hot_used"), g.sem("steps_ready")
    rows_ready, rows_stored, cleared = g.sem("rows_ready"), g.sem("rows_stored"), g.sem("rows_cleared")
    hot_done, counted, ranged = g.sem("hot_done"), g.sem("counted"), g.sem("ranged")
    prefix_done, offsets_done, rows_done = (g.sem("prefix_done"), g.sem("offsets_done"),
                                            g.sem("rows_done"))
    with ExitStack() as ctx:
        sb = lambda n, s, d=F32: g.sb(n, s, d, ctx)
        src_i, dst_i = sb("src_i", [P, EC], I32), sb("dst_i", [P, EC], I32)
        attr_t = sb("attr_t", [P, EC, 3])
        rows = sb("rows", [P, EC, EF])
        part_base, col = sb("part_base", [P, EC]), sb("col", [P, EC])
        hot_a, hot_b = sb("hot_a", [P, 2, U, P], BF16), sb("hot_b", [P, 2, U, NB], BF16)
        count, upto, row_sum, start, tmp = (sb("count", [P, NB]), sb("upto", [P, NB]),
                                            sb("row_sum", [P, 1]), sb("start", [P, NB]), sb("tmp_n", [P, NB]))
        next_i, step_down = sb("next_i", [P, 1], I32), sb("step_down", [P, EC])
        zero_row = sb("zero_row", [P, D])
        next_dst, steps_down = sb("next_dst", [P, 1]), sb("steps_down", [P, 1])
        ps_count = g.ps("count", [P, 512], F32, ctx)

        with nc.Block() as block:
            @block.sync
            def _(sp):
                sp.wait_ge(filled, 5)
                load_edges(g, "dst", dst, dst_i, dst_loaded, sp)
                load_edges(g, "src", src, src_i, loaded, sp)
                load_edges(g, "attr", attr, attr_t, loaded, sp, 3)
                sp.dma_start(next_i[0:P - 1, :], dst[EC:(P - 1) * EC + 1:EC].unsqueeze(1),
                             allow_slow_non_contiguous=True).then_inc(dst_loaded, 16)
                sp.wait_ge(rows_ready, 1)
                sp.wait_ge(rows_copied, 2)
                sp.dma_start(sorted_v, rows[:]).then_inc(rows_stored, 16)
                sp.wait_ge(rows_stored, 16)
                for m in mixtures:
                    sp.dma_start(m.rows_in.rearrange("(p t) f -> p t f", p=P),
                                 zero_row[:].unsqueeze(1).broadcast_to([P, m.tiles, D])).then_inc(cleared, 16)
                sp.wait_ge(cleared, 16 * len(mixtures))

            @block.vector
            def _(dve):
                ch = Chain(dve, prefix_done)
                dve.memset(dst_i[:], N).then_inc(filled, 1)
                dve.memset(src_i[:], 0).then_inc(filled, 1)
                dve.memset(attr_t[:], 0.0).then_inc(filled, 1)
                dve.memset(next_i[:], N).then_inc(filled, 1)
                dve.memset(zero_row[:], 0.0).then_inc(filled, 1)
                ch.mark(dve.memset(rows[:, :, 3:4], 1.0))
                dve.wait_ge(dst_loaded, 48)
                ch.mark(dve.tensor_copy(next_dst[:], next_i[:]))
                ch.link(dve.tensor_copy(rows[:, :, DST], dst_i[:]))
                dve.sem_inc(rows_ready, 1)
                floor_div(ch, dve, part_base[:], rows[:, :, DST], NB, col[:])
                ch.link(dve.tensor_scalar(part_base[:], part_base[:], float(NB), None, ALU.mult))
                ch.link(dve.tensor_tensor(col[:], rows[:, :, DST], part_base[:], ALU.subtract))
                with dve.Fori(0, ROUNDS) as i:
                    for h in range(2):
                        dve.wait_ge(hot_used, 2 * i + h + 1)
                        dve.tensor_tensor(hot_a[:, h, :, :],
                                          part_base[:, ds(2 * U * i + U * h, U)].unsqueeze(2).broadcast_to([P, U, P]),
                                          g.node_base[:].unsqueeze(1).broadcast_to([P, U, P]),
                                          ALU.is_equal).then_inc(hot_done, 1)
                        dve.tensor_tensor(hot_b[:, h, :, :],
                                          col[:, ds(2 * U * i + U * h, U)].unsqueeze(2).broadcast_to([P, U, NB]),
                                          g.ramp[:, 0:NB].unsqueeze(1).broadcast_to([P, U, NB]),
                                          ALU.is_equal).then_inc(hot_done, 1)
                ch.mark(dve.tensor_tensor(step_down[:, 0:EC - 1], rows[:, 0:EC - 1, DST], rows[:, 1:EC, DST], ALU.is_gt))
                ch.link(dve.tensor_tensor(step_down[:, EC - 1:EC], rows[:, EC - 1:EC, DST], next_dst[:], ALU.is_gt))
                dve.tensor_reduce(steps_down[:], step_down[:], AX.X, ALU.add).then_inc(steps_ready, 1)
                dve.wait_ge(counted, 1)
                ch.link(dve.tensor_copy(count[:], ps_count[:, 0:NB]))
                ch.link(dve.tensor_tensor_scan(upto[:], g.ones[:, 0:NB], count[:], 0.0, ALU.mult, ALU.add))
                dve.tensor_copy(row_sum[:], upto[:, NB - 1:NB]).then_inc(ranged, 1)
                dve.wait_ge(offsets_done, 1)
                dve.tensor_scalar(g.unsorted[:], ps_count[:, NB + 1:NB + 2], 1.0, None, ALU.min)
                ch.link(dve.tensor_scalar(upto[:], upto[:], ps_count[:, NB:NB + 1], None, ALU.add))
                dve.tensor_tensor(start[:], upto[:], count[:], ALU.subtract)
                dve.tensor_scalar(g.has_edge[:], count[:], 0.0, None, ALU.is_gt)
                ch.link(dve.tensor_scalar(tmp[:], upto[:], -1.0, 0.0, ALU.add, ALU.max))
                dve.tensor_copy(g.last_at[:], tmp[:])

            @block.tensor
            def _(pe):
                pe.sem_inc(hot_used, 2)

                def count_half(n, h, first=False, last=False):
                    pe.wait_ge(hot_done, 2 * n + 2)
                    for c in range(U):
                        end = pe.matmul(ps_count[:, 0:NB], hot_a[:, h, c, :], hot_b[:, h, c, :],
                                        start=(first and c == 0), stop=(last and c == U - 1))
                    end.then_inc(counted if last else hot_used, 1)

                count_half(0, 0, first=True)
                with pe.Fori(0, ROUNDS - 1) as i:
                    count_half(2 * i + 1, 1)
                    count_half(2 * i + 2, 0)
                count_half(2 * ROUNDS - 1, 1, last=True)
                pe.wait_ge(steps_ready, 1)
                pe.wait_ge(ranged, 1)
                pe.matmul(ps_count[:, NB:NB + 1], g.below[:], row_sum[:], start=True, stop=True)
                pe.matmul(ps_count[:, NB + 1:NB + 2], g.ones[:], steps_down[:], start=True, stop=True)\
                  .then_inc(offsets_done, 1)

            @block.scalar
            def _(act):
                act.wait_ge(loaded, 64)
                act.copy(rows[:, :, SRC], src_i[:]).then_inc(rows_copied, 1)
                act.copy(rows[:, :, 0:3], attr_t[:]).then_inc(rows_copied, 1)

        place_edges(g, ctx, rows, part_base, col, start)


def place_edges(g, ctx, rows, part_base, col, start):
    nc = g.nc
    U = 8
    ROUNDS = EC // U
    sb = lambda n, s, d=F32: g.sb(n, s, d, ctx)
    hot_a, hot_b = sb("hot_a_slot", [P, U, P], BF16), sb("hot_b_slot", [P, U, NB], BF16)
    hotT_f = sb("hotT_f", [P, U, P])
    hotT_b = sb("hotT_b", [P, U, P], BF16)
    seen = sb("seen", [P, U, NB])
    same = sb("same", [P, U, P], BF16)
    picked = sb("picked", [P, U, NB])
    pos_f = sb("pos_f", [P, U])
    pos_i = sb("pos_i", [P, U], I32)
    row_slot = sb("row_slot", [P, U, EF])
    ps_hotT = g.ps("hotT", [P, 2, 1024], BF16, ctx)
    ps_same = g.ps("same", [P, 2, 512], F32, ctx)
    ps_seen = g.ps("seen", [P, 512], F32, ctx)
    ps_pos = g.ps("pos", [P, 2, 512], F32, ctx)
    turned, turned_copied = g.sem("hot_turned"), g.sem("hot_turned_copied")
    seen_ready, seen_copied = g.sem("seen_ready"), g.sem("seen_copied")
    same_ready, same_cut = g.sem("same_ready"), g.sem("same_cut")
    pos_ready, pos_picked = g.sem("pos_ready"), g.sem("pos_picked")
    block_ready, gate, own = g.sem("edge_block_ready"), g.sem("scatter_gate"), g.sem("place_chain")
    hot_ready = g.sem("hot_slots_ready")
    placed = g.place_counts

    with nc.Block() as block:
        @block.tensor
        def _(pe):
            unsorted = pe.value_load(g.unsorted[0:1, 0:1], min_val=0, max_val=1)
            with pe.If(unsorted > 0):
                pe.matmul(ps_seen[:, 0:NB], g.ident[:], start[:], start=True, stop=True).then_inc(seen_ready, 1)

                def step(c, k, last=False):
                    hot, hot_col = hot_a[:, k, :], hot_b[:, k, :]
                    pe.wait_ge(turned_copied, c + 1)
                    pe.transpose(ps_hotT[:, k % 2, 0:P], hot, g.identb[:]).then_inc(turned, 1)
                    pe.wait_ge(turned_copied, c + 3)
                    pe.wait_ge(same_cut, c + 1)
                    pe.matmul(ps_same[:, k % 2, 0:P], hotT_b[:, k, :], hotT_b[:, k, :], start=True, stop=True)\
                      .then_inc(same_ready, 1)
                    pe.wait_ge(seen_copied, c + 1)
                    pe.wait_ge(pos_picked, c + 1)
                    pe.matmul(ps_pos[:, k % 2, 0:NB], hotT_f[:, k, :], seen[:, k, :], start=True, stop=False)
                    pe.wait_ge(same_cut, c + 3)
                    pe.matmul(ps_pos[:, k % 2, 0:NB], same[:, k, :], hot_col, start=False, stop=True)\
                      .then_inc(pos_ready, 1)
                    pe.matmul(ps_seen[:, 0:NB], hot, hot_col, start=False, stop=True,
                              skip_group_check=True).then_inc(seen_ready, 1)

                with pe.Fori(0, ROUNDS) as i:
                    pe.wait_ge(hot_ready, 2 * i + 2)
                    for k in range(U):
                        step(U * i + k, k)

        @block.scalar
        def _(act):
            unsorted = act.value_load(g.unsorted[0:1, 0:1], min_val=0, max_val=1)
            with act.If(unsorted > 0):
                act.preload_act_table(ACT.Copy)
                act.sem_inc(turned_copied, 2)
                with act.Fori(0, ROUNDS) as i:
                    for k in range(U):
                        act.wait_ge(placed[k].sem, placed[k].at(16 * i))
                    act.activation(row_slot[:], rows[:, ds(U * i, U), :], ACT.Copy).then_inc(block_ready, 1)
                    for k in range(U):
                        c = U * i + k
                        act.wait_ge(seen_ready, c + 1)
                        act.activation(seen[:, k, :], ps_seen[:, 0:NB], ACT.Copy).then_inc(seen_copied, 1)
                        act.wait_ge(turned, c + 1)
                        act.activation(hotT_b[:, k, :], ps_hotT[:, k % 2, 0:P], ACT.Copy)
                        act.activation(hotT_f[:, k, :], ps_hotT[:, k % 2, 0:P], ACT.Copy)\
                           .then_inc(turned_copied, 1)

        @block.vector
        def _(dve):
            unsorted = dve.value_load(g.unsorted[0:1, 0:1], min_val=0, max_val=1)
            with dve.If(unsorted > 0):
                dve.sem_inc(same_cut, 2)
                dve.sem_inc(pos_picked, 2)
                with dve.Fori(0, ROUNDS) as i:
                    dve.wait_ge(seen_ready, U * i + 1)
                    dve.tensor_tensor(hot_a[:], part_base[:, ds(U * i, U)].unsqueeze(2).broadcast_to([P, U, P]),
                                      g.node_base[:].unsqueeze(1).broadcast_to([P, U, P]), ALU.is_equal).then_inc(hot_ready, 1)
                    dve.tensor_tensor(hot_b[:], col[:, ds(U * i, U)].unsqueeze(2).broadcast_to([P, U, NB]),
                                      g.ramp[:, 0:NB].unsqueeze(1).broadcast_to([P, U, NB]), ALU.is_equal)\
                       .then_inc(hot_ready, 1)
                    dve.wait_ge(hot_ready, 2 * i + 2)
                    for k in range(U):
                        c = U * i + k
                        dve.wait_ge(same_ready, c + 1)
                        dve.tensor_tensor(same[:, k, :], ps_same[:, k % 2, 0:P], g.below[:], ALU.mult)\
                           .then_inc(same_cut, 1)
                        dve.wait_ge(pos_ready, c + 1)
                        dve.scalar_tensor_tensor(out=picked[:, k, :], in0=ps_pos[:, k % 2, 0:NB], scalar=0.0,
                                                 in1=hot_b[:, k, :],
                                                 op0=ALU.add, op1=ALU.mult, accum_out=pos_f[:, k:k + 1])\
                           .then_inc(pos_picked, 1)
                    for k in range(U):
                        dve.wait_ge(placed[k].sem, placed[k].at(16 * i))
                    dve.wait_ge(pos_picked, U * i + U + 2)
                    dve.tensor_copy(pos_i[:], pos_f[:]).then_inc(own, 1)

        @block.gpsimd
        def _(pool):
            unsorted = pool.value_load(g.unsorted[0:1, 0:1], min_val=0, max_val=1)
            with pool.If(unsorted > 0):
                with pool.Fori(0, ROUNDS) as i:
                    pool.wait_ge(own, i + 1)
                    pool.wait_ge(block_ready, i + 1)
                    pool.sem_inc(gate, 1)
                    for k in range(U):
                        pool.wait_ge(gate, 1)
                        pool.indirect_dma_start(
                            out=g.sorted_edges, out_offset=bass.IndirectOffsetOnAxis(ap=pos_i[:, k:k + 1], axis=0),
                            in_=row_slot[:, k, :], in_offset=None).then_inc(placed[k].sem, 16)
                for k in range(U):
                    pool.wait_ge(placed[k].sem, placed[k].at(16 * ROUNDS))


@staged
def edge_tables(g, x):
    nc = g.nc
    loaded, filled, ready, turned = (g.sem("sorted_loaded"), g.sem("tables_filled"),
                                     g.sem("tables_chain"), g.sem("cont_turned"))
    g.edge_rows = g.sb("edge_rows", [P, EC, EF])
    g.before = g.sb("before", [P, 1])
    g.carry_in_neg = g.sb("carry_in_neg", [P, 1])
    g.first_end = g.sb("first_end", [P, 1], I32)
    g.goes_on_neg = g.sb("goes_on_neg", [P, 1])
    sorted_v = g.sorted_edges.rearrange("(p c) f -> p c f", p=P)
    with ExitStack() as ctx:
        goes_on = g.sb("goes_on", [P, 1], ctx=ctx)
        in_first, first_count = g.sb("in_first", [P, EC], ctx=ctx), g.sb("first_count", [P, 1], ctx=ctx)
        goes_on_row = g.sb("goes_on_row", [P, P], ctx=ctx)
        ps_cont = g.ps("cont", [P, 512], ctx=ctx)
        with nc.Block() as block:
            @block.sync
            def _(sp):
                sp.dma_start(g.edge_rows[:], sorted_v).then_inc(loaded, 16)
                sp.wait_ge(filled, 2)
                sp.dma_start(g.before[1:P, :], sorted_v[0:P - 1, EC - 1, DST:DST + 1], allow_slow_non_contiguous=True).then_inc(loaded, 16)
                sp.dma_start(g.x[0:N // NB, :, :], x.rearrange("(a b) f -> a b f", b=NB)).then_inc(loaded, 16)
                sp.wait_ge(loaded, 48)

            @block.vector
            def _(dve):
                ch = Chain(dve, ready)
                dve.memset(g.before[:], -1.0).then_inc(filled, 1)
                dve.memset(g.x[:], 0.0).then_inc(filled, 1)
                dve.wait_ge(loaded, 48)
                dst = g.edge_rows[:, :, DST]
                dve.memset(g.src_at[:, EC:], 0)
                dve.tensor_copy(g.src_at[:, 0:EC], g.edge_rows[:, :, SRC])
                dve.tensor_copy(g.dst_at[:], dst)
                ch.mark(dve.memset(g.keep[:, 0:1], 0.0))
                ch.mark(dve.tensor_tensor(g.keep[:, 1:EC], dst[:, 1:EC], dst[:, 0:EC - 1], ALU.is_equal))
                ch.link(dve.tensor_tensor(goes_on[:], dst[:, EC - 1:EC], g.before[:], ALU.is_equal))
                ch.mark(dve.tensor_scalar(g.keep_neg[:], g.keep[:], -1.0, BIG, ALU.add, ALU.mult))
                ch.mark(dve.tensor_scalar(goes_on_row[:], g.ones[:], goes_on[:, 0:1], None, ALU.mult))
                dve.tensor_scalar(g.goes_on_neg[:], goes_on[:], -1.0, BIG, ALU.add, ALU.mult)
                ch.mark(dve.tensor_scalar(in_first[:], dst, dst[:, 0:1], None, ALU.is_equal))
                ch.link(dve.tensor_tensor(g.carry_in_neg[:], dst[:, 0:1], g.before[:], ALU.is_equal))
                ch.mark(dve.tensor_reduce(first_count[:], in_first[:], AX.X, ALU.add))
                ch.link(dve.tensor_scalar(g.carry_in_neg[:], g.carry_in_neg[:], -1.0, BIG, ALU.add, ALU.mult))
                ch.link(dve.scalar_tensor_tensor(out=first_count[:], in0=first_count[:], scalar=-1.0,
                                                 in1=g.first_pos[:], op0=ALU.add, op1=ALU.add))
                dve.tensor_copy(g.first_end[:], first_count[:])
                dve.wait_ge(turned, 1)
                ch.link(dve.tensor_copy(g.cont[:], ps_cont[:, 0:P]))
                dve.tensor_scalar(g.cont_neg[:], g.cont[:], -1.0, BIG, ALU.add, ALU.mult)

            @block.tensor
            def _(pe):
                pe.wait_ge(ready, 5)
                pe.matmul(ps_cont[:, 0:P], goes_on_row[:], g.ident[:], start=True, stop=True).then_inc(turned, 1)


@staged
def layer_weights(g, w):
    nc = g.nc
    layers = ["L0_gnn_Wp1", "L0_gnn_Wm1", "L0_gnn_Wm2", "L0_gnn_Wm3", "L1_gnn_W"]
    rows = ["L0_gnn_bp1", "L0_gnn_bm1", "L0_gnn_bm2", "L0_gnn_bm3"]
    spread = ["L0_gnn_ln2_g", "L0_gnn_ln2_b", "L0_gnn_ln3_g", "L0_gnn_ln3_b", "L1_gnn_bias"]
    g.w, g.row, g.wide = {}, {}, {}
    for n in layers:
        g.w[n] = g.sb(n, [P, w[n].shape[1] // P, D + (2 * H if n == "L1_gnn_W" else 0)])
    for n in rows:
        g.row[n] = g.sb(n, [1, D])
    for n in spread:
        g.wide[n] = g.sb(n, [P, D])
    loaded, turned, copied = g.sem("weights_loaded"), g.sem("weights_turned"), g.sem("weights_copied")
    small, zeroed, vectors, folded = (g.sem("small_loaded"), g.sem("heads_zeroed"), g.sem("head_vectors"),
                                      g.sem("weights_folded"))
    with ExitStack() as ctx:
        by_head = g.sb("by_head", [P, 2, 2 * H], ctx=ctx)
        ps_fold = g.ps("fold", [P, 2, 512], ctx=ctx)
        raw = {n: g.sb("raw_" + n, [P, 2, w[n].shape[1]], ctx=ctx) for n in layers}
        ps = g.ps("weights", [P, 2, 512], ctx=ctx)
        blocks = [(n, k) for n in layers for k in range(w[n].shape[1] // P)]
        with nc.Block() as block:
            @block.sync
            def _(sp):
                for n in layers:
                    sp.dma_start(raw[n][:], w[n].rearrange("(o p) k -> p o k", p=P)).then_inc(loaded, 16)
                for n in rows:
                    sp.dma_start(g.row[n][:], w[n].rearrange("(a n) -> a n", a=1)).then_inc(small, 16)
                for n in spread:
                    sp.dma_start(g.wide[n][:], w[n].rearrange("(a n) -> a n", a=1).broadcast_to([P, D]))\
                      .then_inc(small, 16)
                sp.wait_ge(zeroed, 1)
                for j, n in enumerate(("a_src", "a_dst")):
                    for h in range(H):
                        at = h * HD
                        sp.dma_start(by_head[at % P:at % P + HD, at // P, j * H + h:j * H + h + 1],
                                     w["L1_gnn_" + n][h, :].unsqueeze(1), allow_slow_non_contiguous=True)\
                          .then_inc(vectors, 16)
                sp.wait_ge(small, 16 * (len(rows) + len(spread)))

            @block.tensor
            def _(pe):
                pe.wait_ge(loaded, 16 * len(layers))
                for j, (n, k) in enumerate(blocks):
                    if j >= 2:
                        pe.wait_ge(copied, j - 1)
                    for o in range(2):
                        last = pe.transpose(ps[:, j % 2, o * P:(o + 1) * P], raw[n][:, o, k * P:(k + 1) * P], g.ident[:])
                    last.then_inc(turned, 1)
                pe.wait_ge(vectors, 16 * 2 * H)
                for k in range(2):
                    for o in range(2):
                        last = pe.matmul(ps_fold[:, k, 0:2 * H], raw["L1_gnn_W"][:, o, k * P:(k + 1) * P],
                                         by_head[:, o, :], start=(o == 0), stop=(o == 1))
                    last.then_inc(folded, 1)

            @block.vector
            def _(dve):
                dve.memset(by_head[:], 0.0).then_inc(zeroed, 1)
                for j, (n, k) in enumerate(blocks):
                    dve.wait_ge(turned, j + 1)
                    dve.tensor_copy(g.w[n][:, k, 0:D], ps[:, j % 2, 0:D]).then_inc(copied, 1)
                dve.wait_ge(folded, 2)
                dve.tensor_copy(g.w["L1_gnn_W"][:, :, D:], ps_fold[:, :, 0:2 * H])


@staged
def normalise(g, name, src, out, scale=None, shift=None, add_to=None, table=None):
    nc = g.nc
    own, stats_done, mean_ready, var_ready, std_ready, rstd_ready = (
        g.sem(name + "_chain"), g.sem(name + "_stats_done"), g.sem(name + "_mean"), g.sem(name + "_var"),
        g.sem(name + "_std"), g.sem(name + "_rstd"))
    centred, scaled, shifted, stored = (g.sem(name + "_centred"), g.sem(name + "_scaled"),
                                        g.sem(name + "_shifted"), g.sem(name + "_stored"))
    by_act = [b for b in range(NB) if b % 3 == 2]
    with ExitStack() as ctx:
        stats = g.sb(name + "_stats", [P, NB, 6], ctx=ctx)
        moments = g.sb(name + "_moments", [P, NB, 2], ctx=ctx)
        neg_mean, var = g.sb(name + "_neg_mean", [P, NB], ctx=ctx), g.sb(name + "_variance", [P, NB], ctx=ctx)
        std, rstd = g.sb(name + "_stdev", [P, NB], ctx=ctx), g.sb(name + "_rstdev", [P, NB], ctx=ctx)
        with nc.Block() as block:
            @block.vector
            def _(dve):
                for b in range(NB + 2):
                    if b < NB:
                        dve.bn_stats(stats[:, b, :], src[:, b, :]).then_inc(stats_done, 1)
                    if b >= 2:
                        dve.wait_ge(stats_done, b - 1)
                        dve.bn_aggr(moments[:, b - 2, :], stats[:, b - 2, :]).then_inc(own, 1)
                dve.wait_ge(own, NB)
                dve.tensor_scalar(var[:], moments[:, :, 1], EPS, None, ALU.add).then_inc(var_ready, 1)
                dve.tensor_scalar(neg_mean[:], moments[:, :, 0], -1.0, None, ALU.mult).then_inc(mean_ready, 1)
                dve.wait_ge(std_ready, 1)
                dve.reciprocal(rstd[:], std[:]).then_inc(rstd_ready, 1)
                dve.wait_ge(rstd_ready, 1)
                if scale is None:
                    for b in range(NB):
                        if b not in by_act:
                            dve.tensor_scalar(out[:, b, :], src[:, b, :], moments[:, b, 0:1], rstd[:, b:b + 1],
                                              ALU.subtract, ALU.mult)
                    return
                LAG = 3
                for b in range(NB + LAG):
                    if b < NB:
                        dve.wait_ge(centred, b + 1)
                        dve.scalar_tensor_tensor(out=out[:, b, :], in0=out[:, b, :], scalar=rstd[:, b:b + 1],
                                                 in1=scale, op0=ALU.mult, op1=ALU.mult).then_inc(scaled, 1)
                    if add_to is not None and b >= LAG:
                        dve.wait_ge(shifted, b - LAG + 1)
                        dve.tensor_tensor(add_to[:, b - LAG, :], add_to[:, b - LAG, :], out[:, b - LAG, :], ALU.add)

            @block.scalar
            def _(act):
                act.wait_ge(var_ready, 1)
                act.activation(std[:], var[:], ACT.Sqrt).then_inc(std_ready, 1)
                act.wait_ge(mean_ready, 1)
                for b in (by_act if scale is None else range(NB)):
                    act.activation(out[:, b, :], src[:, b, :], ACT.Identity, bias=neg_mean[:, b:b + 1], scale=1.0)\
                       .then_inc(centred, 1)
                if scale is None:
                    act.wait_ge(rstd_ready, 1)
                    for j, b in enumerate(by_act):
                        act.wait_ge(centred, j + 1)
                        act.activation(out[:, b, :], out[:, b, :], ACT.Copy, scale=rstd[:, b:b + 1])

            if scale is not None:
                @block.gpsimd
                def _(pool):
                    for b in range(NB):
                        pool.wait_ge(scaled, b + 1)
                        pool.tensor_tensor(out[:, b, :], out[:, b, :], shift, ALU.add).then_inc(shifted, 1)

            if table is not None:
                @block.sync
                def _(sp):
                    table_v = table.rearrange("(p b) f -> p b f", p=P)
                    R = 5
                    for b in range(0, NB, R):
                        sp.wait_ge(shifted, b + R)
                        sp.dma_start(table_v[:, b:b + R, :], out[:, b:b + R, :]).then_inc(stored, 16)
                    sp.wait_ge(stored, 16 * (NB // R))


@staged
def pool_max(g, name, table, states, x, weights, bias, product):
    nc = g.nc
    HALF = 7
    U = 2 * HALF
    ROUNDS = EC // U
    indices, reached, turned, carried = (g.sem(name + "_indices"), g.sem(name + "_reached"),
                                         g.sem(name + "_turned"), g.sem(name + "_carried"))
    x_turned, x_copied, x_multiplied, x_taken = (g.sem(name + "_x_turned"), g.sem(name + "_x_copied"),
                                                 g.sem(name + "_x_multiplied"), g.sem(name + "_x_taken"))
    gate = g.sem(name + "_gate")
    got = g.dma_counts[0:U]
    stored = g.store_counts
    states_v = states.rearrange("(p c) f -> p c f", p=P)
    with ExitStack() as ctx:
        index = g.sb(name + "_index", [P, U], I32, ctx)
        rows = g.sb(name + "_rows", [P, U, D], ctx=ctx)
        state = g.sb(name + "_state", [P, U, D], ctx=ctx)
        runs = g.sb(name + "_runs", [P, 2, P + 1], ctx=ctx)
        end_row = g.sb(name + "_end_row", [P, D], ctx=ctx)
        x_t = g.sb(name + "_x_t", [P, 2, D], ctx=ctx)
        ps_x = g.ps(name + "_x", [P, 2, 512], ctx=ctx)
        ps_y = g.ps(name + "_y", [P, 2, 512], ctx=ctx)
        ps_t = g.ps(name + "_t", [P, 512], ctx=ctx)
        ps_c = g.ps(name + "_c", [P, 512], ctx=ctx)
        with nc.Block() as block:
            @block.scalar
            def _(act):
                for b in range(NB):
                    act.wait_ge(x_turned, b + 1)
                    if b >= 2:
                        act.wait_ge(x_multiplied, b - 1)
                    act.copy(x_t[:, b % 2, :], ps_x[:, b % 2, 0:D]).then_inc(x_copied, 1)
                    act.wait_ge(x_multiplied, b + 1)
                    act.copy(product[:, b, :], ps_y[:, b % 2, 0:D]).then_inc(x_taken, 1)

            @block.gpsimd
            def _(pool):
                with pool.Fori(0, ROUNDS) as i:
                    for h in range(2):
                        pool.wait_ge(indices, 2 * i + h + 1)
                        pool.sem_inc(gate, 1)
                        for k in range(HALF * h, HALF * (h + 1)):
                            pool.wait_ge(gate, 1)
                            pool.indirect_dma_start(
                                out=rows[:, k, :], out_offset=None, in_=table,
                                in_offset=bass.IndirectOffsetOnAxis(ap=index[:, k:k + 1], axis=0)).then_inc(got[k].sem, 16)
                for q in stored:
                    pool.wait_ge(q.sem, q.at(16 * ROUNDS))
                ends = bass.IndirectOffsetOnAxis(ap=g.first_end[:], axis=0)
                pool.indirect_dma_start(out=end_row[:], out_offset=None, in_=states, in_offset=ends).then_inc(got[0].sem, 16)
                pool.wait_ge(carried, 2)
                pool.indirect_dma_start(out=states, out_offset=ends, in_=end_row[:], in_offset=None).then_inc(got[1].sem, 16)
                pool.wait_ge(got[1].sem, got[1].at(16 * ROUNDS + 16))

            @block.vector
            def _(dve):
                for h in range(2):
                    dve.tensor_copy(index[:, HALF * h:HALF * (h + 1)], g.src_at[:, HALF * h:HALF * (h + 1)])\
                       .then_inc(indices, 1)
                dve.memset(state[:, U - 1, :], -BIG).then_inc(reached, U)
                dve.memset(runs[:, :, 0:1], -BIG)
                with dve.Fori(0, ROUNDS) as i:
                    for k in range(U):
                        if k % HALF == 0:
                            dve.wait_ge(stored[k // HALF].sem, stored[k // HALF].at(16 * i))
                        dve.wait_ge(got[k].sem, got[k].at(16 * i + 16))
                        dve.wait_ge(reached, U * i + U + k)
                        dve.scalar_tensor_tensor(out=state[:, k, :], in0=state[:, (k - 1) % U, :],
                                                 scalar=g.keep_neg[:, ds(U * i + k, 1)], in1=rows[:, k, :],
                                                 op0=ALU.add, op1=ALU.max).then_inc(reached, 1)
                        if k % HALF == HALF - 1:
                            dve.wait_ge(reached, U * i + U + k + 1)
                            dve.tensor_copy(index[:, k - HALF + 1:k + 1], g.src_at[:, ds(U * i + U + k - HALF + 1, HALF)])\
                               .then_inc(indices, 1)
                dve.wait_ge(turned, 1)
                for j in range(2):
                    last = dve.tensor_tensor_scan(runs[:, j, 1:P + 1], g.cont_neg[:], ps_t[:, j * P:(j + 1) * P],
                                                  -BIG, ALU.add, ALU.max)
                last.then_inc(carried, 1)
                dve.wait_ge(turned, 2)
                dve.wait_ge(got[0].sem, got[0].at(16 * ROUNDS + 16))
                dve.scalar_tensor_tensor(out=end_row[:], in0=ps_c[:, 0:D], scalar=g.carry_in_neg[:, 0:1], in1=end_row[:],
                                         op0=ALU.add, op1=ALU.max).then_inc(carried, 1)

            @block.tensor
            def _(pe):
                def turn(b):
                    if b >= 2:
                        pe.wait_ge(x_copied, b - 1)
                    for j in range(2):
                        last = pe.transpose(ps_x[:, b % 2, j * P:(j + 1) * P], x[:, b, j * P:(j + 1) * P], g.ident[:])
                    last.then_inc(x_turned, 1)

                turn(0)
                for b in range(NB):
                    if b + 1 < NB:
                        turn(b + 1)
                    pe.wait_ge(x_copied, b + 1)
                    if b >= 2:
                        pe.wait_ge(x_taken, b - 1)
                    for j in range(2):
                        pe.matmul(ps_y[:, b % 2, 0:D], x_t[:, b % 2, j * P:(j + 1) * P], weights[:, j, :],
                                  start=(j == 0), stop=False)
                    pe.matmul(ps_y[:, b % 2, 0:D], g.ones[0:1, :], bias, start=False, stop=True).then_inc(x_multiplied, 1)
                pe.wait_ge(reached, U + EC)
                for j in range(2):
                    last = pe.transpose(ps_t[:, j * P:(j + 1) * P], state[:, U - 1, j * P:(j + 1) * P], g.ident[:])
                last.then_inc(turned, 1)
                pe.wait_ge(carried, 1)
                for j in range(2):
                    last = pe.transpose(ps_c[:, j * P:(j + 1) * P], runs[:, j, 0:P], g.ident[:])
                last.then_inc(turned, 1)

            @block.sync
            def _(sp):
                with sp.Fori(0, ROUNDS) as i:
                    for h in range(2):
                        sp.wait_ge(reached, U * i + U + HALF * (h + 1))
                        sp.dma_start(states_v[:, ds(U * i + HALF * h, HALF), :],
                                     state[:, HALF * h:HALF * (h + 1), :]).then_inc(stored[h].sem, 16)
                for h in range(2):
                    sp.wait_ge(stored[h].sem, stored[h].at(16 * ROUNDS))
    for q in got + stored:
        q.base += 16 * ROUNDS
    for q in got[0:2]:
        q.base += 16


@staged
def dense(g, name, x, weights, bias, width, relu, out, table=None):
    nc = g.nc
    R, BANKS = 5, 3
    turned, copied, multiplied, finished, stored = (
        g.sem(name + "_turned"), g.sem(name + "_copied"), g.sem(name + "_multiplied"),
        g.sem(name + "_finished"), g.sem(name + "_stored"))
    with ExitStack() as ctx:
        x_t = g.sb(name + "_x_t", [P, BANKS, D], ctx=ctx)
        ps_t = g.ps(name + "_t", [P, BANKS, 512], ctx=ctx)
        ps_y = g.ps(name + "_y", [P, BANKS, 512], ctx=ctx)
        with nc.Block() as block:
            @block.tensor
            def _(pe):
                def turn(b):
                    if b >= BANKS:
                        pe.wait_ge(copied, b - BANKS + 1)
                    for j in range(2):
                        last = pe.transpose(ps_t[:, b % BANKS, j * P:(j + 1) * P], x[:, b, j * P:(j + 1) * P], g.ident[:])
                    last.then_inc(turned, 1)

                turn(0)
                turn(1)
                for b in range(NB):
                    if b + 2 < NB:
                        turn(b + 2)
                    pe.wait_ge(copied, b + 1)
                    if b >= BANKS:
                        pe.wait_ge(finished, b - BANKS + 1)
                    y = ps_y[:, b % BANKS, 0:width]
                    for j in range(2):
                        last = pe.matmul(y, x_t[:, b % BANKS, j * P:(j + 1) * P], weights[:, j, :],
                                         start=(j == 0), stop=(j == 1 and bias is None))
                    if bias is not None:
                        last = pe.matmul(y, g.ones[0:1, :], bias, start=False, stop=True)
                    last.then_inc(multiplied, 1)

            @block.scalar
            def _(act):
                for b in range(NB):
                    act.wait_ge(turned, b + 1)
                    if b >= BANKS:
                        act.wait_ge(multiplied, b - BANKS + 1)
                    act.copy(x_t[:, b % BANKS, :], ps_t[:, b % BANKS, 0:D]).then_inc(copied, 1)

            @block.vector
            def _(dve):
                for b in range(NB):
                    dve.wait_ge(multiplied, b + 1)
                    y = ps_y[:, b % BANKS, 0:width]
                    if relu:
                        dve.tensor_scalar(out[:, b, :], y, 0.0, None, ALU.max).then_inc(finished, 1)
                    else:
                        dve.tensor_copy(out[:, b, :], y).then_inc(finished, 1)

            if table is not None:
                @block.sync
                def _(sp):
                    table_v = table.rearrange("(p b) f -> p b f", p=P)
                    for b in range(0, NB, R):
                        sp.wait_ge(finished, b + R)
                        sp.dma_start(table_v[:, b:b + R, :], out[:, b:b + R, :]).then_inc(stored, 16)
                    sp.wait_ge(stored, 16 * (NB // R))


@staged
def mix(g, name, states, weights, product, x, out, table=None):
    nc = g.nc
    R, BANKS = 5, 3
    SLOTS = 2 * R
    pool_in, turned, copied, multiplied, added, finished, stored = (
        g.sem(name + "_pool_in"), g.sem(name + "_turned"), g.sem(name + "_copied"), g.sem(name + "_multiplied"),
        g.sem(name + "_added"), g.sem(name + "_finished"), g.sem(name + "_stored"))
    got = g.dma_counts[0:SLOTS]
    with ExitStack() as ctx:
        sb = lambda n, s, d=F32: g.sb(name + "_" + n, s, d, ctx)
        last_row, best = sb("last_row", [P, SLOTS, D]), sb("best", [P, R, D])
        p_t = sb("p_t", [P, BANKS, D])
        ps_t = g.ps(name + "_t", [P, BANKS, 512], ctx=ctx)
        ps_y = g.ps(name + "_y", [P, BANKS, 512], ctx=ctx)
        with nc.Block() as block:
            @block.gpsimd
            def _(pool):
                for b in range(NB):
                    k = b % SLOTS
                    if b >= SLOTS:
                        pool.wait_ge(pool_in, b - SLOTS + 1)
                    pool.indirect_dma_start(
                        out=last_row[:, k, :], out_offset=None, in_=states,
                        in_offset=bass.IndirectOffsetOnAxis(ap=g.last_at[:, b:b + 1], axis=0)).then_inc(got[k].sem, 16)

            @block.vector
            def _(dve):
                for t in range(NB + 6):
                    b = t
                    if b < NB:
                        k = b % SLOTS
                        dve.wait_ge(got[k].sem, got[k].at(16 * (b // SLOTS + 1)))
                        if b >= R:
                            dve.wait_ge(turned, b - R + 1)
                        dve.tensor_scalar(best[:, b % R, :], last_row[:, b % SLOTS, :], g.has_edge[:, b:b + 1], None,
                                          ALU.mult).then_inc(pool_in, 1)
                    b = t - 4
                    if 0 <= b < NB:
                        dve.wait_ge(multiplied, b + 1)
                        dve.tensor_tensor(product[:, b, :], product[:, b, :], ps_y[:, b % BANKS, 0:D], ALU.add)\
                           .then_inc(added, 1)
                    b = t - 5
                    if 0 <= b < NB:
                        dve.wait_ge(added, b + 1)
                        if x is None:
                            dve.tensor_scalar(out[:, b, :], product[:, b, :], 0.0, None, ALU.max).then_inc(finished, 1)
                        else:
                            dve.scalar_tensor_tensor(out=out[:, b, :], in0=product[:, b, :], scalar=0.0,
                                                     in1=x[:, b, :], op0=ALU.max, op1=ALU.add).then_inc(finished, 1)

            @block.tensor
            def _(pe):
                def turn(b):
                    if b >= BANKS:
                        pe.wait_ge(copied, b - BANKS + 1)
                    pe.wait_ge(pool_in, b + 1)
                    for j in range(2):
                        last = pe.transpose(ps_t[:, b % BANKS, j * P:(j + 1) * P], best[:, b % R, j * P:(j + 1) * P], g.ident[:])
                    last.then_inc(turned, 1)

                turn(0)
                turn(1)
                for b in range(NB):
                    if b + 2 < NB:
                        turn(b + 2)
                    pe.wait_ge(copied, b + 1)
                    if b >= BANKS:
                        pe.wait_ge(added, b - BANKS + 1)
                    for j in range(2):
                        last = pe.matmul(ps_y[:, b % BANKS, 0:D], p_t[:, b % BANKS, j * P:(j + 1) * P], weights[:, j, :],
                                         start=(j == 0), stop=(j == 1))
                    last.then_inc(multiplied, 1)

            @block.scalar
            def _(act):
                for b in range(NB):
                    act.wait_ge(turned, b + 1)
                    if b >= BANKS:
                        act.wait_ge(multiplied, b - BANKS + 1)
                    act.copy(p_t[:, b % BANKS, :], ps_t[:, b % BANKS, 0:D]).then_inc(copied, 1)

            if table is not None:
                @block.sync
                def _(sp):
                    table_v = table.rearrange("(p b) f -> p b f", p=P)
                    for b in range(0, NB, R):
                        sp.wait_ge(finished, b + R)
                        sp.dma_start(table_v[:, b:b + R, :], out[:, b:b + R, :]).then_inc(stored, 16)
                    sp.wait_ge(stored, 16 * (NB // R))
    for k, q in enumerate(got):
        q.base += 16 * len(range(k, NB, SLOTS))


@staged
def attention_weights(g, w):
    nc = g.nc
    G = 8
    g.encode = g.sb("encode", [G * EF, G, D])
    zeroed, loaded = g.sem("encode_zeroed"), g.sem("encode_loaded")
    with nc.Block() as block:
        @block.vector
        def _(dve):
            dve.memset(g.encode[:], 0.0).then_inc(zeroed, 1)

        @block.sync
        def _(sp):
            sp.wait_ge(zeroed, 1)
            for j in range(G):
                sp.dma_start(g.encode[EF * j:EF * j + 3, j, :], w["L1_gnn_edge_W"].rearrange("o f -> f o"),
                             allow_slow_non_contiguous=True).then_inc(loaded, 16)
                sp.dma_start(g.encode[EF * j + 3:EF * j + 4, j, :], w["L1_gnn_edge_b"].rearrange("(a n) -> a n", a=1))\
                  .then_inc(loaded, 16)
            sp.wait_ge(loaded, 16 * 2 * G)


@staged
def attention_scan(g, name, table, states):
    nc = g.nc
    G = 4
    U = 2 * G
    ROUNDS = EC // U
    W = D + 2 * H
    A = D + H
    indices, edges_in, edges_turned, edges_ready, encoded = (
        g.sem(name + "_indices"), g.sem(name + "_edges_in"), g.sem(name + "_edges_turned"),
        g.sem(name + "_edges_ready"), g.sem(name + "_encoded"))
    weighed, scored, kept_in, exps, used = (g.sem(name + "_weighed"), g.sem(name + "_scored"), g.sem(name + "_kept"),
                                            g.sem(name + "_exps"), g.sem(name + "_used"))
    score_chain, state_chain, gate, turn_gate = (g.sem(name + "_score_chain"), g.sem(name + "_state_chain"),
                                                 g.sem(name + "_gate"), g.sem(name + "_turn_gate"))
    to_dve, to_pe, to_act, to_pool = (g.sem(name + "_to_dve"), g.sem(name + "_to_pe"), g.sem(name + "_to_act"),
                                      g.sem(name + "_to_pool"))
    got = g.dma_counts[0:U]
    stored = g.store_counts
    states_v = states.rearrange("(p c) f -> p c f", p=P)
    blocks = [(0, P), (P, P), (2 * P, A - 2 * P)]
    with ExitStack() as ctx:
        sb = lambda n, s, d=F32: g.sb(name + "_" + n, s, d, ctx)
        src_slot, dst_slot = sb("src_slot", [P, U], I32), sb("dst_slot", [P, U], I32)
        at_dst, at_src = sb("at_dst", [P, U, W]), sb("at_src", [P, U, W])
        edge_group, group_t = sb("edge_group", [P, U * EF]), sb("group_t", [U * EF, P])
        prod, prod_sum = sb("prod", [P, G, D]), sb("prod_sum", [P, G * H])
        score = sb("score", [P, G, H])
        top = sb("top", [P, 2, G + 1, H])
        args = sb("args", [P, 2, 2, G, H])
        decay = sb("decay", [P, 2, G, H])
        kept = sb("kept", [P, 2, G, D])
        part = sb("part", [P, 2, G * H, HD + 1])
        faded = sb("faded", [P, H, HD + 1])
        state = sb("state", [P, U, W])
        top_runs, runs = sb("top_runs", [H, P + 1]), sb("runs", [P, 3, P + 1])
        tops, end_args, end_exps = sb("tops", [P, 2, H]), sb("end_args", [P, 2, H]), sb("end_exps", [P, 2, H])
        end_state, end_decay = sb("end_state", [P, A]), sb("end_decay", [P, A])
        decay_t = sb("decay_t", [P, 3, P])
        end_row = sb("end_row", [P, W])
        join_args, join_exps, carry_top, both_top = (sb("join_args", [P, 2, H]), sb("join_exps", [P, 2, H]),
                                                     sb("carry_top", [P, H]), sb("both_top", [P, H]))
        ps_g = g.ps(name + "_g", [P, 512], ctx=ctx)
        ps_e = g.ps(name + "_e", [P, U, D], ctx=ctx)
        ps_a, ps_b, ps_c = (g.ps(name + n, [P, 512], ctx=ctx) for n in ("_a", "_b", "_c"))
        by_head = lambda ap: ap.rearrange("p (h d) -> p h d", h=H)
        with nc.Block() as block:
            @block.scalar
            def _(act):
                act.preload_act_table(ACT.Exp)
                act.sem_inc(edges_ready, 1)
                act.sem_inc(kept_in, 2)
                act.sem_inc(exps, 2)

                def send_indices(i, h):
                    act.wait_ge(weighed, 2 * i + h + 1)
                    act.wait_ge(kept_in, 2 * i + h + 1)
                    cols = slice(G * h, G * (h + 1))
                    act.copy(src_slot[:, cols], g.src_at[:, ds(U * i + G * h, G)])
                    act.copy(dst_slot[:, cols], g.dst_at[:, ds(U * i + G * h, G)]).then_inc(indices, 1)

                def send_edges(i):
                    act.wait_ge(edges_turned, i + 1)
                    act.copy(edge_group[:], g.edge_rows[:, ds(U * i, U), :].rearrange("p c f -> p (c f)"))\
                       .then_inc(edges_in, 1)
                    act.wait_ge(edges_turned, i + 2)
                    act.wait_ge(encoded, 2 * i + 1)
                    act.copy(group_t[:], ps_g[0:U * EF, 0:P]).then_inc(edges_ready, 1)

                def keep(i, h):
                    n = 2 * i + h
                    act.wait_ge(used, n + 1)
                    for k in range(G * h, G * (h + 1)):
                        act.wait_ge(got[k].sem, got[k].at(32 * i + 32))
                    act.copy(kept[:, h, :, :], at_src[:, G * h:G * (h + 1), 0:D]).then_inc(kept_in, 1)

                def exponentials(i, h):
                    act.wait_ge(scored, 2 * i + h + 3)
                    act.activation(part[:, h, :, HD], args[:, h, 0, :, :].rearrange("p g h -> p (g h)"), ACT.Exp)
                    act.activation(decay[:, h, :, :], args[:, h, 1, :, :], ACT.Exp).then_inc(exps, 1)

                send_indices(0, 0)
                send_edges(0)
                send_indices(0, 1)
                with act.Fori(0, ROUNDS - 1) as i:
                    for h in range(2):
                        keep(i, h)
                        send_indices(i + 1, h)
                        exponentials(i, h)
                        if h == 0:
                            send_edges(i + 1)
                for h in range(2):
                    keep(ROUNDS - 1, h)
                    exponentials(ROUNDS - 1, h)
                act.wait_ge(to_act, 1)
                act.activation(end_exps[:], end_args[:], ACT.Exp).then_inc(to_dve, 1)
                act.wait_ge(to_act, 2)
                for j, (_, n) in enumerate(blocks):
                    last = act.copy(decay_t[0:n, j, :], ps_b[0:n, j * P:(j + 1) * P])
                last.then_inc(to_dve, 1)
                act.wait_ge(to_act, 3)
                act.activation(join_exps[:], join_args[:], ACT.Exp).then_inc(to_dve, 1)

            @block.gpsimd
            def _(pool):
                with pool.Fori(0, ROUNDS) as i:
                    for h in range(2):
                        pool.wait_ge(indices, 2 * i + h + 1)
                        pool.sem_inc(gate, 1)
                        for k in range(G * h, G * (h + 1)):
                            for rows, slot in ((at_dst, dst_slot), (at_src, src_slot)):
                                pool.wait_ge(gate, 1)
                                pool.indirect_dma_start(
                                    out=rows[:, k, :], out_offset=None, in_=table,
                                    in_offset=bass.IndirectOffsetOnAxis(ap=slot[:, k:k + 1], axis=0))\
                                    .then_inc(got[k].sem, 16)
                for q in stored:
                    pool.wait_ge(q.sem, q.at(16 * ROUNDS))
                ends = bass.IndirectOffsetOnAxis(ap=g.first_end[:], axis=0)
                pool.indirect_dma_start(out=end_row[:], out_offset=None, in_=states, in_offset=ends).then_inc(got[0].sem, 16)
                pool.wait_ge(to_pool, 1)
                pool.indirect_dma_start(out=states, out_offset=ends, in_=end_row[:], in_offset=None).then_inc(got[1].sem, 16)
                pool.wait_ge(got[1].sem, got[1].at(32 * ROUNDS + 16))

            @block.tensor
            def _(pe):
                pe.sem_inc(edges_turned, 1)
                pe.sem_inc(encoded, 1)
                with pe.Fori(0, ROUNDS) as i:
                    pe.wait_ge(edges_in, i + 1)
                    pe.wait_ge(edges_ready, i + 1)
                    pe.sem_inc(turn_gate, 1)
                    pe.wait_ge(turn_gate, 1)
                    pe.transpose(ps_g[0:U * EF, 0:P], edge_group[:], g.ident[:]).then_inc(edges_turned, 1)
                    pe.wait_ge(edges_ready, i + 2)
                    for h in range(2):
                        pe.wait_ge(weighed, 2 * i + h + 1)
                        for k in range(G * h, G * (h + 1), 2):
                            last = pe.matmul(ps_e[:, k:k + 2, :].rearrange("p a f -> p (a f)"), group_t[:],
                                             g.encode[:, k:k + 2, :].rearrange("p a f -> p (a f)"),
                                             start=True, stop=True)
                        last.then_inc(encoded, 1)
                pe.wait_ge(used, 2 * ROUNDS + 2)
                pe.wait_ge(edges_ready, ROUNDS + 1)
                pe.transpose(ps_g[0:H, 0:P], top[:, 1, G, :], g.ident[:]).then_inc(to_dve, 1)
                pe.wait_ge(to_pe, 1)
                pe.transpose(ps_c[:, 0:H], top_runs[:, 0:P], g.ident[0:H, 0:H])
                pe.transpose(ps_c[:, H:2 * H], top_runs[:, 1:P + 1], g.ident[0:H, 0:H]).then_inc(to_dve, 1)
                pe.wait_ge(to_pe, 2)
                for j, (at, n) in enumerate(blocks):
                    last = pe.transpose(ps_b[0:n, j * P:(j + 1) * P], end_decay[:, at:at + n], g.ident[:])
                last.then_inc(to_act, 1)
                for j, (at, n) in enumerate(blocks):
                    last = pe.transpose(ps_a[0:n, j * P:(j + 1) * P], end_state[:, at:at + n], g.ident[:])
                last.then_inc(to_dve, 1)
                pe.wait_ge(to_pe, 3)
                for j, (at, n) in enumerate(blocks):
                    last = pe.transpose(ps_c[:, at:at + n], runs[0:n, j, 0:P], g.ident[0:n, 0:n])
                last.then_inc(to_dve, 1)

            @block.vector
            def _(dve):
                for sem in (weighed, scored, used):
                    dve.sem_inc(sem, 2)
                SCORE_STEPS, STATE_STEPS = 8 + G, 2 + 2 * G

                def score_and_state(new, old):
                    if new:
                        i, h = new
                        n = 2 * i + h
                        cols = slice(G * h, G * (h + 1))
                        at = ds(U * i + G * h, G)
                        ch = Chain(dve, score_chain, SCORE_STEPS * n + 1)
                        flat = score[:].rearrange("p c h -> p (c h)")
                        for k in range(G * h, G * (h + 1)):
                            dve.wait_ge(got[k].sem, got[k].at(32 * i + 32))
                        dve.wait_ge(encoded, n + 2)
                        ch.mark(dve.tensor_tensor(score[:], at_dst[:, cols, D + H:W], at_src[:, cols, D:D + H], ALU.add))
                        dve.scalar_tensor_tensor(out=prod[:], in0=ps_e[:, cols, :], scalar=0.0,
                                                 in1=at_dst[:, cols, 0:D], op0=ALU.max, op1=ALU.mult).then_inc(weighed, 1)
                    if old:
                        oi, oh = old
                        on = 2 * oi + oh
                        och = Chain(dve, state_chain, STATE_STEPS * on + 1)
                        dve.wait_ge(kept_in, on + 3)
                        dve.wait_ge(exps, on + 3)
                        och.mark(dve.tensor_tensor(part[:, oh, :, 0:HD],
                                                   kept[:, oh, :, :].rearrange("p g (h d) -> p (g h) d", h=H),
                                                   part[:, oh, :, HD:HD + 1].broadcast_to([P, G * H, HD]), ALU.mult))
                        dve.wait_ge(stored[oh].sem, stored[oh].at(16 * oi))
                        och.mark(dve.tensor_copy(state[:, G * oh:G * (oh + 1), A:W], top[:, oh, 1:G + 1, :]))
                    if new:
                        dve.wait_ge(weighed, n + 3)
                        ch.mark(dve.tensor_reduce(prod_sum[:], prod[:].rearrange("p c (h d) -> p (c h) d", h=H),
                                                  AX.X, ALU.add))
                    for step in range(2 * G):
                        if old:
                            j = step // 2
                            k = G * oh + j
                            och.sync()
                            if step % 2 == 0:
                                och.mark(dve.tensor_tensor(faded[:], by_head(state[:, (k - 1) % U, 0:A]),
                                                           decay[:, oh, j, :].unsqueeze(2)
                                                           .broadcast_to([P, H, HD + 1]), ALU.mult))
                            else:
                                och.mark(dve.tensor_tensor(by_head(state[:, k, 0:A]), faded[:],
                                                           part[:, oh, H * j:H * (j + 1), :], ALU.add))
                        if new:
                            ch.sync()
                            if step == 0:
                                ch.mark(dve.tensor_tensor(flat, flat, prod_sum[:], ALU.add))
                            elif step == 1:
                                ch.mark(dve.scalar_tensor_tensor(out=flat, in0=flat, scalar=0.2, in1=flat,
                                                                 op0=ALU.mult, op1=ALU.max))
                            elif step < G + 2:
                                k = step - 2
                                ch.mark(dve.scalar_tensor_tensor(out=top[:, h, k + 1, :], in0=top[:, h, k, :],
                                                                 scalar=g.keep_neg[:, ds(U * i + G * h + k, 1)],
                                                                 in1=score[:, k, :], op0=ALU.add, op1=ALU.max))
                            elif step == G + 2:
                                dve.wait_ge(exps, n + 1)
                                ch.mark(dve.tensor_tensor(args[:, h, 0, :, :], score[:], top[:, h, 1:G + 1, :], ALU.subtract))
                                ch.mark(dve.tensor_tensor(args[:, h, 1, :, :], top[:, h, 0:G, :],
                                                          g.keep_neg[:, at].unsqueeze(2).broadcast_to([P, G, H]), ALU.add))
                                ch.mark(dve.tensor_copy(top[:, 1 - h, 0, :], top[:, h, G, :]))
                            else:
                                ch.mark(dve.tensor_tensor(args[:, h, 1, :, :], args[:, h, 1, :, :], top[:, h, 1:G + 1, :],
                                                          ALU.subtract))
                    if new:
                        ch.sync()
                        dve.sem_inc(scored, 1)
                    if old:
                        och.sync()
                        dve.sem_inc(used, 1)

                ch = Chain(dve, score_chain)
                ch.link(dve.memset(top[:, 0, 0, :], -BIG))
                ch = Chain(dve, state_chain)
                ch.link(dve.memset(state[:, U - 1, 0:A], 0.0))
                dve.memset(top_runs[:, 0:1], -BIG)
                dve.memset(runs[:, :, 0:1], 0.0)
                score_and_state((0, 0), None)
                with dve.Fori(0, ROUNDS - 1) as i:
                    score_and_state((i, 1), (i, 0))
                    score_and_state((i + 1, 0), (i, 1))
                score_and_state((ROUNDS - 1, 1), (ROUNDS - 1, 0))
                score_and_state(None, (ROUNDS - 1, 1))

                ch = Chain(dve, state_chain, STATE_STEPS * 2 * ROUNDS + 1)
                dve.wait_ge(to_dve, 1)
                dve.tensor_tensor_scan(top_runs[:, 1:P + 1], g.cont_neg[0:H, :], ps_g[0:H, 0:P], -BIG, ALU.add, ALU.max)\
                   .then_inc(to_pe, 1)
                dve.wait_ge(to_dve, 2)
                ch.link(dve.tensor_copy(tops[:], ps_c[:, 0:2 * H].rearrange("p (a h) -> p a h", a=2)))
                ch.mark(dve.tensor_tensor(end_args[:, 0, :], top[:, 1, G, :], tops[:, 1, :], ALU.subtract))
                ch.link(dve.scalar_tensor_tensor(out=end_args[:, 1, :], in0=tops[:, 0, :], scalar=g.goes_on_neg[:, 0:1],
                                                 in1=tops[:, 1, :], op0=ALU.add, op1=ALU.subtract))
                dve.sem_inc(to_act, 1)
                dve.wait_ge(to_dve, 3)
                factor = lambda j: end_exps[:, j, :].unsqueeze(2).broadcast_to([P, H, HD + 1])
                ch.mark(dve.tensor_tensor(by_head(end_state[:]), by_head(state[:, U - 1, 0:A]), factor(0), ALU.mult))
                ch.link(dve.tensor_copy(by_head(end_decay[:]), factor(1)))
                dve.sem_inc(to_pe, 1)
                dve.wait_ge(to_dve, 5)
                for j, (_, n) in enumerate(blocks):
                    last = dve.tensor_tensor_scan(runs[0:n, j, 1:P + 1], decay_t[0:n, j, :], ps_a[0:n, j * P:(j + 1) * P],
                                                  0.0, ALU.mult, ALU.add)
                last.then_inc(to_pe, 1)
                dve.wait_ge(got[0].sem, got[0].at(32 * ROUNDS + 16))
                ch.link(dve.tensor_scalar(carry_top[:], tops[:, 0, :], g.carry_in_neg[:, 0:1], None, ALU.add))
                ch.link(dve.tensor_tensor(both_top[:], carry_top[:], end_row[:, A:W], ALU.max))
                ch.mark(dve.tensor_tensor(join_args[:, 0, :], end_row[:, A:W], both_top[:], ALU.subtract))
                ch.mark(dve.tensor_tensor(join_args[:, 1, :], carry_top[:], both_top[:], ALU.subtract))
                ch.sync()
                dve.sem_inc(to_act, 1)
                dve.wait_ge(to_dve, 7)
                join = lambda j: join_exps[:, j, :].unsqueeze(2).broadcast_to([P, H, HD + 1])
                ch.mark(dve.tensor_copy(end_row[:, A:W], both_top[:]))
                ch.mark(dve.tensor_tensor(by_head(end_row[:, 0:A]), by_head(end_row[:, 0:A]), join(0), ALU.mult))
                ch.link(dve.tensor_tensor(by_head(end_state[:]), by_head(ps_c[:, 0:A]), join(1), ALU.mult))
                ch.link(dve.tensor_tensor(end_row[:, 0:A], end_row[:, 0:A], end_state[:], ALU.add))
                dve.sem_inc(to_pool, 1)

            @block.sync
            def _(sp):
                with sp.Fori(0, ROUNDS) as i:
                    for h in range(2):
                        sp.wait_ge(used, 2 * i + h + 3)
                        sp.dma_start(states_v[:, ds(U * i + G * h, G), :],
                                     state[:, G * h:G * (h + 1), :]).then_inc(stored[h].sem, 16)
                for h in range(2):
                    sp.wait_ge(stored[h].sem, stored[h].at(16 * ROUNDS))
    for q in got:
        q.base += 32 * ROUNDS
    for q in got[0:2]:
        q.base += 16
    for q in stored:
        q.base += 16 * ROUNDS


@staged
def attend(g, name, states, x, bias):
    nc = g.nc
    R = 5
    A, W = D + H, D + 2 * H
    own, used = g.sem(name + "_chain"), g.sem(name + "_used")
    got = g.dma_counts[0:2 * R]
    with ExitStack() as ctx:
        sb = lambda n, s, d=F32: g.sb(name + "_" + n, s, d, ctx)
        row, share = sb("row", [P, 2, R, W]), sb("share", [P, R, D])
        factor = sb("factor", [P, R, H])
        by_head = lambda ap: ap.rearrange("p r (h d) -> p r h d", h=H)
        with nc.Block() as block:
            @block.gpsimd
            def _(pool):
                for b in range(NB):
                    i, k = b // R, b % R
                    if i >= 2 and k == 0:
                        pool.wait_ge(used, i - 1)
                    pool.indirect_dma_start(
                        out=row[:, i % 2, k, :], out_offset=None, in_=states,
                        in_offset=bass.IndirectOffsetOnAxis(ap=g.last_at[:, b:b + 1], axis=0))\
                        .then_inc(got[b % (2 * R)].sem, 16)

            @block.vector
            def _(dve):
                ch = Chain(dve, own)
                ch.link(dve.tensor_tensor(x[:], x[:], bias.unsqueeze(1).broadcast_to([P, NB, D]), ALU.add))
                for i in range(NB // R):
                    cols = slice(R * i, R * (i + 1))
                    state = by_head(row[:, i % 2, :, 0:A])
                    for k in range(R):
                        q = got[(R * i + k) % (2 * R)]
                        dve.wait_ge(q.sem, q.at(16 * (i // 2 + 1)))
                    ch.link(dve.tensor_scalar(factor[:], state[:, :, :, HD], 1e-10, None, ALU.max))
                    ch.link(dve.reciprocal(factor[:], factor[:]))
                    ch.link(dve.tensor_tensor(factor[:], factor[:], g.has_edge[:, cols].unsqueeze(2)
                                              .broadcast_to([P, R, H]), ALU.mult))
                    ch.link(dve.tensor_tensor(by_head(share[:]), state[:, :, :, 0:HD],
                                              factor[:].unsqueeze(3).broadcast_to([P, R, H, HD]), ALU.mult))
                    dve.sem_inc(used, 1)
                    ch.link(dve.tensor_tensor(x[:, cols, :], x[:, cols, :], share[:], ALU.add))
    for k, q in enumerate(got):
        q.base += 16 * len(range(k, NB, 2 * R))


class Mixture:

    def __init__(self, g, name, experts, hidden, gated):
        self.name, self.experts, self.hidden, self.gated = name, experts, hidden, gated
        self.pairs = 2 * NB
        tiles = (P * self.pairs + experts * (P - 1)) // P
        self.tiles = tiles + tiles % 2
        self.nothing = None
        self.rows_in = g.dram(name + "_rows_in", [self.tiles * P, D])
        self.rows_out = g.dram(name + "_rows_out", [self.tiles * P, D])


@staged
def route(g, m, logits):
    nc = g.nc
    n, X, C = m.name, m.experts, m.pairs
    m.row = g.sb(n + "_row", [P, C], I32, m.ctx)
    m.weight = g.sb(n + "_weight", [P, C], ctx=m.ctx)
    m.tile_expert = g.sb(n + "_tile_expert", [P, m.tiles], I32, m.ctx)
    own, gap_ready, exp_ready, summed, totals = (g.sem(n + "_chain"), g.sem(n + "_gap"), g.sem(n + "_exp"),
                                                 g.sem(n + "_summed"), g.sem(n + "_totals"))
    with ExitStack() as ctx:
        sb = lambda k, s, d=F32: g.sb(n + "_" + k, s, d, ctx)
        best, which = sb("best", [P, NB, 8]), sb("which", [P, NB, 8], U32)
        chosen, hot, upto = sb("chosen", [P, NB, 2]), sb("hot", [P, C, X]), sb("upto", [P, C, X])
        gap, total = sb("gap", [P, NB]), sb("total", [P, NB])
        across, expert_sum = sb("across", [P, X]), sb("expert_sum", [P, X])
        tiles_of, tiles_upto, base = sb("tiles_of", [P, X]), sb("tiles_upto", [P, X]), sb("base", [P, X])
        row_f, passed, tile_f = sb("row_f", [P, C]), sb("passed", [P, m.tiles, X]), sb("tile_f", [P, m.tiles])
        ps = g.ps(n + "_route", [P, 2, 512], ctx=ctx)
        with nc.Block() as block:
            @block.vector
            def _(dve):
                ch = Chain(dve, own)
                for b in range(NB):
                    ch.mark(dve.max(best[:, b, :], logits[:, b, 0:X]))
                dve.wait_ge(own, ch.n)
                for b in range(NB):
                    ch.mark(dve.max_index(which[:, b, :], best[:, b, :], logits[:, b, 0:X]))
                dve.tensor_tensor(gap[:], best[:, :, 1], best[:, :, 0], ALU.subtract).then_inc(gap_ready, 1)
                dve.wait_ge(own, ch.n)
                ch.link(dve.tensor_copy(chosen[:], which[:, :, 0:2]))
                ch.link(dve.tensor_tensor(hot[:], chosen[:].rearrange("p b j -> p (b j)").unsqueeze(2).broadcast_to([P, C, X]),
                                          g.ramp[:, 0:X].unsqueeze(1).broadcast_to([P, C, X]), ALU.is_equal))
                for e in range(X):
                    ch.mark(dve.tensor_tensor_scan(upto[:, :, e], g.ones[:, 0:C], hot[:, :, e], 0.0, ALU.mult, ALU.add))
                dve.wait_ge(own, ch.n)
                dve.tensor_copy(expert_sum[:], upto[:, C - 1, :]).then_inc(summed, 1)
                dve.wait_ge(exp_ready, 1)
                ch.link(dve.tensor_scalar(total[:], gap[:], 1.0, None, ALU.add))
                ch.link(dve.reciprocal(total[:], total[:]))
                pair = m.weight[:].rearrange("p (b j) -> p b j", j=2)
                dve.tensor_copy(pair[:, :, 0], total[:])
                dve.tensor_tensor(pair[:, :, 1], gap[:], total[:], ALU.mult)
                dve.wait_ge(totals, 1)
                ch.mark(dve.tensor_copy(across[:], ps[:, 0, 0:X]))
                ch.link(dve.tensor_scalar(expert_sum[:], ps[:, 1, 0:X], float(P - 1), None, ALU.add))
                floor_div(ch, dve, tiles_of[:], expert_sum[:], P, base[:])
                ch.link(dve.tensor_tensor_scan(tiles_upto[:], g.ones[:, 0:X], tiles_of[:], 0.0, ALU.mult, ALU.add))
                ch.link(dve.tensor_tensor(base[:], tiles_upto[:], tiles_of[:], ALU.subtract))
                ch.link(dve.scalar_tensor_tensor(out=base[:], in0=base[:], scalar=float(P), in1=across[:],
                                                 op0=ALU.mult, op1=ALU.add))
                ch.link(dve.tensor_tensor(upto[:], upto[:], base[:].unsqueeze(1).broadcast_to([P, C, X]), ALU.add))
                ch.link(dve.tensor_tensor(upto[:], upto[:], hot[:], ALU.mult))
                ch.link(dve.tensor_reduce(row_f[:], upto[:], AX.X, ALU.add))
                ch.link(dve.tensor_scalar(row_f[:], row_f[:], -1.0, None, ALU.add))
                dve.tensor_copy(m.row[:], row_f[:])
                ch.link(dve.tensor_tensor(passed[:], g.ramp[:, 0:m.tiles].unsqueeze(2).broadcast_to([P, m.tiles, X]),
                                          tiles_upto[:].unsqueeze(1).broadcast_to([P, m.tiles, X]), ALU.is_ge))
                ch.link(dve.tensor_reduce(tile_f[:], passed[:], AX.X, ALU.add))
                ch.link(dve.tensor_scalar(tile_f[:], tile_f[:], float(X - 1), None, ALU.min))
                dve.tensor_copy(m.tile_expert[:], tile_f[:])

            @block.scalar
            def _(act):
                act.wait_ge(gap_ready, 1)
                act.activation(gap[:], gap[:], ACT.Exp).then_inc(exp_ready, 1)

            @block.tensor
            def _(pe):
                pe.wait_ge(summed, 1)
                pe.matmul(ps[:, 0, 0:X], g.below[:], expert_sum[:], start=True, stop=True)
                pe.matmul(ps[:, 1, 0:X], g.ones[:], expert_sum[:], start=True, stop=True).then_inc(totals, 1)


@staged
def dispatch(g, m, x):
    nc = g.nc
    sent = g.dma_counts[0:2]
    with nc.Block() as block:
        @block.gpsimd
        def _(pool):
            for b in range(NB):
                for j in range(2):
                    pool.indirect_dma_start(
                        out=m.rows_in, in_=x[:, b, :], in_offset=None,
                        out_offset=bass.IndirectOffsetOnAxis(ap=m.row[:, 2 * b + j:2 * b + j + 1], axis=0))\
                        .then_inc(sent[j].sem, 16)
            for q in sent:
                pool.wait_ge(q.sem, q.at(16 * NB))
    for q in sent:
        q.base += 16 * NB


@staged
def gelu_biases(g, m, b1, b2):
    nc = g.nc
    X, HC = m.experts, m.hidden // P
    m.b1 = g.sb(m.name + "_b1", [P, X, HC], ctx=m.ctx)
    m.b2 = g.sb(m.name + "_b2", [P, X, D], ctx=m.ctx)
    loaded, turned = g.sem("biases_loaded"), g.sem("biases_turned")
    with ExitStack() as ctx:
        raw = g.sb(m.name + "_b1_raw", [X, m.hidden], ctx=ctx)
        ps = g.ps(m.name + "_b1", [P, 512], ctx=ctx)
        with nc.Block() as block:
            @block.sync
            def _(sp):
                sp.dma_start(raw[:], b1).then_inc(loaded, 16)
                sp.dma_start(m.b2[:], b2.unsqueeze(0).broadcast_to([P, X, D])).then_inc(loaded, 16)
                sp.wait_ge(loaded, 32)

            @block.tensor
            def _(pe):
                pe.wait_ge(loaded, 32)
                for c in range(HC):
                    last = pe.transpose(ps[:, c * X:(c + 1) * X], raw[:, c * P:(c + 1) * P], g.ident[0:X, 0:X])
                last.then_inc(turned, 1)

            @block.vector
            def _(dve):
                dve.wait_ge(turned, 1)
                dve.tensor_copy(m.b1[:].rearrange("p e c -> p c e"), ps[:, 0:HC * X].rearrange("p (c e) -> p c e", c=HC))


@staged
def experts(g, m, weights_in, weights_out):
    nc = g.nc
    n, HC = m.name, m.hidden // P
    NI = len(weights_in)
    COLS = HC * NI * P
    T = m.tiles
    row_loaded = g.dma_counts[0:2]
    w_in_loaded = [g.sem(f"{n}_w_in_loaded{s}") for s in range(2)]
    w_out_loaded = [g.sem(f"{n}_w_out_loaded{s}") for s in range(2)]
    turned, copied, hidden_ready, active, out_ready, out_copied = (
        g.sem(n + "_rows_turned"), g.sem(n + "_rows_copied"), g.sem(n + "_hidden"), g.sem(n + "_active"),
        g.sem(n + "_out"), g.sem(n + "_out_copied"))
    half_active, gate = g.sem(n + "_half_active"), g.sem(n + "_load_gate")
    stored = g.out_counts
    rows_in = m.rows_in.rearrange("(t p) f -> p t f", p=P)
    rows_out = m.rows_out.rearrange("(t p) f -> p t f", p=P)
    with ExitStack() as ctx:
        sb = lambda k, s, d=F32: g.sb(n + "_" + k, s, d, ctx)
        w_in = sb("w_in", [P, 2, NI, 2, m.hidden])
        w_out = sb("w_out", [P, 2, HC, D])
        row, row_t = sb("rows", [P, 2, D]), sb("rows_t", [P, 2, 2 * P])
        act_t = sb("act_t", [P, 2, HC * P])
        gate_t = sb("gate_t", [P, 2, HC * P]) if m.gated else None
        out = sb("out", [P, 2, D])
        nothing = sb("nothing", [1, 2, NI + 1])
        ps_t = g.ps(n + "_t", [P, 2, 512], ctx=ctx)
        ps_h = g.ps(n + "_h", [P, 2, COLS], ctx=ctx)
        ps_o = g.ps(n + "_o", [P, 2, 512], ctx=ctx)
        with nc.Block() as block:
            @block.sync
            def _(sp):
                def expert_of(t):
                    return sp.value_load(m.tile_expert[0:1, ds(t, 1)], min_val=0, max_val=m.experts - 1)

                def after(sem, value):
                    sp.wait_ge(sem, value)
                    sp.sem_inc(gate, 1)
                    sp.wait_ge(gate, 1)

                def load_in(s, expert):
                    for j in range(NI):
                        sp.dma_start(w_in[:, s, j, :, :], weights_in[j][ds(expert, 1), :, :]
                                     .rearrange("e (k p) h -> p (e k) h", p=P)).then_inc(w_in_loaded[s], 16)

                def load_out(s, expert):
                    sp.dma_start(w_out[:, s, :, :], weights_out[ds(expert, 1), :, :]
                                 .rearrange("e (k p) h -> p (e k) h", p=P)).then_inc(w_out_loaded[s], 16)

                def load_nothing(s, k, sem):
                    sp.dma_start(nothing[:, s, k:k + 1], m.nothing).then_inc(sem, 16)

                for s in range(2):
                    expert = expert_of(s)
                    load_in(s, expert)
                    load_out(s, expert)
                with sp.Fori(1, T // 2) as i:
                    for s in range(2):
                        t = 2 * i + s
                        expert, before = expert_of(t), expert_of(t - 2)
                        after(hidden_ready, t + 1)
                        with sp.If(expert != before):
                            load_in(s, expert)
                        with sp.If(expert == before):
                            for j in range(NI):
                                load_nothing(s, j, w_in_loaded[s])
                        after(out_ready, t + 1)
                        with sp.If(expert != before):
                            load_out(s, expert)
                        with sp.If(expert == before):
                            load_nothing(s, NI, w_out_loaded[s])

            @block.tensor
            def _(pe):
                pe.sem_inc(turned, 2)
                pe.sem_inc(hidden_ready, 2)
                pe.sem_inc(out_ready, 2)

                def turn(t, s, rnd):
                    pe.wait_ge(row_loaded[s].sem, row_loaded[s].at(16 * rnd + 16))
                    pe.wait_ge(copied, t + 1)
                    for j in range(2):
                        last = pe.transpose(ps_t[:, s, j * P:(j + 1) * P], row[:, s, j * P:(j + 1) * P], g.ident[:])
                    last.then_inc(turned, 1)

                def hidden(t, s, rnd):
                    pe.wait_ge(copied, t + 3)
                    pe.wait_ge(w_in_loaded[s], 16 * NI * (rnd + 1))
                    pe.wait_ge(active, t + 1)
                    for j in range(NI):
                        for c in range(HC):
                            for k in range(2):
                                last = pe.matmul(ps_h[:, s, (j * HC + c) * P:(j * HC + c + 1) * P],
                                                 w_in[:, s, j, k, c * P:(c + 1) * P],
                                                 row_t[:, s, k * P:(k + 1) * P], start=(k == 0), stop=(k == 1))
                    last.then_inc(hidden_ready, 1)

                def output(t, s, rnd):
                    pe.wait_ge(active, t + 3)
                    pe.wait_ge(w_out_loaded[s], 16 * (rnd + 1))
                    pe.wait_ge(out_copied, t + 1)
                    for c in range(HC):
                        last = pe.matmul(ps_o[:, s, 0:D], act_t[:, s, c * P:(c + 1) * P], w_out[:, s, c, :],
                                         start=(c == 0), stop=(c == HC - 1))
                    last.then_inc(out_ready, 1)

                turn(0, 0, 0)
                hidden(0, 0, 0)
                turn(1, 1, 0)
                with pe.Fori(0, T // 2 - 1) as i:
                    hidden(2 * i + 1, 1, i)
                    turn(2 * i + 2, 0, i + 1)
                    output(2 * i, 0, i)
                    hidden(2 * i + 2, 0, i + 1)
                    turn(2 * i + 3, 1, i + 1)
                    output(2 * i + 1, 1, i)
                hidden(T - 1, 1, T // 2 - 1)
                output(T - 2, 0, T // 2 - 1)
                output(T - 1, 1, T // 2 - 1)

            @block.scalar
            def _(act):
                act.preload_act_table(ACT.Silu if m.gated else ACT.Gelu)
                act.sem_inc(copied, 2)
                if not m.gated:
                    act.sem_inc(active, 2)
                b1 = None if m.gated else m.b1[:].rearrange("p e c -> p (e c)")

                def copy_rows(t, s):
                    act.wait_ge(turned, t + 3)
                    act.wait_ge(hidden_ready, t + 1)
                    act.copy(row_t[:, s, :], ps_t[:, s, 0:2 * P]).then_inc(copied, 1)

                def activate(t, s):
                    if not m.gated:
                        expert = act.value_load(m.tile_expert[0:1, ds(t, 1)], min_val=0, max_val=m.experts - 1)
                    act.wait_ge(hidden_ready, t + 3)
                    act.wait_ge(out_ready, t + 1)
                    if m.gated:
                        act.wait_ge(active, t + 1)
                        act.activation(gate_t[:, s, :], ps_h[:, s, 0:HC * P], ACT.Silu).then_inc(half_active, 1)
                    else:
                        for c in range(HC):
                            last = act.activation(act_t[:, s, c * P:(c + 1) * P], ps_h[:, s, c * P:(c + 1) * P],
                                                  ACT.Gelu, bias=b1[:, ds(expert * HC + c, 1)])
                        last.then_inc(active, 1)

                copy_rows(0, 0)
                with act.Fori(0, T // 2 - 1) as i:
                    copy_rows(2 * i + 1, 1)
                    activate(2 * i, 0)
                    copy_rows(2 * i + 2, 0)
                    activate(2 * i + 1, 1)
                copy_rows(T - 1, 1)
                activate(T - 2, 0)
                activate(T - 1, 1)

            @block.vector
            def _(dve):
                dve.sem_inc(out_copied, 2)
                if m.gated:
                    dve.sem_inc(active, 2)

                def act_mul(t, s):
                    dve.wait_ge(half_active, t + 1)
                    dve.tensor_tensor(act_t[:, s, :], gate_t[:, s, :], ps_h[:, s, HC * P:2 * HC * P], ALU.mult)\
                       .then_inc(active, 1)

                def take_out(t, s, rnd, expert):
                    dve.wait_ge(out_ready, t + 3)
                    dve.wait_ge(stored[s].sem, stored[s].at(16 * rnd))
                    if m.gated:
                        dve.tensor_copy(out[:, s, :], ps_o[:, s, 0:D]).then_inc(out_copied, 1)
                    else:
                        dve.tensor_tensor(out[:, s, :], ps_o[:, s, 0:D],
                                          m.b2[:, ds(expert, 1), :].rearrange("p a f -> p (a f)"), ALU.add)\
                           .then_inc(out_copied, 1)

                if m.gated:
                    act_mul(0, 0)
                    with dve.Fori(0, T // 2 - 1) as i:
                        act_mul(2 * i + 1, 1)
                        take_out(2 * i, 0, i, None)
                        act_mul(2 * i + 2, 0)
                        take_out(2 * i + 1, 1, i, None)
                    act_mul(T - 1, 1)
                    take_out(T - 2, 0, T // 2 - 1, None)
                    take_out(T - 1, 1, T // 2 - 1, None)
                else:
                    with dve.Fori(0, T // 2) as i:
                        for s in range(2):
                            expert = dve.value_load(m.tile_expert[0:1, ds(2 * i + s, 1)], min_val=0,
                                                    max_val=m.experts - 1)
                            take_out(2 * i + s, s, i, expert)

            @block.gpsimd
            def _(pool):
                def load_row(t, s):
                    pool.wait_ge(turned, t + 1)
                    pool.dma_start(row[:, s, :], rows_in[:, ds(t, 1), :].rearrange("p a f -> p (a f)"))\
                        .then_inc(row_loaded[s].sem, 16)

                def store_out(t, s):
                    pool.wait_ge(out_copied, t + 3)
                    pool.dma_start(rows_out[:, ds(t, 1), :].rearrange("p a f -> p (a f)"),
                                   out[:, s, :]).then_inc(stored[s].sem, 16)

                for t in range(3):
                    load_row(t, t % 2)
                with pool.Fori(0, T // 2 - 2) as i:
                    load_row(2 * i + 3, 1)
                    store_out(2 * i, 0)
                    load_row(2 * i + 4, 0)
                    store_out(2 * i + 1, 1)
                load_row(T - 1, 1)
                for t in range(T - 4, T):
                    store_out(t, t % 2)
                for q in stored:
                    pool.wait_ge(q.sem, q.at(16 * (T // 2)))
    for q in stored + row_loaded:
        q.base += 16 * (T // 2)


@staged
def combine(g, m, x):
    nc = g.nc
    SLOTS = 10
    first, second = g.sem(m.name + "_first_added"), g.sem(m.name + "_second_added")
    got = g.dma_counts[0:SLOTS]
    with ExitStack() as ctx:
        back = g.sb(m.name + "_back", [P, SLOTS, 2, D], ctx=ctx)
        with nc.Block() as block:
            @block.gpsimd
            def _(pool):
                for b in range(NB):
                    k = b % SLOTS
                    if b >= SLOTS:
                        pool.wait_ge(second, b - SLOTS + 1)
                    for j in range(2):
                        pool.indirect_dma_start(
                            out=back[:, k, j, :], out_offset=None, in_=m.rows_out,
                            in_offset=bass.IndirectOffsetOnAxis(ap=m.row[:, 2 * b + j:2 * b + j + 1], axis=0))\
                            .then_inc(got[k].sem, 16)

            @block.vector
            def _(dve):
                for t in range(NB + 1):
                    for b, j, added in ((t, 0, first), (t - 1, 1, second)):
                        if not 0 <= b < NB:
                            continue
                        k = b % SLOTS
                        if j == 0:
                            dve.wait_ge(got[k].sem, got[k].at(32 * (b // SLOTS + 1)))
                        else:
                            dve.wait_ge(first, b + 1)
                        dve.scalar_tensor_tensor(out=x[:, b, :], in0=back[:, k, j, :],
                                                 scalar=m.weight[:, 2 * b + j:2 * b + j + 1],
                                                 in1=x[:, b, :], op0=ALU.mult, op1=ALU.add).then_inc(added, 1)
    for k, q in enumerate(got):
        q.base += 32 * len(range(k, NB, SLOTS))


@staged
def store(g, x, out):
    nc = g.nc
    stored = g.sem("stored")
    with nc.Block() as block:
        @block.sync
        def _(sp):
            sp.dma_start(out.rearrange("(a b) f -> a b f", b=NB), x[0:N // NB]).then_inc(stored, 16)
            sp.wait_ge(stored, 16)


@staged
def gate_weights(g, gates):
    nc = g.nc
    loaded = g.sem("gates_loaded")
    with nc.Block() as block:
        @block.sync
        def _(sp):
            for name, (matrix, bias) in gates.items():
                X = matrix.shape[1]
                g.w[name] = g.sb(name, [P, 2, X])
                g.row[name] = g.sb(name + "_bias", [1, X])
                sp.dma_start(g.w[name][:], matrix.rearrange("(k p) e -> p k e", p=P)).then_inc(loaded, 16)
                sp.dma_start(g.row[name][:], bias.rearrange("(a n) -> a n", a=1)).then_inc(loaded, 16)
            sp.wait_ge(loaded, 32 * len(gates))


def mixture(g, m, x, biases, weights_in, weights_out):
    normalise(g, m.name + "_norm", x, g.cur)
    with ExitStack() as ctx:
        m.ctx = ctx
        m.nothing = weights_out[0, 0:1, 0:1]
        logits = g.sb(m.name + "_logits", [P, NB, m.experts], ctx=ctx)
        dense(g, m.name + "_gate", g.cur, g.w[m.name], g.row[m.name][:], m.experts, False, logits)
        route(g, m, logits)
        dispatch(g, m, g.cur)
        if biases:
            gelu_biases(g, m, *biases)
        experts(g, m, weights_in, weights_out)
        combine(g, m, x)


def write_program(nc, A, out):
    with ExitStack() as ctx:
        g = Program(nc, ctx)
        constants(g, A["src"])
        mix0, mix1 = Mixture(g, "L0_ffn", 8, 1024, False), Mixture(g, "L1_ffn", 16, 512, True)
        sort_edges(g, A["src"], A["dst"], A["edge_attr_3"], (mix0, mix1))
        resident(g)
        edge_tables(g, A["x"])
        layer_weights(g, A)
        gate_weights(g, {"L0_ffn": (A["L0_ffn_Wg"], A["L0_ffn_bg"]), "L1_ffn": (A["L1_ffn_gate_w"], A["L1_ffn_gate_b"])})
        attention_weights(g, A)

        table, states = g.dram("table", [NPAD, D]), g.dram("states", [EPAD, D])
        w, row = g.w, g.row
        normalise(g, "norm0", g.x, g.cur)
        dense(g, "pool_in", g.cur, w["L0_gnn_Wp1"], row["L0_gnn_bp1"][:], D, True, g.new, table)
        pool_max(g, "pool1", table, states, g.cur, w["L0_gnn_Wm1"], row["L0_gnn_bm1"][:], g.new)
        mix(g, "mix1", states, w["L0_gnn_Wm1"][:, 2:4, :], g.new, None, g.cur, table)
        pool_max(g, "pool2", table, states, g.cur, w["L0_gnn_Wm2"], row["L0_gnn_bm2"][:], g.new)
        mix(g, "mix2", states, w["L0_gnn_Wm2"][:, 2:4, :], g.new, g.cur, g.new)
        normalise(g, "norm2", g.new, g.cur, g.wide["L0_gnn_ln2_g"][:], g.wide["L0_gnn_ln2_b"][:], None, table)
        pool_max(g, "pool3", table, states, g.cur, w["L0_gnn_Wm3"], row["L0_gnn_bm3"][:], g.new)
        mix(g, "mix3", states, w["L0_gnn_Wm3"][:, 2:4, :], g.new, g.cur, g.new)
        normalise(g, "norm3", g.new, g.cur, g.wide["L0_gnn_ln3_g"][:], g.wide["L0_gnn_ln3_b"][:], g.x)

        mixture(g, mix0, g.x, (A["L0_ffn_b1"], A["L0_ffn_b2"]),
                [A["L0_ffn_W1"]], A["L0_ffn_W2"])

        W = D + 2 * H
        head_table, head_states = g.dram("head_table", [NPAD, W]), g.dram("head_states", [EPAD, W])
        normalise(g, "norm4", g.x, g.cur)
        with ExitStack() as scope:
            heads = g.sb("heads", [P, NB, W], ctx=scope)
            dense(g, "heads", g.cur, g.w["L1_gnn_W"], None, W, False, heads, head_table)
        attention_scan(g, "att", head_table, head_states)
        attend(g, "attend", head_states, g.x, g.wide["L1_gnn_bias"][:])

        mixture(g, mix1, g.x, None, [A["L1_ffn_w1"], A["L1_ffn_w2"]], A["L1_ffn_w3"])
        store(g, g.x, out)


def kernel(**inputs):
    import numpy as _np
    import concourse.bacc as _bacc
    from concourse import mybir as _mybir
    from concourse.bass_utils import run_bass_kernel_spmd as _run

    nc = _bacc.Bacc("TRN2", target_bir_lowering=False, num_devices=1)
    arrays, args = {}, {}
    for name, value in inputs.items():
        a = _np.ascontiguousarray(value)
        arrays[f"in_{name}_dram"] = a
        args[name] = nc.dram_tensor(f"in_{name}_dram", a.shape, _mybir.dt.from_np(a.dtype), kind="ExternalInput").ap()
    out = nc.dram_tensor("out_0_dram", (N, D), _mybir.dt.float32, kind="ExternalOutput").ap()
    write_program(nc, args, out)
    r = _run(nc, [arrays], core_ids=[0])
    return r.results[0]["out_0_dram"]
```

```python
from contextlib import ExitStack, contextmanager

import concourse.bass as bass
from concourse import mybir

ALU = mybir.AluOpType
ACT = mybir.ActivationFunctionType
AX = mybir.AxisListType
F32 = mybir.dt.float32
BF16 = mybir.dt.bfloat16
I32 = mybir.dt.int32
U32 = mybir.dt.uint32

P = 128
N = 3125
NB = 25
NPAD = P * NB
E = 50000
EC = 392
EPAD = P * EC
D = 256
H = 8
HD = D // H
EF = 6
SRC, DST = 4, 5
BIG = 1e38
MAGIC = 12582912.0
EPS = 1e-5
ds = bass.ds


class DmaCount:

    def __init__(self, sem):
        self.sem, self.base = sem, 16

    def at(self, n):
        return self.base + n


class Chain:

    def __init__(self, eng, sem, at=0):
        self.eng, self.sem, self.n = eng, sem, at

    def mark(self, ins):
        self.n = self.n + 1
        ins.then_inc(self.sem, 1)

    def sync(self):
        self.eng.wait_ge(self.sem, self.n)

    def link(self, ins):
        self.mark(ins)
        self.sync()


def staged(write):
    def run(g, *args, **kwargs):
        with g.stage():
            return write(g, *args, **kwargs)
    return run


class Program:

    def __init__(self, nc, ctx):
        self.nc, self.ctx = nc, ctx
        counts = lambda name, n: [DmaCount(ctx.enter_context(nc.semaphore(f"{name}{k}"))) for k in range(n)]
        self.dma_counts = counts("gpsimd_dma", 14)
        self.place_counts = counts("place_dma", 8)
        self.store_counts = counts("sync_store", 2)
        self.out_counts = counts("gpsimd_store", 2)

    def sem(self, name):
        handle = self.stage_ctx.enter_context(self.nc.semaphore(name))
        self.stage_sems.append(handle)
        return handle

    @contextmanager
    def stage(self):
        self.stage_sems = []
        with ExitStack() as self.stage_ctx:
            yield
            for handle in self.stage_sems:
                self.nc.gpsimd.sem_clear(handle)

    def sb(self, name, shape, dt=F32, ctx=None):
        return (ctx or self.ctx).enter_context(self.nc.sbuf_tensor("sb_" + name, shape, dt))

    def ps(self, name, shape, dt=F32, ctx=None):
        return (ctx or self.ctx).enter_context(self.nc.psum_tensor("ps_" + name, shape, dt))

    def dram(self, name, shape, dt=F32):
        return self.nc.dram_tensor("dram_" + name, shape, dt, kind="Internal").ap()


def floor_div(ch, eng, out, in_, by, ctx_tmp):
    ch.link(eng.tensor_scalar(ctx_tmp, in_, -(by - 1) / 2.0, 1.0 / by, ALU.add, ALU.mult))
    ch.link(eng.tensor_scalar(out, ctx_tmp, MAGIC, None, ALU.add))
    ch.link(eng.tensor_scalar(out, out, -MAGIC, None, ALU.add))


def resident(g):
    g.x = g.sb("x", [P, NB, D])
    g.cur = g.sb("cur", [P, NB, D])
    g.new = g.sb("new", [P, NB, D])
    g.stats = g.sb("stats", [P, NB, 6])
    g.moments = g.sb("moments", [P, NB, 2])
    g.src_at = g.sb("src_at", [P, EC + 14], I32)
    g.dst_at = g.sb("dst_at", [P, EC], I32)
    g.edge_rows = g.sb("edge_rows", [P, EC, EF])
    g.before = g.sb("before", [P, 1])
    g.carry_in_neg = g.sb("carry_in_neg", [P, 1])
    g.first_end = g.sb("first_end", [P, 1], I32)
    g.goes_on_neg = g.sb("goes_on_neg", [P, 1])
    g.keep = g.sb("keep", [P, EC])
    g.keep_neg = g.sb("keep_neg", [P, EC])
    g.cont = g.sb("cont", [P, P])
    g.cont_neg = g.sb("cont_neg", [P, P])


@staged
def constants(g):
    nc = g.nc
    g.ident = g.sb("ident", [P, P])
    g.identb = g.sb("identb", [P, P], BF16)
    g.below = g.sb("below", [P, P])
    g.ones = g.sb("ones", [P, P])
    g.node_base = g.sb("node_base", [P, P])
    g.ramp = g.sb("ramp", [P, P])
    g.rampb = g.sb("rampb", [P, P], BF16)
    g.part_index = g.sb("part_index", [P, 1])
    g.first_pos = g.sb("first_pos", [P, 1])
    zero_done, tri_done, ramp_done = g.sem("zero_done"), g.sem("tri_done"), g.sem("ramp_done")
    with nc.Block() as block:
        @block.gpsimd
        def _(pool):
            pool.memset(g.ident[:], 0.0).then_inc(zero_done, 1)
            pool.memset(g.below[:], 1.0).then_inc(zero_done, 1)
            pool.memset(g.ones[:], 1.0)
            pool.wait_ge(zero_done, 2)
            pool.affine_select(out=g.ident[:], in_=g.ident[:], compare_op=ALU.not_equal, fill=1.0,
                               base=0, pattern=[[-1, P]], channel_multiplier=1).then_inc(tri_done, 1)
            pool.affine_select(out=g.below[:], in_=g.below[:], compare_op=ALU.is_ge, fill=0.0,
                               base=-1, pattern=[[1, P]], channel_multiplier=-1).then_inc(tri_done, 1)
            pool.iota(g.ramp[:], pattern=[[1, P]], base=0, channel_multiplier=0,
                      allow_small_or_imprecise_dtypes=True).then_inc(ramp_done, 1)
            pool.iota(g.part_index[:], pattern=[[0, 1]], base=0, channel_multiplier=1,
                      allow_small_or_imprecise_dtypes=True)
            pool.iota(g.first_pos[:], pattern=[[0, 1]], base=0, channel_multiplier=EC,
                      allow_small_or_imprecise_dtypes=True)

        @block.vector
        def _(dve):
            dve.wait_ge(tri_done, 2)
            dve.tensor_copy(g.identb[:], g.ident[:])
            dve.wait_ge(ramp_done, 1)
            dve.tensor_scalar(g.node_base[:], g.ramp[:], float(NB), None, ALU.mult)
            dve.tensor_copy(g.rampb[:], g.ramp[:])


def load_edges(src, tile, sem, eng, width=1):
    full = E // EC
    rest = E - full * EC
    if width == 1:
        eng.dma_start(tile[0:full, :], src[0:full * EC].rearrange("(p c) -> p c", c=EC)).then_inc(sem, 16)
        eng.dma_start(tile[full:full + 1, 0:rest], src[full * EC:E].rearrange("(p c) -> p c", p=1)).then_inc(sem, 16)
    else:
        eng.dma_start(tile[0:full, :, :], src[0:full * EC, :].rearrange("(p c) w -> p c w", c=EC)).then_inc(sem, 16)
        eng.dma_start(tile[full:full + 1, 0:rest, :],
                      src[full * EC:E, :].rearrange("(p c) w -> p c w", p=1)).then_inc(sem, 16)


class LayerWeights:

    LAYERS = ["L0_gnn_Wp1", "L0_gnn_Wm1", "L0_gnn_Wm2", "L0_gnn_Wm3", "L1_gnn_W"]
    ROWS = ["L0_gnn_bm1", "L0_gnn_bm2", "L0_gnn_bm3"]
    SPREAD = ["L0_gnn_bp1", "L0_gnn_ln2_g", "L0_gnn_ln2_b", "L0_gnn_ln3_g", "L0_gnn_ln3_b", "L1_gnn_bias"]
    GROUP = 8

    def __init__(self, g, w):
        self.g, self.w = g, w
        g.w, g.row, g.wide = {}, {}, {}
        for n in self.LAYERS:
            g.w[n] = g.sb(n, [P, w[n].shape[1] // P, D + (2 * H if n == "L1_gnn_W" else 0)])
        for n in self.ROWS:
            g.row[n] = g.sb(n, [1, D])
        for n in self.SPREAD:
            g.wide[n] = g.sb(n, [P, D])
        self.gates = {"L0_ffn": (w["L0_ffn_Wg"], w["L0_ffn_bg"]), "L1_ffn": (w["L1_ffn_gate_w"], w["L1_ffn_gate_b"])}
        for n, (matrix, bias) in self.gates.items():
            g.w[n] = g.sb(n, [P, 2, matrix.shape[1]])
            g.wide[n] = g.sb(n + "_bias", [P, matrix.shape[1]])
        g.encode = g.sb("encode", [self.GROUP * EF, self.GROUP, D])
        self.loaded, self.small, self.zeroed, self.vectors = (
            g.sem("weights_loaded"), g.sem("small_loaded"), g.sem("weights_zeroed"), g.sem("head_vectors"))
        self.blocks = [(n, k) for n in self.LAYERS for k in range(w[n].shape[1] // P)]

    def allocate(self, ctx):
        g, w = self.g, self.w
        self.by_head = g.sb("by_head", [P, 2, 2 * H], ctx=ctx)
        self.raw = {n: g.sb("raw_" + n, [P, 2, w[n].shape[1]], ctx=ctx) for n in self.LAYERS}

    def allocate_turning(self, ctx):
        g = self.g
        self.turned, self.copied, self.folded = g.sem("weights_turned"), g.sem("weights_copied"), g.sem("weights_folded")
        self.ps_fold = g.ps("fold", [P, 2, 512], ctx=ctx)
        self.ps = g.ps("weights", [P, 2, 512], ctx=ctx)

    def zero(self, pool):
        pool.memset(self.by_head[:], 0.0).then_inc(self.zeroed, 1)
        pool.memset(self.g.encode[:], 0.0).then_inc(self.zeroed, 1)

    def load(self, act):
        g, w = self.g, self.w
        for n in self.LAYERS:
            act.dma_start(self.raw[n][:], w[n].rearrange("(o p) k -> p o k", p=P)).then_inc(self.loaded, 16)
        act.wait_ge(self.zeroed, 2)
        for j, n in enumerate(("a_src", "a_dst")):
            for h in range(H):
                at = h * HD
                act.dma_start(self.by_head[at % P:at % P + HD, at // P, j * H + h:j * H + h + 1],
                              w["L1_gnn_" + n][h, :].unsqueeze(1), allow_slow_non_contiguous=True)\
                   .then_inc(self.vectors, 16)
        pairs = [(g.row[n][:], w[n].rearrange("(a n) -> a n", a=1)) for n in self.ROWS]
        pairs += [(g.wide[n][:], w[n].rearrange("(a n) -> a n", a=1).broadcast_to([P, D])) for n in self.SPREAD]
        for n, (matrix, bias) in self.gates.items():
            pairs += [(g.w[n][:], matrix.rearrange("(k p) e -> p k e", p=P)),
                      (g.wide[n][:], bias.rearrange("(a n) -> a n", a=1).broadcast_to([P, matrix.shape[1]]))]
        for j in range(self.GROUP):
            pairs += [(g.encode[EF * j:EF * j + 3, j, :], w["L1_gnn_edge_W"].rearrange("o f -> f o")),
                      (g.encode[EF * j + 3:EF * j + 4, j, :], w["L1_gnn_edge_b"].rearrange("(a n) -> a n", a=1))]
        for out, in_ in pairs:
            act.dma_start(out, in_, allow_slow_non_contiguous=True).then_inc(self.small, 16)
        act.wait_ge(self.small, 16 * len(pairs))
        act.wait_ge(self.loaded, 16 * len(self.LAYERS))
        act.wait_ge(self.vectors, 16 * 2 * H)

    def copy(self, act):
        g = self.g
        for j, (n, k) in enumerate(self.blocks):
            act.wait_ge(self.turned, j + 1)
            act.copy(g.w[n][:, k, 0:D], self.ps[:, j % 2, 0:D]).then_inc(self.copied, 1)
        act.wait_ge(self.folded, 2)
        act.copy(g.w["L1_gnn_W"][:, :, D:], self.ps_fold[:, :, 0:2 * H])

    def turn(self, pe):
        for j, (n, k) in enumerate(self.blocks):
            if j >= 2:
                pe.wait_ge(self.copied, j - 1)
            for o in range(2):
                last = pe.transpose(self.ps[:, j % 2, o * P:(o + 1) * P], self.raw[n][:, o, k * P:(k + 1) * P],
                                    self.g.ident[:])
            last.then_inc(self.turned, 1)
        for k in range(2):
            for o in range(2):
                last = pe.matmul(self.ps_fold[:, k, 0:2 * H], self.raw["L1_gnn_W"][:, o, k * P:(k + 1) * P],
                                 self.by_head[:, o, :], start=(o == 0), stop=(o == 1))
            last.then_inc(self.folded, 1)


@staged
def sort_edges(g, src, dst, attr, x, w, weights_ctx):
    nc = g.nc
    weights = g.weights = LayerWeights(g, w)
    g.sorted_edges = g.dram("sorted_edges", [EPAD, EF])
    g.has_edge = g.sb("has_edge", [P, NB])
    g.last_at = g.sb("last_at", [P, NB], I32)
    g.unsorted = g.sb("unsorted", [P, 1], I32)
    sorted_v = g.sorted_edges.rearrange("(p c) f -> p c f", p=P)
    U = 7
    ROUNDS = EC // (2 * U)
    loaded, dst_loaded, filled = g.sem("edges_loaded"), g.sem("dst_loaded"), g.sem("edges_filled")
    rows_copied, hot_used, steps_ready = g.sem("rows_copied"), g.sem("hot_used"), g.sem("steps_ready")
    rows_ready, rows_stored = g.sem("rows_ready"), g.sem("rows_stored")
    hot_done, counted, ranged = g.sem("hot_done"), g.sem("counted"), g.sem("ranged")
    x_filled, x_loaded = g.sem("x_filled"), g.sem("x_loaded")
    prefix_done, offsets_done = g.sem("prefix_done"), g.sem("offsets_done")
    weights.allocate(weights_ctx)
    with ExitStack() as ctx:
        sb = lambda n, s, d=F32: g.sb(n, s, d, ctx)
        src_i, dst_i = sb("src_i", [P, EC], I32), sb("dst_i", [P, EC], I32)
        attr_t = sb("attr_t", [P, EC, 3])
        rows = sb("rows", [P, EC, EF])
        part_base, col = sb("part_base", [P, EC]), sb("col", [P, EC])
        part_b, col_b = sb("part_b", [P, EC], BF16), sb("col_b", [P, EC], BF16)
        hot_a, hot_b = sb("hot_a", [P, 2, U, P], BF16), sb("hot_b", [P, 2, U, NB], BF16)
        count, upto, row_sum, start, tmp = (sb("count", [P, NB]), sb("upto", [P, NB]),
                                            sb("row_sum", [P, 1]), sb("start", [P, NB]), sb("tmp_n", [P, NB]))
        next_i, step_down = sb("next_i", [P, 1], I32), sb("step_down", [P, EC])
        first_load = sb("first_load", [1, 32], I32)
        next_dst, steps_down = sb("next_dst", [P, 1]), sb("steps_down", [P, 1])
        ps_count = g.ps("count", [P, 512], F32, ctx)

        with nc.Block() as block:
            @block.sync
            def _(sp):
                sp.wait_ge(filled, 4)
                load_edges(dst, dst_i, dst_loaded, sp)
                sp.dma_start(next_i[0:P - 1, :], dst[EC:(P - 1) * EC + 1:EC].unsqueeze(1),
                             allow_slow_non_contiguous=True).then_inc(dst_loaded, 16)
                load_edges(src, src_i, loaded, sp)
                load_edges(attr, attr_t, loaded, sp, 3)
                sp.wait_ge(x_filled, 1)
                sp.dma_start(g.x[0:N // NB, :, :], x.rearrange("(a b) f -> a b f", b=NB)).then_inc(x_loaded, 16)
                sp.wait_ge(rows_ready, 1)
                sp.wait_ge(rows_copied, 2)
                sp.dma_start(sorted_v, rows[:]).then_inc(rows_stored, 16)
                sp.wait_ge(rows_stored, 16)
                for k, q in enumerate(g.store_counts):
                    sp.dma_start(first_load[:, k:k + 1], src[k:k + 1].rearrange("(a n) -> a n", a=1)).then_inc(q.sem, 16)
                for q in g.store_counts:
                    sp.wait_ge(q.sem, 16)
                sp.wait_ge(x_loaded, 16)

            @block.vector
            def _(dve):
                ch = Chain(dve, prefix_done)
                dve.memset(dst_i[:], N).then_inc(filled, 1)
                dve.memset(src_i[:], 0).then_inc(filled, 1)
                dve.memset(attr_t[:], 0.0).then_inc(filled, 1)
                dve.memset(next_i[:], N).then_inc(filled, 1)
                ch.mark(dve.memset(rows[:, :, 3:4], 1.0))
                dve.wait_ge(dst_loaded, 48)
                ch.mark(dve.tensor_copy(next_dst[:], next_i[:]))
                ch.link(dve.tensor_copy(rows[:, :, DST], dst_i[:]))
                dve.sem_inc(rows_ready, 1)
                floor_div(ch, dve, part_base[:], rows[:, :, DST], NB, col[:])
                ch.link(dve.tensor_copy(part_b[:], part_base[:]))
                ch.link(dve.tensor_scalar(part_base[:], part_base[:], float(NB), None, ALU.mult))
                ch.link(dve.tensor_tensor(col[:], rows[:, :, DST], part_base[:], ALU.subtract))
                ch.link(dve.tensor_copy(col_b[:], col[:]))
                with dve.Fori(0, ROUNDS) as i:
                    for h in range(2):
                        dve.wait_ge(hot_used, 2 * i + h + 1)
                        dve.tensor_tensor(hot_a[:, h, :, :],
                                          part_b[:, ds(2 * U * i + U * h, U)].unsqueeze(2).broadcast_to([P, U, P]),
                                          g.rampb[:].unsqueeze(1).broadcast_to([P, U, P]),
                                          ALU.is_equal).then_inc(hot_done, 1)
                        dve.tensor_tensor(hot_b[:, h, :, :],
                                          col_b[:, ds(2 * U * i + U * h, U)].unsqueeze(2).broadcast_to([P, U, NB]),
                                          g.rampb[:, 0:NB].unsqueeze(1).broadcast_to([P, U, NB]),
                                          ALU.is_equal).then_inc(hot_done, 1)
                ch.mark(dve.tensor_tensor(step_down[:, 0:EC - 1], rows[:, 0:EC - 1, DST], rows[:, 1:EC, DST], ALU.is_gt))
                ch.link(dve.tensor_tensor(step_down[:, EC - 1:EC], rows[:, EC - 1:EC, DST], next_dst[:], ALU.is_gt))
                dve.tensor_reduce(steps_down[:], step_down[:], AX.X, ALU.add).then_inc(steps_ready, 1)
                dve.wait_ge(counted, 1)
                ch.link(dve.tensor_copy(count[:], ps_count[:, 0:NB]))
                ch.link(dve.tensor_tensor_scan(upto[:], g.ones[:, 0:NB], count[:], 0.0, ALU.mult, ALU.add))
                dve.tensor_copy(row_sum[:], upto[:, NB - 1:NB]).then_inc(ranged, 1)
                dve.wait_ge(offsets_done, 1)
                dve.tensor_scalar(g.unsorted[:], ps_count[:, NB + 1:NB + 2], 1.0, None, ALU.min)
                ch.link(dve.tensor_scalar(upto[:], upto[:], ps_count[:, NB:NB + 1], None, ALU.add))
                dve.tensor_tensor(start[:], upto[:], count[:], ALU.subtract)
                dve.tensor_scalar(g.has_edge[:], count[:], 0.0, None, ALU.is_gt)
                ch.link(dve.tensor_scalar(tmp[:], upto[:], -1.0, 0.0, ALU.add, ALU.max))
                dve.tensor_copy(g.last_at[:], tmp[:])

            @block.tensor
            def _(pe):
                pe.sem_inc(hot_used, 2)

                def count_half(n, h, first=False, last=False):
                    pe.wait_ge(hot_done, 2 * n + 2)
                    for c in range(U):
                        end = pe.matmul(ps_count[:, 0:NB], hot_a[:, h, c, :], hot_b[:, h, c, :],
                                        start=(first and c == 0), stop=(last and c == U - 1))
                    end.then_inc(counted if last else hot_used, 1)

                count_half(0, 0, first=True)
                with pe.Fori(0, ROUNDS - 1) as i:
                    count_half(2 * i + 1, 1)
                    count_half(2 * i + 2, 0)
                count_half(2 * ROUNDS - 1, 1, last=True)
                pe.wait_ge(steps_ready, 1)
                pe.wait_ge(ranged, 1)
                pe.matmul(ps_count[:, NB:NB + 1], g.below[:], row_sum[:], start=True, stop=True)
                pe.matmul(ps_count[:, NB + 1:NB + 2], g.ones[:], steps_down[:], start=True, stop=True)\
                  .then_inc(offsets_done, 1)

            @block.gpsimd
            def _(pool):
                pool.memset(g.x[:], 0.0).then_inc(x_filled, 1)
                weights.zero(pool)
                gpsimd_counts = g.dma_counts + g.place_counts + g.out_counts
                for k, q in enumerate(gpsimd_counts, len(g.store_counts)):
                    pool.dma_start(first_load[:, k:k + 1], src[k:k + 1].rearrange("(a n) -> a n", a=1)).then_inc(q.sem, 16)
                for q in gpsimd_counts:
                    pool.wait_ge(q.sem, 16)

            @block.scalar
            def _(act):
                act.wait_ge(loaded, 64)
                act.copy(rows[:, :, SRC], src_i[:]).then_inc(rows_copied, 1)
                act.copy(rows[:, :, 0:3], attr_t[:]).then_inc(rows_copied, 1)
                weights.load(act)

        place_edges(g, ctx, rows, part_base, col, start)


def place_edges(g, ctx, rows, part_base, col, start):
    nc = g.nc
    U = 8
    ROUNDS = EC // U
    sb = lambda n, s, d=F32: g.sb(n, s, d, ctx)
    hot_a, hot_b = sb("hot_a_slot", [P, U, P], BF16), sb("hot_b_slot", [P, U, NB], BF16)
    hotT_f = sb("hotT_f", [P, U, P])
    hotT_b = sb("hotT_b", [P, U, P], BF16)
    seen = sb("seen", [P, U, NB])
    same = sb("same", [P, U, P], BF16)
    picked = sb("picked", [P, U, NB])
    pos_f = sb("pos_f", [P, U])
    pos_i = sb("pos_i", [P, U], I32)
    row_slot = sb("row_slot", [P, U, EF])
    ps_hotT = g.ps("hotT", [P, 2, 1024], BF16, ctx)
    ps_same = g.ps("same", [P, 2, 512], F32, ctx)
    ps_seen = g.ps("seen", [P, 512], F32, ctx)
    ps_pos = g.ps("pos", [P, 2, 512], F32, ctx)
    turned, turned_copied = g.sem("hot_turned"), g.sem("hot_turned_copied")
    seen_ready, seen_copied = g.sem("seen_ready"), g.sem("seen_copied")
    same_ready, same_cut = g.sem("same_ready"), g.sem("same_cut")
    pos_ready, pos_picked = g.sem("pos_ready"), g.sem("pos_picked")
    block_ready, gate, own = g.sem("edge_block_ready"), g.sem("scatter_gate"), g.sem("place_chain")
    hot_ready = g.sem("hot_slots_ready")
    placed = g.place_counts

    with nc.Block() as block:
        @block.tensor
        def _(pe):
            unsorted = pe.value_load(g.unsorted[0:1, 0:1], min_val=0, max_val=1)
            with pe.If(unsorted > 0):
                pe.matmul(ps_seen[:, 0:NB], g.ident[:], start[:], start=True, stop=True).then_inc(seen_ready, 1)

                def step(c, k, last=False):
                    hot, hot_col = hot_a[:, k, :], hot_b[:, k, :]
                    pe.wait_ge(turned_copied, c + 1)
                    pe.transpose(ps_hotT[:, k % 2, 0:P], hot, g.identb[:]).then_inc(turned, 1)
                    pe.wait_ge(turned_copied, c + 3)
                    pe.wait_ge(same_cut, c + 1)
                    pe.matmul(ps_same[:, k % 2, 0:P], hotT_b[:, k, :], hotT_b[:, k, :], start=True, stop=True)\
                      .then_inc(same_ready, 1)
                    pe.wait_ge(seen_copied, c + 1)
                    pe.wait_ge(pos_picked, c + 1)
                    pe.matmul(ps_pos[:, k % 2, 0:NB], hotT_f[:, k, :], seen[:, k, :], start=True, stop=False)
                    pe.wait_ge(same_cut, c + 3)
                    pe.matmul(ps_pos[:, k % 2, 0:NB], same[:, k, :], hot_col, start=False, stop=True)\
                      .then_inc(pos_ready, 1)
                    pe.matmul(ps_seen[:, 0:NB], hot, hot_col, start=False, stop=True,
                              skip_group_check=True).then_inc(seen_ready, 1)

                with pe.Fori(0, ROUNDS) as i:
                    pe.wait_ge(hot_ready, 2 * i + 2)
                    for k in range(U):
                        step(U * i + k, k)

        @block.scalar
        def _(act):
            unsorted = act.value_load(g.unsorted[0:1, 0:1], min_val=0, max_val=1)
            with act.If(unsorted > 0):
                act.preload_act_table(ACT.Copy)
                act.sem_inc(turned_copied, 2)
                with act.Fori(0, ROUNDS) as i:
                    for k in range(U):
                        act.wait_ge(placed[k].sem, placed[k].at(16 * i))
                    act.activation(row_slot[:], rows[:, ds(U * i, U), :], ACT.Copy).then_inc(block_ready, 1)
                    for k in range(U):
                        c = U * i + k
                        act.wait_ge(seen_ready, c + 1)
                        act.activation(seen[:, k, :], ps_seen[:, 0:NB], ACT.Copy).then_inc(seen_copied, 1)
                        act.wait_ge(turned, c + 1)
                        act.activation(hotT_b[:, k, :], ps_hotT[:, k % 2, 0:P], ACT.Copy)
                        act.activation(hotT_f[:, k, :], ps_hotT[:, k % 2, 0:P], ACT.Copy)\
                           .then_inc(turned_copied, 1)

        @block.vector
        def _(dve):
            unsorted = dve.value_load(g.unsorted[0:1, 0:1], min_val=0, max_val=1)
            with dve.If(unsorted > 0):
                dve.sem_inc(same_cut, 2)
                dve.sem_inc(pos_picked, 2)
                with dve.Fori(0, ROUNDS) as i:
                    dve.wait_ge(seen_ready, U * i + 1)
                    dve.tensor_tensor(hot_a[:], part_base[:, ds(U * i, U)].unsqueeze(2).broadcast_to([P, U, P]),
                                      g.node_base[:].unsqueeze(1).broadcast_to([P, U, P]), ALU.is_equal).then_inc(hot_ready, 1)
                    dve.tensor_tensor(hot_b[:], col[:, ds(U * i, U)].unsqueeze(2).broadcast_to([P, U, NB]),
                                      g.ramp[:, 0:NB].unsqueeze(1).broadcast_to([P, U, NB]), ALU.is_equal)\
                       .then_inc(hot_ready, 1)
                    dve.wait_ge(hot_ready, 2 * i + 2)
                    for k in range(U):
                        c = U * i + k
                        dve.wait_ge(same_ready, c + 1)
                        dve.tensor_tensor(same[:, k, :], ps_same[:, k % 2, 0:P], g.below[:], ALU.mult)\
                           .then_inc(same_cut, 1)
                        dve.wait_ge(pos_ready, c + 1)
                        dve.scalar_tensor_tensor(out=picked[:, k, :], in0=ps_pos[:, k % 2, 0:NB], scalar=0.0,
                                                 in1=hot_b[:, k, :],
                                                 op0=ALU.add, op1=ALU.mult, accum_out=pos_f[:, k:k + 1])\
                           .then_inc(pos_picked, 1)
                    for k in range(U):
                        dve.wait_ge(placed[k].sem, placed[k].at(16 * i))
                    dve.wait_ge(pos_picked, U * i + U + 2)
                    dve.tensor_copy(pos_i[:], pos_f[:]).then_inc(own, 1)

        @block.gpsimd
        def _(pool):
            unsorted = pool.value_load(g.unsorted[0:1, 0:1], min_val=0, max_val=1)
            with pool.If(unsorted > 0):
                with pool.Fori(0, ROUNDS) as i:
                    pool.wait_ge(own, i + 1)
                    pool.wait_ge(block_ready, i + 1)
                    pool.sem_inc(gate, 1)
                    for k in range(U):
                        pool.wait_ge(gate, 1)
                        pool.indirect_dma_start(
                            out=g.sorted_edges, out_offset=bass.IndirectOffsetOnAxis(ap=pos_i[:, k:k + 1], axis=0),
                            in_=row_slot[:, k, :], in_offset=None).then_inc(placed[k].sem, 16)
                for k in range(U):
                    pool.wait_ge(placed[k].sem, placed[k].at(16 * ROUNDS))


@staged
def edge_tables(g):
    nc = g.nc
    loaded, filled, ready, turned = (g.sem("sorted_loaded"), g.sem("tables_filled"),
                                     g.sem("tables_chain"), g.sem("cont_turned"))
    sorted_v = g.sorted_edges.rearrange("(p c) f -> p c f", p=P)
    with ExitStack() as ctx:
        goes_on = g.sb("goes_on", [P, 1], ctx=ctx)
        in_first, first_count = g.sb("in_first", [P, EC], ctx=ctx), g.sb("first_count", [P, 1], ctx=ctx)
        goes_on_row = g.sb("goes_on_row", [P, P], ctx=ctx)
        ps_cont = g.ps("cont", [P, 512], ctx=ctx)
        g.weights.allocate_turning(ctx)
        with nc.Block() as block:
            @block.sync
            def _(sp):
                sp.dma_start(g.edge_rows[:], sorted_v).then_inc(loaded, 16)
                sp.wait_ge(filled, 1)
                sp.dma_start(g.before[1:P, :], sorted_v[0:P - 1, EC - 1, DST:DST + 1],
                             allow_slow_non_contiguous=True).then_inc(loaded, 16)
                sp.wait_ge(loaded, 32)

            @block.vector
            def _(dve):
                ch = Chain(dve, ready)
                dve.memset(g.before[:], -1.0).then_inc(filled, 1)
                dve.wait_ge(loaded, 32)
                dst = g.edge_rows[:, :, DST]
                dve.memset(g.src_at[:, EC:], 0)
                dve.tensor_copy(g.src_at[:, 0:EC], g.edge_rows[:, :, SRC])
                dve.tensor_copy(g.dst_at[:], dst)
                ch.mark(dve.memset(g.keep[:, 0:1], 0.0))
                ch.mark(dve.tensor_tensor(g.keep[:, 1:EC], dst[:, 1:EC], dst[:, 0:EC - 1], ALU.is_equal))
                ch.link(dve.tensor_tensor(goes_on[:], dst[:, EC - 1:EC], g.before[:], ALU.is_equal))
                ch.mark(dve.tensor_scalar(g.keep_neg[:], g.keep[:], -1.0, BIG, ALU.add, ALU.mult))
                ch.mark(dve.tensor_scalar(goes_on_row[:], g.ones[:], goes_on[:, 0:1], None, ALU.mult))
                dve.tensor_scalar(g.goes_on_neg[:], goes_on[:], -1.0, BIG, ALU.add, ALU.mult)
                ch.mark(dve.tensor_scalar(in_first[:], dst, dst[:, 0:1], None, ALU.is_equal))
                ch.link(dve.tensor_tensor(g.carry_in_neg[:], dst[:, 0:1], g.before[:], ALU.is_equal))
                ch.mark(dve.tensor_reduce(first_count[:], in_first[:], AX.X, ALU.add))
                ch.link(dve.tensor_scalar(g.carry_in_neg[:], g.carry_in_neg[:], -1.0, BIG, ALU.add, ALU.mult))
                ch.link(dve.scalar_tensor_tensor(out=first_count[:], in0=first_count[:], scalar=-1.0,
                                                 in1=g.first_pos[:], op0=ALU.add, op1=ALU.add))
                dve.tensor_copy(g.first_end[:], first_count[:])
                dve.wait_ge(turned, 1)
                ch.link(dve.tensor_copy(g.cont[:], ps_cont[:, 0:P]))
                dve.tensor_scalar(g.cont_neg[:], g.cont[:], -1.0, BIG, ALU.add, ALU.mult)

            @block.tensor
            def _(pe):
                g.weights.turn(pe)
                pe.wait_ge(ready, 5)
                pe.matmul(ps_cont[:, 0:P], goes_on_row[:], g.ident[:], start=True, stop=True).then_inc(turned, 1)

            @block.scalar
            def _(act):
                g.weights.copy(act)


@staged
def normalise(g, name, src, out, scale=None, shift=None, add_to=None, table=None, have_moments=False):
    nc = g.nc
    own, stats_done, mean_ready, var_ready, std_ready, rstd_ready = (
        g.sem(name + "_chain"), g.sem(name + "_stats_done"), g.sem(name + "_mean"), g.sem(name + "_var"),
        g.sem(name + "_std"), g.sem(name + "_rstd"))
    centred, scaled, shifted, stored = (g.sem(name + "_centred"), g.sem(name + "_scaled"),
                                        g.sem(name + "_shifted"), g.sem(name + "_stored"))
    by_act = [b for b in range(NB) if b % 3 == 2]
    with ExitStack() as ctx:
        stats, moments = g.stats, g.moments
        neg_mean, var = g.sb(name + "_neg_mean", [P, NB], ctx=ctx), g.sb(name + "_variance", [P, NB], ctx=ctx)
        std, rstd = g.sb(name + "_stdev", [P, NB], ctx=ctx), g.sb(name + "_rstdev", [P, NB], ctx=ctx)
        with nc.Block() as block:
            @block.vector
            def _(dve):
                if not have_moments:
                    for b in range(NB + 2):
                        if b < NB:
                            dve.bn_stats(stats[:, b, :], src[:, b, :]).then_inc(stats_done, 1)
                        if b >= 2:
                            dve.wait_ge(stats_done, b - 1)
                            dve.bn_aggr(moments[:, b - 2, :], stats[:, b - 2, :]).then_inc(own, 1)
                    dve.wait_ge(own, NB)
                dve.tensor_scalar(var[:], moments[:, :, 1], EPS, None, ALU.add).then_inc(var_ready, 1)
                dve.tensor_scalar(neg_mean[:], moments[:, :, 0], -1.0, None, ALU.mult).then_inc(mean_ready, 1)
                dve.wait_ge(std_ready, 1)
                dve.reciprocal(rstd[:], std[:]).then_inc(rstd_ready, 1)
                dve.wait_ge(rstd_ready, 1)
                if scale is None:
                    for b in range(NB):
                        if b not in by_act:
                            dve.tensor_scalar(out[:, b, :], src[:, b, :], moments[:, b, 0:1], rstd[:, b:b + 1],
                                              ALU.subtract, ALU.mult)
                    return
                LAG = 3
                for b in range(NB + LAG):
                    if b < NB:
                        dve.wait_ge(centred, b + 1)
                        dve.scalar_tensor_tensor(out=out[:, b, :], in0=out[:, b, :], scalar=rstd[:, b:b + 1],
                                                 in1=scale, op0=ALU.mult, op1=ALU.mult).then_inc(scaled, 1)
                    if add_to is not None and b >= LAG:
                        dve.wait_ge(shifted, b - LAG + 1)
                        dve.tensor_tensor(add_to[:, b - LAG, :], add_to[:, b - LAG, :], out[:, b - LAG, :], ALU.add)

            @block.scalar
            def _(act):
                act.wait_ge(var_ready, 1)
                act.activation(std[:], var[:], ACT.Sqrt).then_inc(std_ready, 1)
                act.wait_ge(mean_ready, 1)
                for b in (by_act if scale is None else range(NB)):
                    act.activation(out[:, b, :], src[:, b, :], ACT.Identity, bias=neg_mean[:, b:b + 1], scale=1.0)\
                       .then_inc(centred, 1)
                if scale is None:
                    act.wait_ge(rstd_ready, 1)
                    for j, b in enumerate(by_act):
                        act.wait_ge(centred, j + 1)
                        act.activation(out[:, b, :], out[:, b, :], ACT.Copy, scale=rstd[:, b:b + 1])

            if scale is not None:
                @block.gpsimd
                def _(pool):
                    for b in range(NB):
                        pool.wait_ge(scaled, b + 1)
                        pool.tensor_tensor(out[:, b, :], out[:, b, :], shift, ALU.add).then_inc(shifted, 1)

            if table is not None:
                @block.sync
                def _(sp):
                    table_v = table.rearrange("(p b) f -> p b f", p=P)
                    R = 5
                    for b in range(0, NB, R):
                        sp.wait_ge(shifted, b + R)
                        sp.dma_start(table_v[:, b:b + R, :], out[:, b:b + R, :]).then_inc(stored, 16)
                    sp.wait_ge(stored, 16 * (NB // R))


@staged
def pool_max(g, name, table, states, x, weights, bias, product):
    nc = g.nc
    HALF = 7
    U = 2 * HALF
    ROUNDS = EC // U
    indices, reached, turned, carried = (g.sem(name + "_indices"), g.sem(name + "_reached"),
                                         g.sem(name + "_turned"), g.sem(name + "_carried"))
    x_turned, x_copied, x_multiplied, x_taken = (g.sem(name + "_x_turned"), g.sem(name + "_x_copied"),
                                                 g.sem(name + "_x_multiplied"), g.sem(name + "_x_taken"))
    gate = g.sem(name + "_gate")
    got = g.dma_counts[0:U]
    stored = g.store_counts
    states_v = states.rearrange("(p c) f -> p c f", p=P)
    with ExitStack() as ctx:
        index = g.sb(name + "_index", [P, U], I32, ctx)
        rows = g.sb(name + "_rows", [P, U, D], ctx=ctx)
        state = g.sb(name + "_state", [P, U, D], ctx=ctx)
        runs = g.sb(name + "_runs", [P, 2, P + 1], ctx=ctx)
        end_row = g.sb(name + "_end_row", [P, D], ctx=ctx)
        x_t = g.sb(name + "_x_t", [P, 2, D], ctx=ctx)
        ps_x = g.ps(name + "_x", [P, 2, 512], ctx=ctx)
        ps_y = g.ps(name + "_y", [P, 2, 512], ctx=ctx)
        ps_t = g.ps(name + "_t", [P, 512], ctx=ctx)
        ps_c = g.ps(name + "_c", [P, 512], ctx=ctx)
        with nc.Block() as block:
            @block.scalar
            def _(act):
                for b in range(NB):
                    act.wait_ge(x_turned, b + 1)
                    if b >= 2:
                        act.wait_ge(x_multiplied, b - 1)
                    act.copy(x_t[:, b % 2, :], ps_x[:, b % 2, 0:D]).then_inc(x_copied, 1)
                    act.wait_ge(x_multiplied, b + 1)
                    act.copy(product[:, b, :], ps_y[:, b % 2, 0:D]).then_inc(x_taken, 1)

            @block.gpsimd
            def _(pool):
                with pool.Fori(0, ROUNDS) as i:
                    for h in range(2):
                        pool.wait_ge(indices, 2 * i + h + 1)
                        pool.sem_inc(gate, 1)
                        for k in range(HALF * h, HALF * (h + 1)):
                            pool.wait_ge(gate, 1)
                            pool.indirect_dma_start(
                                out=rows[:, k, :], out_offset=None, in_=table,
                                in_offset=bass.IndirectOffsetOnAxis(ap=index[:, k:k + 1], axis=0)).then_inc(got[k].sem, 16)
                for q in stored:
                    pool.wait_ge(q.sem, q.at(16 * ROUNDS))
                ends = bass.IndirectOffsetOnAxis(ap=g.first_end[:], axis=0)
                pool.indirect_dma_start(out=end_row[:], out_offset=None, in_=states, in_offset=ends).then_inc(got[0].sem, 16)
                pool.wait_ge(carried, 2)
                pool.indirect_dma_start(out=states, out_offset=ends, in_=end_row[:], in_offset=None).then_inc(got[1].sem, 16)
                pool.wait_ge(got[1].sem, got[1].at(16 * ROUNDS + 16))

            @block.vector
            def _(dve):
                for h in range(2):
                    dve.tensor_copy(index[:, HALF * h:HALF * (h + 1)], g.src_at[:, HALF * h:HALF * (h + 1)])\
                       .then_inc(indices, 1)
                dve.memset(state[:, U - 1, :], -BIG).then_inc(reached, U)
                dve.memset(runs[:, :, 0:1], -BIG)
                with dve.Fori(0, ROUNDS) as i:
                    for k in range(U):
                        if k % HALF == 0:
                            dve.wait_ge(stored[k // HALF].sem, stored[k // HALF].at(16 * i))
                        dve.wait_ge(got[k].sem, got[k].at(16 * i + 16))
                        dve.wait_ge(reached, U * i + U + k)
                        dve.scalar_tensor_tensor(out=state[:, k, :], in0=state[:, (k - 1) % U, :],
                                                 scalar=g.keep_neg[:, ds(U * i + k, 1)], in1=rows[:, k, :],
                                                 op0=ALU.add, op1=ALU.max).then_inc(reached, 1)
                        if k % HALF == HALF - 1:
                            dve.wait_ge(reached, U * i + U + k + 1)
                            dve.tensor_copy(index[:, k - HALF + 1:k + 1], g.src_at[:, ds(U * i + U + k - HALF + 1, HALF)])\
                               .then_inc(indices, 1)
                dve.wait_ge(turned, 1)
                for j in range(2):
                    last = dve.tensor_tensor_scan(runs[:, j, 1:P + 1], g.cont_neg[:], ps_t[:, j * P:(j + 1) * P],
                                                  -BIG, ALU.add, ALU.max)
                last.then_inc(carried, 1)
                dve.wait_ge(turned, 2)
                dve.wait_ge(got[0].sem, got[0].at(16 * ROUNDS + 16))
                dve.scalar_tensor_tensor(out=end_row[:], in0=ps_c[:, 0:D], scalar=g.carry_in_neg[:, 0:1], in1=end_row[:],
                                         op0=ALU.add, op1=ALU.max).then_inc(carried, 1)

            @block.tensor
            def _(pe):
                def turn(b):
                    if b >= 2:
                        pe.wait_ge(x_copied, b - 1)
                    for j in range(2):
                        last = pe.transpose(ps_x[:, b % 2, j * P:(j + 1) * P], x[:, b, j * P:(j + 1) * P], g.ident[:])
                    last.then_inc(x_turned, 1)

                turn(0)
                for b in range(NB):
                    if b + 1 < NB:
                        turn(b + 1)
                    pe.wait_ge(x_copied, b + 1)
                    if b >= 2:
                        pe.wait_ge(x_taken, b - 1)
                    for j in range(2):
                        pe.matmul(ps_y[:, b % 2, 0:D], x_t[:, b % 2, j * P:(j + 1) * P], weights[:, j, :],
                                  start=(j == 0), stop=False)
                    pe.matmul(ps_y[:, b % 2, 0:D], g.ones[0:1, :], bias, start=False, stop=True).then_inc(x_multiplied, 1)
                pe.wait_ge(reached, U + EC)
                for j in range(2):
                    last = pe.transpose(ps_t[:, j * P:(j + 1) * P], state[:, U - 1, j * P:(j + 1) * P], g.ident[:])
                last.then_inc(turned, 1)
                pe.wait_ge(carried, 1)
                for j in range(2):
                    last = pe.transpose(ps_c[:, j * P:(j + 1) * P], runs[:, j, 0:P], g.ident[:])
                last.then_inc(turned, 1)

            @block.sync
            def _(sp):
                with sp.Fori(0, ROUNDS) as i:
                    for h in range(2):
                        sp.wait_ge(reached, U * i + U + HALF * (h + 1))
                        sp.dma_start(states_v[:, ds(U * i + HALF * h, HALF), :],
                                     state[:, HALF * h:HALF * (h + 1), :]).then_inc(stored[h].sem, 16)
                for h in range(2):
                    sp.wait_ge(stored[h].sem, stored[h].at(16 * ROUNDS))
    for q in got + stored:
        q.base += 16 * ROUNDS
    for q in got[0:2]:
        q.base += 16


@staged
def dense(g, name, x, weights, width, out, table=None, relu_bias=None, x_table=None):
    nc = g.nc
    R, BANKS = 5, 3
    turned, copied, multiplied, taken, finished, stored = (
        g.sem(name + "_turned"), g.sem(name + "_copied"), g.sem(name + "_multiplied"),
        g.sem(name + "_taken"), g.sem(name + "_finished"), g.sem(name + "_stored"))
    with ExitStack() as ctx:
        x_t = g.sb(name + "_x_t", [P, BANKS, D], ctx=ctx)
        ps_t = g.ps(name + "_t", [P, BANKS, 512], ctx=ctx)
        ps_y = g.ps(name + "_y", [P, BANKS, 512], ctx=ctx)
        with nc.Block() as block:
            @block.tensor
            def _(pe):
                def turn(b):
                    if b >= BANKS:
                        pe.wait_ge(copied, b - BANKS + 1)
                    for j in range(2):
                        last = pe.transpose(ps_t[:, b % BANKS, j * P:(j + 1) * P], x[:, b, j * P:(j + 1) * P], g.ident[:])
                    last.then_inc(turned, 1)

                turn(0)
                turn(1)
                for b in range(NB):
                    if b + 2 < NB:
                        turn(b + 2)
                    pe.wait_ge(copied, b + 1)
                    if b >= BANKS:
                        pe.wait_ge(taken, b - BANKS + 1)
                    y = ps_y[:, b % BANKS, 0:width]
                    for j in range(2):
                        last = pe.matmul(y, x_t[:, b % BANKS, j * P:(j + 1) * P], weights[:, j, :],
                                         start=(j == 0), stop=(j == 1))
                    last.then_inc(multiplied, 1)

            @block.scalar
            def _(act):
                for b in range(NB):
                    act.wait_ge(turned, b + 1)
                    if b >= BANKS:
                        act.wait_ge(multiplied, b - BANKS + 1)
                    act.copy(x_t[:, b % BANKS, :], ps_t[:, b % BANKS, 0:D]).then_inc(copied, 1)

            @block.vector
            def _(dve):
                for b in range(NB + 1):
                    if b < NB:
                        dve.wait_ge(multiplied, b + 1)
                        y = ps_y[:, b % BANKS, 0:width]
                        if relu_bias is not None:
                            dve.tensor_tensor(out[:, b, :], y, relu_bias, ALU.add).then_inc(taken, 1)
                        else:
                            dve.tensor_copy(out[:, b, :], y).then_inc(taken, 1)
                    if relu_bias is not None and b >= 1:
                        dve.wait_ge(taken, b)
                        dve.tensor_scalar(out[:, b - 1, :], out[:, b - 1, :], 0.0, None, ALU.max).then_inc(finished, 1)

            if table is not None:
                @block.sync
                def _(sp):
                    table_v = table.rearrange("(p b) f -> p b f", p=P)
                    for b in range(0, NB, R):
                        sp.wait_ge(finished if relu_bias is not None else taken, b + R)
                        sp.dma_start(table_v[:, b:b + R, :], out[:, b:b + R, :]).then_inc(stored, 16)
                    sp.wait_ge(stored, 16 * (NB // R))

            if x_table is not None:
                @block.sync
                def _(sp):
                    sp.dma_start(x_table.rearrange("(p b) f -> p b f", p=P), x[:]).then_inc(stored, 16)
                    sp.wait_ge(stored, 16)


@staged
def mix(g, name, states, weights, product, x, out, table=None, moments=False):
    nc = g.nc
    R, BANKS = 5, 3
    SLOTS = 2 * R
    pool_in, turned, copied, multiplied, added, finished, stored = (
        g.sem(name + "_pool_in"), g.sem(name + "_turned"), g.sem(name + "_copied"), g.sem(name + "_multiplied"),
        g.sem(name + "_added"), g.sem(name + "_finished"), g.sem(name + "_stored"))
    stats_done = g.sem(name + "_stats_done")
    got = g.dma_counts[0:SLOTS]
    with ExitStack() as ctx:
        sb = lambda n, s, d=F32: g.sb(name + "_" + n, s, d, ctx)
        last_row, best = sb("last_row", [P, SLOTS, D]), sb("best", [P, R, D])
        p_t = sb("p_t", [P, BANKS, D])
        ps_t = g.ps(name + "_t", [P, BANKS, 512], ctx=ctx)
        ps_y = g.ps(name + "_y", [P, BANKS, 512], ctx=ctx)
        with nc.Block() as block:
            @block.gpsimd
            def _(pool):
                for b in range(NB):
                    k = b % SLOTS
                    if b >= SLOTS:
                        pool.wait_ge(pool_in, b - SLOTS + 1)
                    pool.indirect_dma_start(
                        out=last_row[:, k, :], out_offset=None, in_=states,
                        in_offset=bass.IndirectOffsetOnAxis(ap=g.last_at[:, b:b + 1], axis=0)).then_inc(got[k].sem, 16)

            @block.vector
            def _(dve):
                for t in range(NB + 8):
                    b = t
                    if b < NB:
                        k = b % SLOTS
                        dve.wait_ge(got[k].sem, got[k].at(16 * (b // SLOTS + 1)))
                        if b >= R:
                            dve.wait_ge(turned, b - R + 1)
                        dve.tensor_scalar(best[:, b % R, :], last_row[:, b % SLOTS, :], g.has_edge[:, b:b + 1], None,
                                          ALU.mult).then_inc(pool_in, 1)
                    b = t - 4
                    if 0 <= b < NB:
                        dve.wait_ge(multiplied, b + 1)
                        dve.tensor_tensor(product[:, b, :], product[:, b, :], ps_y[:, b % BANKS, 0:D], ALU.add)\
                           .then_inc(added, 1)
                    b = t - 5
                    if 0 <= b < NB:
                        dve.wait_ge(added, b + 1)
                        if x is None:
                            dve.tensor_scalar(out[:, b, :], product[:, b, :], 0.0, None, ALU.max).then_inc(finished, 1)
                        else:
                            dve.scalar_tensor_tensor(out=out[:, b, :], in0=product[:, b, :], scalar=0.0,
                                                     in1=x[:, b, :], op0=ALU.max, op1=ALU.add).then_inc(finished, 1)
                    b = t - 6
                    if moments and 0 <= b < NB:
                        dve.wait_ge(finished, b + 1)
                        dve.bn_stats(g.stats[:, b, :], out[:, b, :]).then_inc(stats_done, 1)
                    b = t - 7
                    if moments and 0 <= b < NB:
                        dve.wait_ge(stats_done, b + 1)
                        dve.bn_aggr(g.moments[:, b, :], g.stats[:, b, :])

            @block.tensor
            def _(pe):
                def turn(b):
                    if b >= BANKS:
                        pe.wait_ge(copied, b - BANKS + 1)
                    pe.wait_ge(pool_in, b + 1)
                    for j in range(2):
                        last = pe.transpose(ps_t[:, b % BANKS, j * P:(j + 1) * P], best[:, b % R, j * P:(j + 1) * P], g.ident[:])
                    last.then_inc(turned, 1)

                turn(0)
                turn(1)
                for b in range(NB):
                    if b + 2 < NB:
                        turn(b + 2)
                    pe.wait_ge(copied, b + 1)
                    if b >= BANKS:
                        pe.wait_ge(added, b - BANKS + 1)
                    for j in range(2):
                        last = pe.matmul(ps_y[:, b % BANKS, 0:D], p_t[:, b % BANKS, j * P:(j + 1) * P], weights[:, j, :],
                                         start=(j == 0), stop=(j == 1))
                    last.then_inc(multiplied, 1)

            @block.scalar
            def _(act):
                for b in range(NB):
                    act.wait_ge(turned, b + 1)
                    if b >= BANKS:
                        act.wait_ge(multiplied, b - BANKS + 1)
                    act.copy(p_t[:, b % BANKS, :], ps_t[:, b % BANKS, 0:D]).then_inc(copied, 1)

            if table is not None:
                @block.sync
                def _(sp):
                    table_v = table.rearrange("(p b) f -> p b f", p=P)
                    for b in range(0, NB, R):
                        sp.wait_ge(finished, b + R)
                        sp.dma_start(table_v[:, b:b + R, :], out[:, b:b + R, :]).then_inc(stored, 16)
                    sp.wait_ge(stored, 16 * (NB // R))
    for k, q in enumerate(got):
        q.base += 16 * len(range(k, NB, SLOTS))


@staged
def attention_scan(g, name, table, states):
    nc = g.nc
    G = 4
    U = 2 * G
    ROUNDS = EC // U
    W = D + 2 * H
    A = D + H
    indices, edges_in, edges_turned, edges_ready, encoded = (
        g.sem(name + "_indices"), g.sem(name + "_edges_in"), g.sem(name + "_edges_turned"),
        g.sem(name + "_edges_ready"), g.sem(name + "_encoded"))
    weighed, scored, kept_in, exps, used = (g.sem(name + "_weighed"), g.sem(name + "_scored"), g.sem(name + "_kept"),
                                            g.sem(name + "_exps"), g.sem(name + "_used"))
    score_chain, state_chain, gate, turn_gate = (g.sem(name + "_score_chain"), g.sem(name + "_state_chain"),
                                                 g.sem(name + "_gate"), g.sem(name + "_turn_gate"))
    to_dve, to_pe, to_act, to_pool = (g.sem(name + "_to_dve"), g.sem(name + "_to_pe"), g.sem(name + "_to_act"),
                                      g.sem(name + "_to_pool"))
    got = g.dma_counts[0:U]
    stored = g.store_counts
    states_v = states.rearrange("(p c) f -> p c f", p=P)
    blocks = [(0, P), (P, P), (2 * P, A - 2 * P)]
    with ExitStack() as ctx:
        sb = lambda n, s, d=F32: g.sb(name + "_" + n, s, d, ctx)
        src_slot, dst_slot = sb("src_slot", [P, U], I32), sb("dst_slot", [P, U], I32)
        at_dst, at_src = sb("at_dst", [P, U, W]), sb("at_src", [P, U, W])
        edge_group, group_t = sb("edge_group", [P, U * EF]), sb("group_t", [U * EF, P])
        prod, prod_sum = sb("prod", [P, G, D]), sb("prod_sum", [P, G * H])
        score = sb("score", [P, G, H])
        top = sb("top", [P, 2, G + 1, H])
        args = sb("args", [P, 2, 2, G, H])
        decay = sb("decay", [P, 2, G, H])
        kept = sb("kept", [P, 2, G, D])
        part = sb("part", [P, 2, G * H, HD + 1])
        faded = sb("faded", [P, H, HD + 1])
        state = sb("state", [P, U, W])
        top_runs, runs = sb("top_runs", [H, P + 1]), sb("runs", [P, 3, P + 1])
        tops, end_args, end_exps = sb("tops", [P, 2, H]), sb("end_args", [P, 2, H]), sb("end_exps", [P, 2, H])
        end_state, end_decay = sb("end_state", [P, A]), sb("end_decay", [P, A])
        decay_t = sb("decay_t", [P, 3, P])
        end_row = sb("end_row", [P, W])
        join_args, join_exps, carry_top, both_top = (sb("join_args", [P, 2, H]), sb("join_exps", [P, 2, H]),
                                                     sb("carry_top", [P, H]), sb("both_top", [P, H]))
        ps_g = g.ps(name + "_g", [P, 512], ctx=ctx)
        ps_e = g.ps(name + "_e", [P, U, D], ctx=ctx)
        ps_a, ps_b, ps_c = (g.ps(name + n, [P, 512], ctx=ctx) for n in ("_a", "_b", "_c"))
        by_head = lambda ap: ap.rearrange("p (h d) -> p h d", h=H)
        with nc.Block() as block:
            @block.scalar
            def _(act):
                act.preload_act_table(ACT.Exp)
                act.sem_inc(edges_ready, 1)
                act.sem_inc(kept_in, 2)
                act.sem_inc(exps, 2)

                def send_indices(i, h):
                    act.wait_ge(weighed, 2 * i + h + 1)
                    act.wait_ge(kept_in, 2 * i + h + 1)
                    cols = slice(G * h, G * (h + 1))
                    act.copy(src_slot[:, cols], g.src_at[:, ds(U * i + G * h, G)])
                    act.copy(dst_slot[:, cols], g.dst_at[:, ds(U * i + G * h, G)]).then_inc(indices, 1)

                def send_edges(i):
                    act.wait_ge(edges_turned, i + 1)
                    act.copy(edge_group[:], g.edge_rows[:, ds(U * i, U), :].rearrange("p c f -> p (c f)"))\
                       .then_inc(edges_in, 1)
                    act.wait_ge(edges_turned, i + 2)
                    act.wait_ge(encoded, 2 * i + 1)
                    act.copy(group_t[:], ps_g[0:U * EF, 0:P]).then_inc(edges_ready, 1)

                def keep(i, h):
                    n = 2 * i + h
                    act.wait_ge(used, n + 1)
                    for k in range(G * h, G * (h + 1)):
                        act.wait_ge(got[k].sem, got[k].at(32 * i + 32))
                    act.copy(kept[:, h, :, :], at_src[:, G * h:G * (h + 1), 0:D]).then_inc(kept_in, 1)

                def exponentials(i, h):
                    act.wait_ge(scored, 2 * i + h + 3)
                    act.activation(part[:, h, :, HD], args[:, h, 0, :, :].rearrange("p g h -> p (g h)"), ACT.Exp)
                    act.activation(decay[:, h, :, :], args[:, h, 1, :, :], ACT.Exp).then_inc(exps, 1)

                send_indices(0, 0)
                send_edges(0)
                send_indices(0, 1)
                with act.Fori(0, ROUNDS - 1) as i:
                    for h in range(2):
                        keep(i, h)
                        send_indices(i + 1, h)
                        exponentials(i, h)
                        if h == 0:
                            send_edges(i + 1)
                for h in range(2):
                    keep(ROUNDS - 1, h)
                    exponentials(ROUNDS - 1, h)
                act.wait_ge(to_act, 1)
                act.activation(end_exps[:], end_args[:], ACT.Exp).then_inc(to_dve, 1)
                act.wait_ge(to_act, 2)
                for j, (_, n) in enumerate(blocks):
                    last = act.copy(decay_t[0:n, j, :], ps_b[0:n, j * P:(j + 1) * P])
                last.then_inc(to_dve, 1)
                act.wait_ge(to_act, 3)
                act.activation(join_exps[:], join_args[:], ACT.Exp).then_inc(to_dve, 1)

            @block.gpsimd
            def _(pool):
                with pool.Fori(0, ROUNDS) as i:
                    for h in range(2):
                        pool.wait_ge(indices, 2 * i + h + 1)
                        pool.sem_inc(gate, 1)
                        for k in range(G * h, G * (h + 1)):
                            for rows, slot in ((at_dst, dst_slot), (at_src, src_slot)):
                                pool.wait_ge(gate, 1)
                                pool.indirect_dma_start(
                                    out=rows[:, k, :], out_offset=None, in_=table,
                                    in_offset=bass.IndirectOffsetOnAxis(ap=slot[:, k:k + 1], axis=0))\
                                    .then_inc(got[k].sem, 16)
                for q in stored:
                    pool.wait_ge(q.sem, q.at(16 * ROUNDS))
                ends = bass.IndirectOffsetOnAxis(ap=g.first_end[:], axis=0)
                pool.indirect_dma_start(out=end_row[:], out_offset=None, in_=states, in_offset=ends).then_inc(got[0].sem, 16)
                pool.wait_ge(to_pool, 1)
                pool.indirect_dma_start(out=states, out_offset=ends, in_=end_row[:], in_offset=None).then_inc(got[1].sem, 16)
                pool.wait_ge(got[1].sem, got[1].at(32 * ROUNDS + 16))

            @block.tensor
            def _(pe):
                pe.sem_inc(edges_turned, 1)
                pe.sem_inc(encoded, 1)
                with pe.Fori(0, ROUNDS) as i:
                    pe.wait_ge(edges_in, i + 1)
                    pe.wait_ge(edges_ready, i + 1)
                    pe.sem_inc(turn_gate, 1)
                    pe.wait_ge(turn_gate, 1)
                    pe.transpose(ps_g[0:U * EF, 0:P], edge_group[:], g.ident[:]).then_inc(edges_turned, 1)
                    pe.wait_ge(edges_ready, i + 2)
                    for h in range(2):
                        pe.wait_ge(weighed, 2 * i + h + 1)
                        for k in range(G * h, G * (h + 1), 2):
                            last = pe.matmul(ps_e[:, k:k + 2, :].rearrange("p a f -> p (a f)"), group_t[:],
                                             g.encode[:, k:k + 2, :].rearrange("p a f -> p (a f)"),
                                             start=True, stop=True)
                        last.then_inc(encoded, 1)
                pe.wait_ge(used, 2 * ROUNDS + 2)
                pe.wait_ge(edges_ready, ROUNDS + 1)
                pe.transpose(ps_g[0:H, 0:P], top[:, 1, G, :], g.ident[:]).then_inc(to_dve, 1)
                pe.wait_ge(to_pe, 1)
                pe.transpose(ps_c[:, 0:H], top_runs[:, 0:P], g.ident[0:H, 0:H])
                pe.transpose(ps_c[:, H:2 * H], top_runs[:, 1:P + 1], g.ident[0:H, 0:H]).then_inc(to_dve, 1)
                pe.wait_ge(to_pe, 2)
                for j, (at, n) in enumerate(blocks):
                    last = pe.transpose(ps_b[0:n, j * P:(j + 1) * P], end_decay[:, at:at + n], g.ident[:])
                last.then_inc(to_act, 1)
                for j, (at, n) in enumerate(blocks):
                    last = pe.transpose(ps_a[0:n, j * P:(j + 1) * P], end_state[:, at:at + n], g.ident[:])
                last.then_inc(to_dve, 1)
                pe.wait_ge(to_pe, 3)
                for j, (at, n) in enumerate(blocks):
                    last = pe.transpose(ps_c[:, at:at + n], runs[0:n, j, 0:P], g.ident[0:n, 0:n])
                last.then_inc(to_dve, 1)

            @block.vector
            def _(dve):
                for sem in (weighed, scored, used):
                    dve.sem_inc(sem, 2)
                SCORE_STEPS, STATE_STEPS = 8 + G, 2 + 2 * G

                def score_and_state(new, old):
                    if new:
                        i, h = new
                        n = 2 * i + h
                        cols = slice(G * h, G * (h + 1))
                        at = ds(U * i + G * h, G)
                        ch = Chain(dve, score_chain, SCORE_STEPS * n + 1)
                        flat = score[:].rearrange("p c h -> p (c h)")
                        for k in range(G * h, G * (h + 1)):
                            dve.wait_ge(got[k].sem, got[k].at(32 * i + 32))
                        dve.wait_ge(encoded, n + 2)
                        ch.mark(dve.tensor_tensor(score[:], at_dst[:, cols, D + H:W], at_src[:, cols, D:D + H], ALU.add))
                        dve.scalar_tensor_tensor(out=prod[:], in0=ps_e[:, cols, :], scalar=0.0,
                                                 in1=at_dst[:, cols, 0:D], op0=ALU.max, op1=ALU.mult).then_inc(weighed, 1)
                    if old:
                        oi, oh = old
                        on = 2 * oi + oh
                        och = Chain(dve, state_chain, STATE_STEPS * on + 1)
                        dve.wait_ge(kept_in, on + 3)
                        dve.wait_ge(exps, on + 3)
                        och.mark(dve.tensor_tensor(part[:, oh, :, 0:HD],
                                                   kept[:, oh, :, :].rearrange("p g (h d) -> p (g h) d", h=H),
                                                   part[:, oh, :, HD:HD + 1].broadcast_to([P, G * H, HD]), ALU.mult))
                        dve.wait_ge(stored[oh].sem, stored[oh].at(16 * oi))
                        och.mark(dve.tensor_copy(state[:, G * oh:G * (oh + 1), A:W], top[:, oh, 1:G + 1, :]))
                    if new:
                        dve.wait_ge(weighed, n + 3)
                        ch.mark(dve.tensor_reduce(prod_sum[:], prod[:].rearrange("p c (h d) -> p (c h) d", h=H),
                                                  AX.X, ALU.add))
                    for step in range(2 * G):
                        if old:
                            j = step // 2
                            k = G * oh + j
                            och.sync()
                            if step % 2 == 0:
                                och.mark(dve.tensor_tensor(faded[:], by_head(state[:, (k - 1) % U, 0:A]),
                                                           decay[:, oh, j, :].unsqueeze(2)
                                                           .broadcast_to([P, H, HD + 1]), ALU.mult))
                            else:
                                och.mark(dve.tensor_tensor(by_head(state[:, k, 0:A]), faded[:],
                                                           part[:, oh, H * j:H * (j + 1), :], ALU.add))
                        if new:
                            ch.sync()
                            if step == 0:
                                ch.mark(dve.tensor_tensor(flat, flat, prod_sum[:], ALU.add))
                            elif step == 1:
                                ch.mark(dve.scalar_tensor_tensor(out=flat, in0=flat, scalar=0.2, in1=flat,
                                                                 op0=ALU.mult, op1=ALU.max))
                            elif step < G + 2:
                                k = step - 2
                                ch.mark(dve.scalar_tensor_tensor(out=top[:, h, k + 1, :], in0=top[:, h, k, :],
                                                                 scalar=g.keep_neg[:, ds(U * i + G * h + k, 1)],
                                                                 in1=score[:, k, :], op0=ALU.add, op1=ALU.max))
                            elif step == G + 2:
                                dve.wait_ge(exps, n + 1)
                                ch.mark(dve.tensor_tensor(args[:, h, 0, :, :], score[:], top[:, h, 1:G + 1, :], ALU.subtract))
                                ch.mark(dve.tensor_tensor(args[:, h, 1, :, :], top[:, h, 0:G, :],
                                                          g.keep_neg[:, at].unsqueeze(2).broadcast_to([P, G, H]), ALU.add))
                                ch.mark(dve.tensor_copy(top[:, 1 - h, 0, :], top[:, h, G, :]))
                            else:
                                ch.mark(dve.tensor_tensor(args[:, h, 1, :, :], args[:, h, 1, :, :], top[:, h, 1:G + 1, :],
                                                          ALU.subtract))
                    if new:
                        ch.sync()
                        dve.sem_inc(scored, 1)
                    if old:
                        och.sync()
                        dve.sem_inc(used, 1)

                ch = Chain(dve, score_chain)
                ch.link(dve.memset(top[:, 0, 0, :], -BIG))
                ch = Chain(dve, state_chain)
                ch.link(dve.memset(state[:, U - 1, 0:A], 0.0))
                dve.memset(top_runs[:, 0:1], -BIG)
                dve.memset(runs[:, :, 0:1], 0.0)
                score_and_state((0, 0), None)
                with dve.Fori(0, ROUNDS - 1) as i:
                    score_and_state((i, 1), (i, 0))
                    score_and_state((i + 1, 0), (i, 1))
                score_and_state((ROUNDS - 1, 1), (ROUNDS - 1, 0))
                score_and_state(None, (ROUNDS - 1, 1))

                ch = Chain(dve, state_chain, STATE_STEPS * 2 * ROUNDS + 1)
                dve.wait_ge(to_dve, 1)
                dve.tensor_tensor_scan(top_runs[:, 1:P + 1], g.cont_neg[0:H, :], ps_g[0:H, 0:P], -BIG, ALU.add, ALU.max)\
                   .then_inc(to_pe, 1)
                dve.wait_ge(to_dve, 2)
                ch.link(dve.tensor_copy(tops[:], ps_c[:, 0:2 * H].rearrange("p (a h) -> p a h", a=2)))
                ch.mark(dve.tensor_tensor(end_args[:, 0, :], top[:, 1, G, :], tops[:, 1, :], ALU.subtract))
                ch.link(dve.scalar_tensor_tensor(out=end_args[:, 1, :], in0=tops[:, 0, :], scalar=g.goes_on_neg[:, 0:1],
                                                 in1=tops[:, 1, :], op0=ALU.add, op1=ALU.subtract))
                dve.sem_inc(to_act, 1)
                dve.wait_ge(to_dve, 3)
                factor = lambda j: end_exps[:, j, :].unsqueeze(2).broadcast_to([P, H, HD + 1])
                ch.mark(dve.tensor_tensor(by_head(end_state[:]), by_head(state[:, U - 1, 0:A]), factor(0), ALU.mult))
                ch.link(dve.tensor_copy(by_head(end_decay[:]), factor(1)))
                dve.sem_inc(to_pe, 1)
                dve.wait_ge(to_dve, 5)
                for j, (_, n) in enumerate(blocks):
                    last = dve.tensor_tensor_scan(runs[0:n, j, 1:P + 1], decay_t[0:n, j, :], ps_a[0:n, j * P:(j + 1) * P],
                                                  0.0, ALU.mult, ALU.add)
                last.then_inc(to_pe, 1)
                dve.wait_ge(got[0].sem, got[0].at(32 * ROUNDS + 16))
                ch.link(dve.tensor_scalar(carry_top[:], tops[:, 0, :], g.carry_in_neg[:, 0:1], None, ALU.add))
                ch.link(dve.tensor_tensor(both_top[:], carry_top[:], end_row[:, A:W], ALU.max))
                ch.mark(dve.tensor_tensor(join_args[:, 0, :], end_row[:, A:W], both_top[:], ALU.subtract))
                ch.mark(dve.tensor_tensor(join_args[:, 1, :], carry_top[:], both_top[:], ALU.subtract))
                ch.sync()
                dve.sem_inc(to_act, 1)
                dve.wait_ge(to_dve, 7)
                join = lambda j: join_exps[:, j, :].unsqueeze(2).broadcast_to([P, H, HD + 1])
                ch.mark(dve.tensor_copy(end_row[:, A:W], both_top[:]))
                ch.mark(dve.tensor_tensor(by_head(end_row[:, 0:A]), by_head(end_row[:, 0:A]), join(0), ALU.mult))
                ch.link(dve.tensor_tensor(by_head(end_state[:]), by_head(ps_c[:, 0:A]), join(1), ALU.mult))
                ch.link(dve.tensor_tensor(end_row[:, 0:A], end_row[:, 0:A], end_state[:], ALU.add))
                dve.sem_inc(to_pool, 1)

            @block.sync
            def _(sp):
                with sp.Fori(0, ROUNDS) as i:
                    for h in range(2):
                        sp.wait_ge(used, 2 * i + h + 3)
                        sp.dma_start(states_v[:, ds(U * i + G * h, G), :],
                                     state[:, G * h:G * (h + 1), :]).then_inc(stored[h].sem, 16)
                for h in range(2):
                    sp.wait_ge(stored[h].sem, stored[h].at(16 * ROUNDS))
    for q in got:
        q.base += 32 * ROUNDS
    for q in got[0:2]:
        q.base += 16
    for q in stored:
        q.base += 16 * ROUNDS


@staged
def attend(g, name, states, x, bias):
    nc = g.nc
    R = 5
    A, W = D + H, D + 2 * H
    own, used = g.sem(name + "_chain"), g.sem(name + "_used")
    got = g.dma_counts[0:2 * R]
    with ExitStack() as ctx:
        sb = lambda n, s, d=F32: g.sb(name + "_" + n, s, d, ctx)
        row, share = sb("row", [P, 2, R, W]), sb("share", [P, R, D])
        factor = sb("factor", [P, R, H])
        by_head = lambda ap: ap.rearrange("p r (h d) -> p r h d", h=H)
        with nc.Block() as block:
            @block.gpsimd
            def _(pool):
                for b in range(NB):
                    i, k = b // R, b % R
                    if i >= 2 and k == 0:
                        pool.wait_ge(used, i - 1)
                    pool.indirect_dma_start(
                        out=row[:, i % 2, k, :], out_offset=None, in_=states,
                        in_offset=bass.IndirectOffsetOnAxis(ap=g.last_at[:, b:b + 1], axis=0))\
                        .then_inc(got[b % (2 * R)].sem, 16)

            @block.vector
            def _(dve):
                ch = Chain(dve, own)
                ch.link(dve.tensor_tensor(x[:], x[:], bias.unsqueeze(1).broadcast_to([P, NB, D]), ALU.add))
                for i in range(NB // R):
                    cols = slice(R * i, R * (i + 1))
                    state = by_head(row[:, i % 2, :, 0:A])
                    for k in range(R):
                        q = got[(R * i + k) % (2 * R)]
                        dve.wait_ge(q.sem, q.at(16 * (i // 2 + 1)))
                    ch.link(dve.tensor_scalar(factor[:], state[:, :, :, HD], 1e-10, None, ALU.max))
                    ch.link(dve.reciprocal(factor[:], factor[:]))
                    ch.link(dve.tensor_tensor(factor[:], factor[:], g.has_edge[:, cols].unsqueeze(2)
                                              .broadcast_to([P, R, H]), ALU.mult))
                    ch.link(dve.tensor_tensor(by_head(share[:]), state[:, :, :, 0:HD],
                                              factor[:].unsqueeze(3).broadcast_to([P, R, H, HD]), ALU.mult))
                    dve.sem_inc(used, 1)
                    ch.link(dve.tensor_tensor(x[:, cols, :], x[:, cols, :], share[:], ALU.add))
    for k, q in enumerate(got):
        q.base += 16 * len(range(k, NB, 2 * R))


class Mixture:

    def __init__(self, g, name, experts, hidden, gated):
        self.name, self.experts, self.hidden, self.gated = name, experts, hidden, gated
        self.pairs = 2 * NB
        tiles = (P * self.pairs + experts * (P - 1)) // P
        self.tiles = tiles + tiles % 2
        self.nothing = None
        self.x_table = g.dram(name + "_x_table", [NPAD, D])
        self.rows_out = g.dram(name + "_rows_out", [self.tiles * P, D])


@staged
def route(g, m, logits, biases):
    nc = g.nc
    n, X, C = m.name, m.experts, m.pairs
    m.row = g.sb(n + "_row", [P, C], I32, m.ctx)
    m.weight = g.sb(n + "_weight", [P, C], ctx=m.ctx)
    m.tile_expert = g.sb(n + "_tile_expert", [P, m.tiles], I32, m.ctx)
    m.tile_load = g.sb(n + "_tile_load", [P, m.tiles], I32, m.ctx)
    m.node = g.sb(n + "_node", [P, m.tiles], I32, m.ctx)
    if biases:
        HC = m.hidden // P
        m.b1 = g.sb(n + "_b1", [P, X, HC], ctx=m.ctx)
        m.b2 = g.sb(n + "_b2", [P, X, D], ctx=m.ctx)
        biases_loaded, biases_turned = g.sem("biases_loaded"), g.sem("biases_turned")
    placed_ready, node_ready = g.sem(n + "_placed_ready"), g.sem(n + "_node_ready")
    own, gap_ready, exp_ready, summed, totals = (g.sem(n + "_chain"), g.sem(n + "_gap"), g.sem(n + "_exp"),
                                                 g.sem(n + "_summed"), g.sem(n + "_totals"))
    with ExitStack() as ctx:
        sb = lambda k, s, d=F32: g.sb(n + "_" + k, s, d, ctx)
        best, which = sb("best", [P, NB, 8]), sb("which", [P, NB, 8], U32)
        chosen, hot, upto = sb("chosen", [P, NB, 2]), sb("hot", [P, C, X]), sb("upto", [P, C, X])
        gap, total = sb("gap", [P, NB]), sb("total", [P, NB])
        across, expert_sum = sb("across", [P, X]), sb("expert_sum", [P, X])
        tiles_of, tiles_upto, base = sb("tiles_of", [P, X]), sb("tiles_upto", [P, X]), sb("base", [P, X])
        row_f, passed, tile_f = sb("row_f", [P, C]), sb("passed", [P, m.tiles, X]), sb("tile_f", [P, m.tiles])
        repeat = sb("repeat", [P, m.tiles])
        tile_of, in_tile, place_tmp = sb("tile_of", [P, C]), sb("in_tile", [P, C]), sb("place_tmp", [P, C])
        hot_in, hot_tile = sb("hot_in", [P, C, P], BF16), sb("hot_tile", [P, C, m.tiles], BF16)
        node_parts, node_f = sb("node_parts", [P, C, 2, m.tiles], BF16), sb("node_f", [P, m.tiles])
        ps = g.ps(n + "_route", [P, 2, 512], ctx=ctx)
        ps_node = g.ps(n + "_node", [P, 512], ctx=ctx)
        if biases:
            raw_b1 = sb("b1_raw", [X, m.hidden])
            ps_b1 = g.ps(n + "_b1", [P, 512], ctx=ctx)
        with nc.Block() as block:
            @block.vector
            def _(dve):
                ch = Chain(dve, own)
                ch.link(dve.tensor_tensor(logits[:], logits[:], g.wide[n][:].unsqueeze(1).broadcast_to([P, NB, X]), ALU.add))
                for b in range(NB):
                    ch.mark(dve.max(best[:, b, :], logits[:, b, 0:X]))
                dve.wait_ge(own, ch.n)
                for b in range(NB):
                    ch.mark(dve.max_index(which[:, b, :], best[:, b, :], logits[:, b, 0:X]))
                dve.tensor_tensor(gap[:], best[:, :, 1], best[:, :, 0], ALU.subtract).then_inc(gap_ready, 1)
                dve.wait_ge(own, ch.n)
                ch.link(dve.tensor_copy(chosen[:], which[:, :, 0:2]))
                ch.link(dve.tensor_tensor(hot[:], chosen[:].rearrange("p b j -> p (b j)").unsqueeze(2).broadcast_to([P, C, X]),
                                          g.ramp[:, 0:X].unsqueeze(1).broadcast_to([P, C, X]), ALU.is_equal))
                for e in range(X):
                    ch.mark(dve.tensor_tensor_scan(upto[:, :, e], g.ones[:, 0:C], hot[:, :, e], 0.0, ALU.mult, ALU.add))
                dve.wait_ge(own, ch.n)
                dve.tensor_copy(expert_sum[:], upto[:, C - 1, :]).then_inc(summed, 1)
                dve.wait_ge(exp_ready, 1)
                ch.link(dve.tensor_scalar(total[:], gap[:], 1.0, None, ALU.add))
                ch.link(dve.reciprocal(total[:], total[:]))
                pair = m.weight[:].rearrange("p (b j) -> p b j", j=2)
                dve.tensor_copy(pair[:, :, 0], total[:])
                dve.tensor_tensor(pair[:, :, 1], gap[:], total[:], ALU.mult)
                dve.wait_ge(totals, 1)
                ch.mark(dve.tensor_copy(across[:], ps[:, 0, 0:X]))
                ch.link(dve.tensor_scalar(expert_sum[:], ps[:, 1, 0:X], float(P - 1), None, ALU.add))
                floor_div(ch, dve, tiles_of[:], expert_sum[:], P, base[:])
                ch.link(dve.tensor_tensor_scan(tiles_upto[:], g.ones[:, 0:X], tiles_of[:], 0.0, ALU.mult, ALU.add))
                ch.link(dve.tensor_tensor(base[:], tiles_upto[:], tiles_of[:], ALU.subtract))
                ch.link(dve.scalar_tensor_tensor(out=base[:], in0=base[:], scalar=float(P), in1=across[:],
                                                 op0=ALU.mult, op1=ALU.add))
                ch.link(dve.tensor_tensor(upto[:], upto[:], base[:].unsqueeze(1).broadcast_to([P, C, X]), ALU.add))
                ch.link(dve.tensor_tensor(upto[:], upto[:], hot[:], ALU.mult))
                ch.link(dve.tensor_reduce(row_f[:], upto[:], AX.X, ALU.add))
                ch.link(dve.tensor_scalar(row_f[:], row_f[:], -1.0, None, ALU.add))
                ch.mark(dve.tensor_copy(m.row[:], row_f[:]))
                floor_div(ch, dve, tile_of[:], row_f[:], P, place_tmp[:])
                ch.link(dve.scalar_tensor_tensor(out=in_tile[:], in0=tile_of[:], scalar=-float(P), in1=row_f[:],
                                                 op0=ALU.mult, op1=ALU.add))
                ch.link(dve.tensor_tensor(hot_tile[:], tile_of[:].unsqueeze(2).broadcast_to([P, C, m.tiles]),
                                          g.ramp[:, 0:m.tiles].unsqueeze(1).broadcast_to([P, C, m.tiles]), ALU.is_equal))
                ch.mark(dve.tensor_scalar(node_parts[:, :, 0, :], hot_tile[:], g.part_index[:, 0:1], None, ALU.mult))
                ch.mark(dve.tensor_tensor(node_parts[:, :, 1, :].rearrange("p (b j) t -> p b j t", j=2),
                                          hot_tile[:].rearrange("p (b j) t -> p b j t", j=2),
                                          g.ramp[:, 0:NB].unsqueeze(2).unsqueeze(3).broadcast_to([P, NB, 2, m.tiles]),
                                          ALU.mult))
                ch.link(dve.tensor_tensor(hot_in[:], in_tile[:].unsqueeze(2).broadcast_to([P, C, P]),
                                          g.ramp[:].unsqueeze(1).broadcast_to([P, C, P]), ALU.is_equal))
                dve.sem_inc(placed_ready, 1)
                ch.link(dve.tensor_tensor(passed[:], g.ramp[:, 0:m.tiles].unsqueeze(2).broadcast_to([P, m.tiles, X]),
                                          tiles_upto[:].unsqueeze(1).broadcast_to([P, m.tiles, X]), ALU.is_ge))
                ch.link(dve.tensor_reduce(tile_f[:], passed[:], AX.X, ALU.add))
                ch.link(dve.tensor_scalar(tile_f[:], tile_f[:], float(X - 1), None, ALU.min))
                ch.mark(dve.tensor_copy(m.tile_expert[:], tile_f[:]))
                ch.link(dve.tensor_tensor(repeat[:, 2:], tile_f[:, 2:], tile_f[:, 0:m.tiles - 2], ALU.is_equal))
                ch.link(dve.scalar_tensor_tensor(out=tile_f[:, 2:], in0=repeat[:, 2:], scalar=float(X), in1=tile_f[:, 2:],
                                                 op0=ALU.mult, op1=ALU.add))
                dve.tensor_copy(m.tile_load[:], tile_f[:])
                dve.wait_ge(node_ready, 1)
                ch.link(dve.tensor_copy(node_f[:], ps_node[:, m.tiles:2 * m.tiles]))
                ch.link(dve.scalar_tensor_tensor(out=node_f[:], in0=ps_node[:, 0:m.tiles], scalar=float(NB), in1=node_f[:],
                                                 op0=ALU.mult, op1=ALU.add))
                dve.tensor_copy(m.node[:], node_f[:])

            @block.scalar
            def _(act):
                act.wait_ge(gap_ready, 1)
                act.activation(gap[:], gap[:], ACT.Exp).then_inc(exp_ready, 1)
                if biases:
                    act.wait_ge(biases_turned, 1)
                    act.copy(m.b1[:].rearrange("p e c -> p c e"), ps_b1[:, 0:HC * X].rearrange("p (c e) -> p c e", c=HC))

            if biases:
                @block.sync
                def _(sp):
                    sp.dma_start(raw_b1[:], biases[0]).then_inc(biases_loaded, 16)
                    sp.dma_start(m.b2[:], biases[1].unsqueeze(0).broadcast_to([P, X, D])).then_inc(biases_loaded, 16)
                    sp.wait_ge(biases_loaded, 32)

            @block.tensor
            def _(pe):
                if biases:
                    pe.wait_ge(biases_loaded, 32)
                    for j in range(HC):
                        last = pe.transpose(ps_b1[:, j * X:(j + 1) * X], raw_b1[:, j * P:(j + 1) * P], g.ident[0:X, 0:X])
                    last.then_inc(biases_turned, 1)
                pe.wait_ge(summed, 1)
                pe.matmul(ps[:, 0, 0:X], g.below[:], expert_sum[:], start=True, stop=True)
                pe.matmul(ps[:, 1, 0:X], g.ones[:], expert_sum[:], start=True, stop=True).then_inc(totals, 1)
                pe.wait_ge(placed_ready, 1)
                for j in range(C):
                    last = pe.matmul(ps_node[:, 0:2 * m.tiles], hot_in[:, j, :],
                                     node_parts[:, j, :, :].rearrange("p k t -> p (k t)"), start=(j == 0), stop=(j == C - 1))
                last.then_inc(node_ready, 1)


@staged
def experts(g, m, weights_in, weights_out):
    nc = g.nc
    n, HC = m.name, m.hidden // P
    NI = len(weights_in)
    COLS = HC * NI * P
    T = m.tiles
    row_loaded = g.dma_counts[0:2]
    w_in_loaded = [[g.sem(f"{n}_w_in_loaded{s}_{j}") for j in range(NI)] for s in range(2)]
    w_out_loaded = [g.sem(f"{n}_w_out_loaded{s}") for s in range(2)]
    turned, copied, hidden_ready, active, out_ready, out_copied = (
        g.sem(n + "_rows_turned"), g.sem(n + "_rows_copied"), g.sem(n + "_hidden"), g.sem(n + "_active"),
        g.sem(n + "_out"), g.sem(n + "_out_copied"))
    half_hidden = g.sem(n + "_half_hidden")
    half_active, gate = g.sem(n + "_half_active"), g.sem(n + "_load_gate")
    stored = g.out_counts
    rows_out = m.rows_out.rearrange("(t p) f -> p t f", p=P)
    with ExitStack() as ctx:
        sb = lambda k, s, d=F32: g.sb(n + "_" + k, s, d, ctx)
        w_in = sb("w_in", [P, 2, NI, 2, m.hidden])
        w_out = sb("w_out", [P, 2, HC, D])
        row, row_t = sb("rows", [P, 2, D]), sb("rows_t", [P, 2, 2 * P])
        act_t = sb("act_t", [P, 2, HC * P])
        gate_t = sb("gate_t", [P, 2, HC * P]) if m.gated else None
        out = sb("out", [P, 2, D])
        nothing = sb("nothing", [1, 2, NI + 1])
        ps_t = g.ps(n + "_t", [P, 2, 512], ctx=ctx)
        ps_h = g.ps(n + "_h", [P, 2, COLS], ctx=ctx)
        ps_o = g.ps(n + "_o", [P, 2, 512], ctx=ctx)
        with nc.Block() as block:
            @block.sync
            def _(sp):
                def after(sem, value):
                    sp.wait_ge(sem, value)
                    sp.sem_inc(gate, 1)
                    sp.wait_ge(gate, 1)

                def load_in(s, j, expert):
                    sp.dma_start(w_in[:, s, j, :, :], weights_in[j][ds(expert, 1), :, :]
                                 .rearrange("e (k p) h -> p (e k) h", p=P)).then_inc(w_in_loaded[s][j], 16)

                def load_out(s, expert):
                    sp.dma_start(w_out[:, s, :, :], weights_out[ds(expert, 1), :, :]
                                 .rearrange("e (k p) h -> p (e k) h", p=P)).then_inc(w_out_loaded[s], 16)

                def load_nothing(s, k, sem):
                    sp.dma_start(nothing[:, s, k:k + 1], m.nothing).then_inc(sem, 16)

                for s in range(2):
                    expert = sp.value_load(m.tile_load[0:1, s:s + 1], min_val=0, max_val=m.experts - 1)
                    for j in range(NI):
                        load_in(s, j, expert)
                    load_out(s, expert)
                with sp.Fori(1, T // 2) as i:
                    for s in range(2):
                        t = 2 * i + s
                        load = sp.value_load(m.tile_load[0:1, ds(t, 1)], min_val=0, max_val=2 * m.experts - 1)
                        for j in range(NI):
                            after(hidden_ready if j == NI - 1 else half_hidden, t + 1)
                            with sp.If(load < m.experts):
                                load_in(s, j, load % m.experts)
                            with sp.If(load >= m.experts):
                                load_nothing(s, j, w_in_loaded[s][j])
                        after(out_ready, t + 1)
                        with sp.If(load < m.experts):
                            load_out(s, load % m.experts)
                        with sp.If(load >= m.experts):
                            load_nothing(s, NI, w_out_loaded[s])

            @block.tensor
            def _(pe):
                pe.sem_inc(turned, 2)
                pe.sem_inc(hidden_ready, 2)
                pe.sem_inc(half_hidden, 2)
                pe.sem_inc(out_ready, 2)

                def turn(t, s, rnd):
                    pe.wait_ge(row_loaded[s].sem, row_loaded[s].at(16 * rnd + 16))
                    pe.wait_ge(copied, t + 1)
                    for j in range(2):
                        last = pe.transpose(ps_t[:, s, j * P:(j + 1) * P], row[:, s, j * P:(j + 1) * P], g.ident[:])
                    last.then_inc(turned, 1)

                def hidden(t, s, rnd):
                    pe.wait_ge(copied, t + 3)
                    pe.wait_ge(active, t + 1)
                    for j in range(NI):
                        pe.wait_ge(w_in_loaded[s][j], 16 * (rnd + 1))
                        if j == 1:
                            last.then_inc(half_hidden, 1)
                        for c in range(HC):
                            for k in range(2):
                                last = pe.matmul(ps_h[:, s, (j * HC + c) * P:(j * HC + c + 1) * P],
                                                 w_in[:, s, j, k, c * P:(c + 1) * P],
                                                 row_t[:, s, k * P:(k + 1) * P], start=(k == 0), stop=(k == 1))
                    last.then_inc(hidden_ready, 1)

                def output(t, s, rnd):
                    pe.wait_ge(active, t + 3)
                    pe.wait_ge(w_out_loaded[s], 16 * (rnd + 1))
                    pe.wait_ge(out_copied, t + 1)
                    for c in range(HC):
                        last = pe.matmul(ps_o[:, s, 0:D], act_t[:, s, c * P:(c + 1) * P], w_out[:, s, c, :],
                                         start=(c == 0), stop=(c == HC - 1))
                    last.then_inc(out_ready, 1)

                turn(0, 0, 0)
                hidden(0, 0, 0)
                turn(1, 1, 0)
                with pe.Fori(0, T // 2 - 1) as i:
                    hidden(2 * i + 1, 1, i)
                    turn(2 * i + 2, 0, i + 1)
                    output(2 * i, 0, i)
                    hidden(2 * i + 2, 0, i + 1)
                    turn(2 * i + 3, 1, i + 1)
                    output(2 * i + 1, 1, i)
                hidden(T - 1, 1, T // 2 - 1)
                output(T - 2, 0, T // 2 - 1)
                output(T - 1, 1, T // 2 - 1)

            @block.scalar
            def _(act):
                act.preload_act_table(ACT.Silu if m.gated else ACT.Gelu)
                act.sem_inc(copied, 2)
                if not m.gated:
                    act.sem_inc(active, 2)
                b1 = None if m.gated else m.b1[:].rearrange("p e c -> p (e c)")

                def copy_rows(t, s):
                    act.wait_ge(turned, t + 3)
                    act.wait_ge(hidden_ready, t + 1)
                    act.copy(row_t[:, s, :], ps_t[:, s, 0:2 * P]).then_inc(copied, 1)

                def activate(t, s):
                    if not m.gated:
                        expert = act.value_load(m.tile_expert[0:1, ds(t, 1)], min_val=0, max_val=m.experts - 1)
                    act.wait_ge(hidden_ready, t + 3)
                    act.wait_ge(out_ready, t + 1)
                    if m.gated:
                        act.wait_ge(active, t + 1)
                        act.activation(gate_t[:, s, :], ps_h[:, s, 0:HC * P], ACT.Silu).then_inc(half_active, 1)
                    else:
                        for c in range(HC):
                            last = act.activation(act_t[:, s, c * P:(c + 1) * P], ps_h[:, s, c * P:(c + 1) * P],
                                                  ACT.Gelu, bias=b1[:, ds(expert * HC + c, 1)])
                        last.then_inc(active, 1)

                copy_rows(0, 0)
                with act.Fori(0, T // 2 - 1) as i:
                    copy_rows(2 * i + 1, 1)
                    activate(2 * i, 0)
                    copy_rows(2 * i + 2, 0)
                    activate(2 * i + 1, 1)
                copy_rows(T - 1, 1)
                activate(T - 2, 0)
                activate(T - 1, 1)

            @block.vector
            def _(dve):
                dve.sem_inc(out_copied, 2)
                if m.gated:
                    dve.sem_inc(active, 2)

                def act_mul(t, s):
                    dve.wait_ge(half_active, t + 1)
                    dve.tensor_tensor(act_t[:, s, :], gate_t[:, s, :], ps_h[:, s, HC * P:2 * HC * P], ALU.mult)\
                       .then_inc(active, 1)

                def take_out(t, s, rnd, expert):
                    dve.wait_ge(out_ready, t + 3)
                    dve.wait_ge(stored[s].sem, stored[s].at(16 * rnd))
                    if m.gated:
                        dve.tensor_copy(out[:, s, :], ps_o[:, s, 0:D]).then_inc(out_copied, 1)
                    else:
                        dve.tensor_tensor(out[:, s, :], ps_o[:, s, 0:D],
                                          m.b2[:, ds(expert, 1), :].rearrange("p a f -> p (a f)"), ALU.add)\
                           .then_inc(out_copied, 1)

                if m.gated:
                    act_mul(0, 0)
                    with dve.Fori(0, T // 2 - 1) as i:
                        act_mul(2 * i + 1, 1)
                        take_out(2 * i, 0, i, None)
                        act_mul(2 * i + 2, 0)
                        take_out(2 * i + 1, 1, i, None)
                    act_mul(T - 1, 1)
                    take_out(T - 2, 0, T // 2 - 1, None)
                    take_out(T - 1, 1, T // 2 - 1, None)
                else:
                    with dve.Fori(0, T // 2) as i:
                        for s in range(2):
                            expert = dve.value_load(m.tile_expert[0:1, ds(2 * i + s, 1)], min_val=0,
                                                    max_val=m.experts - 1)
                            take_out(2 * i + s, s, i, expert)

            @block.gpsimd
            def _(pool):
                for t in range(T + 3):
                    if t < T:
                        pool.wait_ge(turned, t + 1)
                        pool.indirect_dma_start(out=row[:, t % 2, :], out_offset=None, in_=m.x_table,
                                                in_offset=bass.IndirectOffsetOnAxis(ap=m.node[:, t:t + 1], axis=0))\
                            .then_inc(row_loaded[t % 2].sem, 16)
                    if t >= 3:
                        pool.wait_ge(out_copied, t)
                        pool.dma_start(rows_out[:, t - 3, :], out[:, (t - 3) % 2, :]).then_inc(stored[(t - 3) % 2].sem, 16)
                for q in stored:
                    pool.wait_ge(q.sem, q.at(16 * (T // 2)))
    for q in stored + row_loaded:
        q.base += 16 * (T // 2)


@staged
def combine(g, m, x, out):
    nc = g.nc
    SLOTS = 10
    R = 5
    first, second = g.sem(m.name + "_first_added"), g.sem(m.name + "_second_added")
    stats_done, stored = g.sem(m.name + "_stats_done"), g.sem(m.name + "_out_stored")
    got = g.dma_counts[0:SLOTS]
    with ExitStack() as ctx:
        back = g.sb(m.name + "_back", [P, SLOTS, 2, D], ctx=ctx)
        with nc.Block() as block:
            @block.gpsimd
            def _(pool):
                for b in range(NB):
                    k = b % SLOTS
                    if b >= SLOTS:
                        pool.wait_ge(second, b - SLOTS + 1)
                    for j in range(2):
                        pool.indirect_dma_start(
                            out=back[:, k, j, :], out_offset=None, in_=m.rows_out,
                            in_offset=bass.IndirectOffsetOnAxis(ap=m.row[:, 2 * b + j:2 * b + j + 1], axis=0))\
                            .then_inc(got[k].sem, 16)

            @block.vector
            def _(dve):
                for t in range(NB + 4):
                    for b, j, added in ((t, 0, first), (t - 1, 1, second)):
                        if not 0 <= b < NB:
                            continue
                        k = b % SLOTS
                        if j == 0:
                            dve.wait_ge(got[k].sem, got[k].at(32 * (b // SLOTS + 1)))
                        else:
                            dve.wait_ge(first, b + 1)
                        dve.scalar_tensor_tensor(out=x[:, b, :], in0=back[:, k, j, :],
                                                 scalar=m.weight[:, 2 * b + j:2 * b + j + 1],
                                                 in1=x[:, b, :], op0=ALU.mult, op1=ALU.add).then_inc(added, 1)
                    b = t - 2
                    if out is None and 0 <= b < NB:
                        dve.wait_ge(second, b + 1)
                        dve.bn_stats(g.stats[:, b, :], x[:, b, :]).then_inc(stats_done, 1)
                    b = t - 3
                    if out is None and 0 <= b < NB:
                        dve.wait_ge(stats_done, b + 1)
                        dve.bn_aggr(g.moments[:, b, :], g.stats[:, b, :])

            if out is not None:
                @block.sync
                def _(sp):
                    out_v = out.rearrange("(a b) f -> a b f", b=NB)
                    for b in range(0, NB, R):
                        sp.wait_ge(second, b + R)
                        sp.dma_start(out_v[:, b:b + R, :], x[0:N // NB, b:b + R, :]).then_inc(stored, 16)
                    sp.wait_ge(stored, 16 * (NB // R))
    for k, q in enumerate(got):
        q.base += 32 * len(range(k, NB, SLOTS))


def mixture(g, m, x, biases, weights_in, weights_out, out=None):
    normalise(g, m.name + "_norm", x, g.cur)
    with ExitStack() as ctx:
        m.ctx = ctx
        m.nothing = weights_out[0, 0:1, 0:1]
        logits = g.sb(m.name + "_logits", [P, NB, m.experts], ctx=ctx)
        dense(g, m.name + "_gate", g.cur, g.w[m.name], m.experts, logits, x_table=m.x_table)
        route(g, m, logits, biases)
        experts(g, m, weights_in, weights_out)
        combine(g, m, x, out)


def write_program(nc, A, out):
    with ExitStack() as ctx:
        g = Program(nc, ctx)
        constants(g)
        mix0, mix1 = Mixture(g, "L0_ffn", 8, 1024, False), Mixture(g, "L1_ffn", 16, 512, True)
        resident(g)
        with ExitStack() as weights_ctx:
            sort_edges(g, A["src"], A["dst"], A["edge_attr_3"], A["x"], A, weights_ctx)
            edge_tables(g)

        table, states = g.dram("table", [NPAD, D]), g.dram("states", [EPAD, D])
        w, row = g.w, g.row
        normalise(g, "norm0", g.x, g.cur)
        dense(g, "pool_in", g.cur, w["L0_gnn_Wp1"], D, g.new, table, g.wide["L0_gnn_bp1"][:])
        pool_max(g, "pool1", table, states, g.cur, w["L0_gnn_Wm1"], row["L0_gnn_bm1"][:], g.new)
        mix(g, "mix1", states, w["L0_gnn_Wm1"][:, 2:4, :], g.new, None, g.cur, table)
        pool_max(g, "pool2", table, states, g.cur, w["L0_gnn_Wm2"], row["L0_gnn_bm2"][:], g.new)
        mix(g, "mix2", states, w["L0_gnn_Wm2"][:, 2:4, :], g.new, g.cur, g.new, None, True)
        normalise(g, "norm2", g.new, g.cur, g.wide["L0_gnn_ln2_g"][:], g.wide["L0_gnn_ln2_b"][:], None, table, True)
        pool_max(g, "pool3", table, states, g.cur, w["L0_gnn_Wm3"], row["L0_gnn_bm3"][:], g.new)
        mix(g, "mix3", states, w["L0_gnn_Wm3"][:, 2:4, :], g.new, g.cur, g.new, None, True)
        normalise(g, "norm3", g.new, g.cur, g.wide["L0_gnn_ln3_g"][:], g.wide["L0_gnn_ln3_b"][:], g.x, None, True)

        mixture(g, mix0, g.x, (A["L0_ffn_b1"], A["L0_ffn_b2"]),
                [A["L0_ffn_W1"]], A["L0_ffn_W2"])

        W = D + 2 * H
        head_table, head_states = g.dram("head_table", [NPAD, W]), g.dram("head_states", [EPAD, W])
        normalise(g, "norm4", g.x, g.cur, have_moments=True)
        with ExitStack() as scope:
            heads = g.sb("heads", [P, NB, W], ctx=scope)
            dense(g, "heads", g.cur, g.w["L1_gnn_W"], W, heads, head_table)
        attention_scan(g, "att", head_table, head_states)
        attend(g, "attend", head_states, g.x, g.wide["L1_gnn_bias"][:])

        mixture(g, mix1, g.x, None, [A["L1_ffn_w1"], A["L1_ffn_w2"]], A["L1_ffn_w3"], out)


def kernel(**inputs):
    import numpy as _np
    import concourse.bacc as _bacc
    from concourse import mybir as _mybir
    from concourse.bass_utils import run_bass_kernel_spmd as _run

    nc = _bacc.Bacc("TRN2", target_bir_lowering=False, num_devices=1)
    arrays, args = {}, {}
    for name, value in inputs.items():
        a = _np.ascontiguousarray(value)
        arrays[f"in_{name}_dram"] = a
        args[name] = nc.dram_tensor(f"in_{name}_dram", a.shape, _mybir.dt.from_np(a.dtype), kind="ExternalInput").ap()
    out = nc.dram_tensor("out_0_dram", (N, D), _mybir.dt.float32, kind="ExternalOutput").ap()
    write_program(nc, args, out)
    r = _run(nc, [arrays], core_ids=[0])
    return r.results[0]["out_0_dram"]
```
